# Optimizing a Trainium2 kernel written in Bass

```python
import numpy as np
import jax
import jax.numpy as jnp

def _softmax(x, axis=-1):
    return jax.nn.softmax(x, axis=axis)

def _gelu(x):
    return jax.nn.gelu(x, approximate=True)

def _silu(x):
    return jax.nn.silu(x)

def _sigmoid(x):
    return jax.nn.sigmoid(x)

def _layernorm(x, axis=-1, eps=1e-05):
    m = jnp.mean(x, axis=axis, keepdims=True)
    v = jnp.var(x, axis=axis, keepdims=True)
    return (x - m) / jnp.sqrt(v + eps)

def _scatter_add(tgt, idx, src, axis=0):
    return tgt.at[idx].add(src)

def _segment_sum(src, seg, n):
    return jax.ops.segment_sum(src, seg, n)
kernel_name = 'mk_flamingo_gated_d2_seqx_r8_3fe86b'

def setup_inputs(seed: int=0):
    np.random.seed(seed)
    _w = jnp.asarray

    def _rec_inputs():
        import jax
        import jax.numpy as jnp
        _rk = jax.random.key(seed)
        x = 0.0003765 + 1 * jax.random.normal(jax.random.fold_in(_rk, 1), (16, 128, 256), jnp.float32)
        _lenS = 128 - jax.random.randint(jax.random.fold_in(_rk, 7), (16,), 0, max(1, 128 // 4) + 1, jnp.int32)
        _lenS2 = 128 - jax.random.randint(jax.random.fold_in(_rk, 8), (16,), 0, max(1, 128 // 4) + 1, jnp.int32)
        _ctx_2048P = jax.random.normal(jax.random.fold_in(_rk, 11), (16, 16, 256), jnp.float32)
        _ctx_2048c = jax.random.dirichlet(jax.random.fold_in(_rk, 511), 0.3 * jnp.ones((16,), jnp.float32), (16, 128))
        _ctx_2048t = jnp.einsum('bsk,bkd->bsd', _ctx_2048c, _ctx_2048P)
        _ctx_2048t = _ctx_2048t * jax.lax.rsqrt(jnp.mean(jnp.square(_ctx_2048t)) + 1e-12) * 0.953939
        ctx_2048 = -0.000292821 + 1.00034 * (_ctx_2048t + 0.3 * jax.random.normal(jax.random.fold_in(_rk, 611), (16, 128, 256), jnp.float32))
        itok_BxS_0_1023 = jax.random.randint(jax.random.fold_in(_rk, 12), (16, 128), 0, 128, jnp.int32)
        _g = jax.random.normal(jax.random.fold_in(_rk, 9001), (2, 2), jnp.float32)
        _g = jnp.sign(_g) * jnp.maximum(jnp.abs(_g), 1.0) + (_g == 0) * 1.0
        g_xattn = _g[0]
        g_ffn = _g[1]
        return (x, ctx_2048, itok_BxS_0_1023, g_xattn, g_ffn)
    x, ctx_2048, itok_BxS_0_1023, g_xattn, g_ffn = _rec_inputs()

    def _L0_xattn_setup():
        import jax, jax.numpy as jnp
        import numpy as np
        key = jax.random.key(seed)
        k1, k2, k3, k4, k5 = jax.random.split(key, 5)
        B, D_MODEL, L = (2, 128, 256)
        HEAD_DIM = 8
        H = D_MODEL // HEAD_DIM
        return {'k': jax.random.normal(k1, (B, D_MODEL, L), dtype=jnp.float32), 'v': jax.random.normal(k2, (B, D_MODEL, L), dtype=jnp.float32), 'q': jax.random.normal(k3, (B, D_MODEL, L), dtype=jnp.float32), 'ssm_kernel': jax.random.normal(k4, (H, L), dtype=jnp.float32), 'D': jax.random.normal(k5, (H,), dtype=jnp.float32), 'head_dim': HEAD_DIM}
    _L0_xattn_all = _L0_xattn_setup()
    _L0_xattn_in = {k: v for k, v in _L0_xattn_all.items() if k in ('ssm_kernel', 'D')}
    del _L0_xattn_all

    def _L0_ffn_setup():
        import jax, jax.numpy as jnp
        import numpy as np
        TOPK = 2
        NORM_TOPK = True
        SCALE = 1.0
        EPS = 1e-09
        key = jax.random.key(seed)
        ks = jax.random.split(key, 9)
        h, i, E = (256, 128, 16)
        std = 0.02
        return {'x': jax.random.normal(ks[0], (1, 256, h), jnp.float32), 'Wr': jax.random.normal(ks[1], (E, h), jnp.float32) * std, 'bias': jnp.zeros((E,), jnp.float32), 'Wg': jax.random.normal(ks[2], (E, h, i), jnp.float32) * std, 'Wu': jax.random.normal(ks[3], (E, h, i), jnp.float32) * std, 'Wd': jax.random.normal(ks[4], (E, i, h), jnp.float32) * std, 'sWg': jax.random.normal(ks[5], (h, i), jnp.float32) * std, 'sWu': jax.random.normal(ks[6], (h, i), jnp.float32) * std, 'sWd': jax.random.normal(ks[7], (i, h), jnp.float32) * std}
    _L0_ffn_all = _L0_ffn_setup()
    _L0_ffn_in = {k: v for k, v in _L0_ffn_all.items() if k in ('Wr', 'bias', 'Wg', 'Wu', 'Wd', 'sWg', 'sWu', 'sWd')}
    del _L0_ffn_all

    def _L1_xattn_setup():
        import jax, jax.numpy as jnp
        import numpy as np
        B, Lq, Lk = (2, 512, 128)
        Q_DIM, KV_DIM = (256, 256)
        H, HD = (16, 128)
        KVC, QC, R = (64, 96, 64)
        LOOKBACK = 8
        NEG = -1e+30

        def _rope(x, L):
            half = x.shape[-1] // 2
            inv_freq = 1.0 / 10000.0 ** (jnp.arange(half, dtype=jnp.float32) / half)
            ang = jnp.arange(L, dtype=jnp.float32)[:, None] * inv_freq
            cos, sin = (jnp.cos(ang), jnp.sin(ang))
            x1, x2 = (x[..., :half], x[..., half:])
            return jnp.concatenate([x1 * cos - x2 * sin, x1 * sin + x2 * cos], axis=-1)
        key = jax.random.key(seed)
        ks = jax.random.split(key, 11)

        def w(k, shape, fan_in):
            return jax.random.normal(k, shape, jnp.float32) / np.sqrt(fan_in).astype(np.float32)
        return {'q': jax.random.normal(ks[0], (B, Lq, Q_DIM), jnp.float32), 'kv': jax.random.normal(ks[1], (B, Lk, KV_DIM), jnp.float32), 'seg_id': jnp.sort(jax.random.randint(ks[2], (B, Lq), 0, Lk), axis=-1), 'W_kvc': w(ks[3], (KV_DIM, KVC), KV_DIM), 'W_dq': w(ks[4], (Q_DIM, QC), Q_DIM), 'W_uq': w(ks[5], (QC, H * HD), QC), 'W_qr': w(ks[6], (QC, H * R), QC), 'W_uk': w(ks[7], (KVC, H * HD), KVC), 'W_kr': w(ks[8], (KVC, R), KVC), 'W_uv': w(ks[9], (KVC, H * HD), KVC), 'W_o': w(ks[10], (H * HD, Q_DIM), H * HD)}
    _L1_xattn_all = _L1_xattn_setup()
    _L1_xattn_in = {k: v for k, v in _L1_xattn_all.items() if k in ('W_kvc', 'W_dq', 'W_uq', 'W_qr', 'W_uk', 'W_kr', 'W_uv', 'W_o')}
    del _L1_xattn_all

    def _L1_ffn_setup():
        import jax, jax.numpy as jnp
        import numpy as np
        D_MODEL = 256
        HIDDEN = int(2 * D_MODEL * 4 / 3)

        def ternary_quant(w):
            s = jnp.mean(jnp.abs(w))
            q = jnp.clip(jnp.round(w / s), -1.0, 1.0) * s
            return w + jax.lax.stop_gradient(q - w)
        key = jax.random.key(seed)
        k0, k1, k2, k3 = jax.random.split(key, 4)
        x = jax.random.normal(k0, (4, 512, D_MODEL), dtype=jnp.float32)
        std_in = 1.0 / np.sqrt(D_MODEL)
        std_h = 1.0 / np.sqrt(HIDDEN)
        w1 = jax.random.uniform(k1, (HIDDEN, D_MODEL), jnp.float32, -std_in, std_in)
        w3 = jax.random.uniform(k2, (HIDDEN, D_MODEL), jnp.float32, -std_in, std_in)
        w2 = jax.random.uniform(k3, (D_MODEL, HIDDEN), jnp.float32, -std_h, std_h)
        return {'x': x, 'w1': w1, 'w3': w3, 'w2': w2}
    _L1_ffn_all = _L1_ffn_setup()
    _L1_ffn_in = {k: v for k, v in _L1_ffn_all.items() if k in ('w1', 'w3', 'w2')}
    del _L1_ffn_all
    return {'x': x, 'ctx_2048': ctx_2048, 'itok_BxS_0_1023': itok_BxS_0_1023, 'g_xattn': g_xattn, 'g_ffn': g_ffn, 'L0_xattn_ssm_kernel': _L0_xattn_in['ssm_kernel'], 'L0_xattn_D': _L0_xattn_in['D'], 'L0_ffn_Wr': _L0_ffn_in['Wr'], 'L0_ffn_bias': _L0_ffn_in['bias'], 'L0_ffn_Wg': _L0_ffn_in['Wg'], 'L0_ffn_Wu': _L0_ffn_in['Wu'], 'L0_ffn_Wd': _L0_ffn_in['Wd'], 'L0_ffn_sWg': _L0_ffn_in['sWg'], 'L0_ffn_sWu': _L0_ffn_in['sWu'], 'L0_ffn_sWd': _L0_ffn_in['sWd'], 'L1_xattn_W_kvc': _L1_xattn_in['W_kvc'], 'L1_xattn_W_dq': _L1_xattn_in['W_dq'], 'L1_xattn_W_uq': _L1_xattn_in['W_uq'], 'L1_xattn_W_qr': _L1_xattn_in['W_qr'], 'L1_xattn_W_uk': _L1_xattn_in['W_uk'], 'L1_xattn_W_kr': _L1_xattn_in['W_kr'], 'L1_xattn_W_uv': _L1_xattn_in['W_uv'], 'L1_xattn_W_o': _L1_xattn_in['W_o'], 'L1_ffn_w1': _L1_ffn_in['w1'], 'L1_ffn_w3': _L1_ffn_in['w3'], 'L1_ffn_w2': _L1_ffn_in['w2']}

def reference(x, ctx_2048, itok_BxS_0_1023, g_xattn, g_ffn, L0_xattn_ssm_kernel, L0_xattn_D, L0_ffn_Wr, L0_ffn_bias, L0_ffn_Wg, L0_ffn_Wu, L0_ffn_Wd, L0_ffn_sWg, L0_ffn_sWu, L0_ffn_sWd, L1_xattn_W_kvc, L1_xattn_W_dq, L1_xattn_W_uq, L1_xattn_W_qr, L1_xattn_W_uk, L1_xattn_W_kr, L1_xattn_W_uv, L1_xattn_W_o, L1_ffn_w1, L1_ffn_w3, L1_ffn_w2):
    import jax
    import jax.numpy as jnp

    def _L0_xattn_ref(k, v, q, ssm_kernel, D, head_dim):
        import jax, jax.numpy as jnp
        import numpy as np
        B, HD, L = k.shape
        H = HD // head_dim
        fft_size = 2 * L
        k_ = k.reshape(B, H, head_dim, L)
        v_ = v.reshape(B, H, head_dim, L)
        q_ = q.reshape(B, H, head_dim, L)
        kv = jnp.einsum('bhil,bhjl->bijhl', k_, v_)
        kv_f = jnp.fft.rfft(kv, n=fft_size)
        kernel_f = jnp.fft.rfft(ssm_kernel, n=fft_size)
        y = jnp.fft.irfft(kv_f * kernel_f, n=fft_size)[..., :L]
        out = y + kv * D[None, None, None, :, None]
        out = jnp.einsum('bijhl,bhil->bjhl', out, q_)
        out = jnp.transpose(out, (0, 2, 1, 3)).reshape(B, H * head_dim, L)
        return out.astype(k.dtype)

    def _L0_ffn_ref(x, Wr, bias, Wg, Wu, Wd, sWg, sWu, sWd):
        import jax, jax.numpy as jnp
        import numpy as np
        TOPK = 2
        NORM_TOPK = True
        SCALE = 1.0
        EPS = 1e-09
        b, s, h = x.shape
        E = Wr.shape[0]
        xt = x.reshape(b * s, h)
        logits = xt @ Wr.T + bias
        probs = jax.nn.softmax(logits, axis=-1)
        topk_val, topk_idx = jax.lax.top_k(probs, TOPK)
        if NORM_TOPK:
            w = topk_val / (jnp.sum(topk_val, axis=-1, keepdims=True) + EPS)
        else:
            w = topk_val
        w = w * SCALE
        g = jnp.einsum('th,ehi->tei', xt, Wg)
        u = jnp.einsum('th,ehi->tei', xt, Wu)
        y = jnp.einsum('tei,eih->teh', jax.nn.silu(g) * u, Wd)
        oh = jax.nn.one_hot(topk_idx, E, dtype=x.dtype)
        routed = jnp.einsum('tke,tk,teh->th', oh, w, y)
        shared = jax.nn.silu(xt @ sWg) * (xt @ sWu) @ sWd
        return (routed + shared).reshape(b, s, h)

    def _L1_xattn_ref(q, kv, seg_id, W_kvc, W_dq, W_uq, W_qr, W_uk, W_kr, W_uv, W_o):
        import jax, jax.numpy as jnp
        import numpy as np
        B, Lq, Lk = (2, 512, 128)
        Q_DIM, KV_DIM = (256, 256)
        H, HD = (16, 128)
        KVC, QC, R = (64, 96, 64)
        LOOKBACK = 8
        NEG = -1e+30

        def _rope(x, L):
            half = x.shape[-1] // 2
            inv_freq = 1.0 / 10000.0 ** (jnp.arange(half, dtype=jnp.float32) / half)
            ang = jnp.arange(L, dtype=jnp.float32)[:, None] * inv_freq
            cos, sin = (jnp.cos(ang), jnp.sin(ang))
            x1, x2 = (x[..., :half], x[..., half:])
            return jnp.concatenate([x1 * cos - x2 * sin, x1 * sin + x2 * cos], axis=-1)
        b, lq, _ = q.shape
        lk = kv.shape[1]
        kv_c = kv @ W_kvc
        q_c = q @ W_dq
        q_nope = (q_c @ W_uq).reshape(b, lq, H, HD).transpose(0, 2, 1, 3)
        q_rope = (q_c @ W_qr).reshape(b, lq, H, R).transpose(0, 2, 1, 3)
        k_nope = (kv_c @ W_uk).reshape(b, lk, H, HD)
        v = (kv_c @ W_uv).reshape(b, lk, H, HD)
        k_rope = kv_c @ W_kr
        q_rope = _rope(q_rope, lq)
        k_rope = _rope(k_rope, lk)
        scale = 1.0 / np.sqrt(HD + R).astype(np.float32)
        scores = (jnp.einsum('bhqd,bkhd->bhqk', q_nope, k_nope) + jnp.einsum('bhqr,bkr->bhqk', q_rope, k_rope)) * scale
        k_ids = jnp.arange(lk)[None, None, :]
        qs = seg_id[:, :, None]
        good = (k_ids <= qs) & (k_ids >= qs - LOOKBACK)
        scores = jnp.where(good[:, None, :, :], scores, NEG)
        attn = jax.nn.softmax(scores, axis=-1)
        out = jnp.einsum('bhqk,bkhd->bqhd', attn, v).reshape(b, lq, H * HD)
        return out @ W_o

    def _L1_ffn_ref(x, w1, w3, w2):
        import jax, jax.numpy as jnp
        import numpy as np
        D_MODEL = 256
        HIDDEN = int(2 * D_MODEL * 4 / 3)

        def ternary_quant(w):
            s = jnp.mean(jnp.abs(w))
            q = jnp.clip(jnp.round(w / s), -1.0, 1.0) * s
            return w + jax.lax.stop_gradient(q - w)
        w1q = ternary_quant(w1)
        w3q = ternary_quant(w3)
        w2q = ternary_quant(w2)
        h1 = jnp.einsum('bsd,hd->bsh', x, w1q)
        h3 = jnp.einsum('bsd,hd->bsh', x, w3q)
        g = jax.nn.silu(h1) * h3
        return jnp.einsum('bsh,dh->bsd', g, w2q)
    x = x + jnp.tanh(g_xattn[0]) * _L0_xattn_ref(ctx_2048, ctx_2048, _layernorm(x, axis=-1), L0_xattn_ssm_kernel, L0_xattn_D, 8)
    x = x + jnp.tanh(g_ffn[0]) * _L0_ffn_ref(_layernorm(x, axis=-1), L0_ffn_Wr, L0_ffn_bias, L0_ffn_Wg, L0_ffn_Wu, L0_ffn_Wd, L0_ffn_sWg, L0_ffn_sWu, L0_ffn_sWd)
    x = x + jnp.tanh(g_xattn[1]) * _L1_xattn_ref(_layernorm(x, axis=-1), ctx_2048, itok_BxS_0_1023, L1_xattn_W_kvc, L1_xattn_W_dq, L1_xattn_W_uq, L1_xattn_W_qr, L1_xattn_W_uk, L1_xattn_W_kr, L1_xattn_W_uv, L1_xattn_W_o)
    x = x + jnp.tanh(g_ffn[1]) * _L1_ffn_ref(_layernorm(x, axis=-1), L1_ffn_w1, L1_ffn_w3, L1_ffn_w2)
    return x

_drawn_inputs = setup_inputs


def setup_inputs(seed=0):
    import zlib

    import numpy as np

    out = dict(_drawn_inputs(seed))
    spreads = {'g_ffn': (-1.0, 0.6), 'L0_ffn_bias': (0.0, 0.8)}
    factors = {'L0_ffn_Wr': 8.0,
     'L0_ffn_Wg': 8.0,
     'L0_ffn_Wu': 8.0,
     'L0_ffn_Wd': 8.0,
     'L0_ffn_sWg': 8.0,
     'L0_ffn_sWu': 8.0,
     'L0_ffn_sWd': 8.0,
     'L1_xattn_W_dq': 5.714,
     'L1_xattn_W_uq': 6.783,
     'L1_xattn_W_qr': 8.0,
     'L1_xattn_W_uk': 6.768,
     'L1_xattn_W_kr': 8.0,
     'L1_ffn_w1': 8.0,
     'L1_ffn_w3': 8.0,
     'L1_ffn_w2': 8.0}
    for name, (base, spread) in spreads.items():
        noise = np.random.default_rng([zlib.crc32(name.encode()), seed]).standard_normal(out[name].shape)
        drawn = base * np.exp(spread * noise) if base else spread * noise
        out[name] = jnp.asarray(drawn.astype(out[name].dtype))
    for name, factor in factors.items():
        out[name] = (out[name] * factor).astype(out[name].dtype)
    return out
```

```python
import concourse.bass as bass
from concourse import mybir
from contextlib import ExitStack

B, S, D = 16, 128, 256
NT = 16
DK = D // 128
E, I = 16, 128
NH0, HD0 = 16, 8
NB = 47
H, HD, KVC, QC, R = 16, 128, 64, 96, 64
HID = 682
NC = (HID + 127) // 128
NPAIR = HD0 * (HD0 + 1) // 2
PA = 21
PB = NPAIR - PA
LN_EPS = 1e-5
W_EPS = 1e-9
NEG = -1e30
LOOKBACK = 8
SCALE = 1.0 / (HD + R) ** 0.5

C_ID, C_COS, C_SIN, C_K4 = 0, 128, 256, 384
C_TRI, C_THR, C_IOTA, C_BLK, C_UP = 512, 768, 784, 800, 800 + NB
NCF = C_UP + 128


def flamingo_kernel(nc, x, ctxd, segT, gates, ssm, ssmD, WrT, rbias, Wg, Wu, Wd, sWg, sWu, sWd,
                    Wkvc, Wdq, WuqT, Wqr, WukT, Wkr, WuvT, Wo, w1T, w3T, w2T, constf, out):
    f32, bf16, i32, u32 = mybir.dt.float32, mybir.dt.bfloat16, mybir.dt.int32, mybir.dt.uint32
    ALU = mybir.AluOpType
    ACT = mybir.ActivationFunctionType
    AX = mybir.AxisListType.X

    def pair(i):
        return i * (i + 1) // 2

    ctx = ExitStack()
    with ctx:
        def sb(name, shape, dt=f32):
            return ctx.enter_context(nc.sbuf_tensor(name, shape, dt))

        def sem(name):
            return ctx.enter_context(nc.semaphore(name))

        cf = sb("cf", [128, NCF])
        cb = sb("cb", [128, 256], bf16)
        ident, cosT, sinT = cf[:, C_ID:C_ID + 128], cf[:, C_COS:C_COS + 128], cf[:, C_SIN:C_SIN + 128]
        identb, trib = cb[:, 0:128], cb[:, 128:256]
        onesb = sb("onesb", [128, 128], bf16)
        onesf = sb("onesf", [128, 128])
        X = sb("X", [128, NT, D])
        XN = sb("XN", [128, NT, D])
        CT = sb("CT", [128, DK, NT, 128])
        QT = sb("QT", [128, DK, NT, 128])
        WE = sb("WE", [128, (DK * E * 2 * I) + E * D])
        WGU = WE[:, 0:DK * E * 2 * I].rearrange("p (k e c) -> p k e c", k=DK, e=E)
        WD = WE[:, DK * E * 2 * I:].rearrange("p (e d) -> p e d", e=E)
        sWgu = sb("sWgu", [128, DK, 2, I])
        sWdn = sb("sWdn", [128, D])
        Wr = sb("Wr", [128, DK, E])
        rb = sb("rb", [128, E])
        gt = sb("gt", [128, 4])
        tg = sb("tg", [128, 4])
        WN = sb("WN", [QC, H // 2, 2, KVC])
        WRA = WE[0:QC, 9216:10240].rearrange("p (m a c) -> p m a c", m=H // 2, a=2)
        WRB = WE[0:QC, 10240:11264].rearrange("p (m a c) -> p m a c", m=H // 2, a=2)
        R2 = sb("R2", [128, 1536])
        CW = sb("CW", [128, H // 2, D])
        Wk2 = sb("Wk2", [128, DK, 2, KVC])
        Wkr2 = sb("Wkr2", [KVC, 2, 2, R])
        Wdqs = sb("Wdqs", [128, DK, QC])
        st = sb("st", [128, NT, 6])
        mv = sb("mv", [128, NT, 2])
        rstd = sb("rstd", [128, NT])
        mhalf = sb("mhalf", [128, NT])
        zero = sb("zero", [128, D])
        zk = sb("zk", [NH0, 384])
        dsb = sb("dsb", [NH0, 1])
        small = sb("small", [128, 64])
        wc = sb("wc", [128, 2, NT])
        slot = sb("slot", [128, 2, NT], i32)
        eid = sb("eid", [128, NB], i32)
        segi = sb("segi", [128, B], i32)
        segf = sb("segf", [128, B])

        AR = sb("AR", [128, 15872])

        def ar(lo, n):
            return AR[:, lo:lo + n]

        T = ar(0, 4096).rearrange("p (h l) -> p h l", h=NH0)
        CS = ar(4096, 4096).rearrange("p (t d) -> p t d", t=NT)
        kv = ar(8192, 2 * DK * NPAIR * B).rearrange("p (u k n) -> p u k n", u=2, k=DK)
        o = 8192 + 2 * DK * NPAIR * B
        prod = ar(o, 2 * DK * 64 * B).rearrange("p (u k n) -> p u k n", u=2, k=DK)
        K01 = ar(0, 2048).rearrange("p (b s) -> p b s", b=B)
        K10 = ar(2048, 2048).rearrange("p (b s) -> p b s", b=B)
        KVr = ar(4096, 1024).rearrange("p (b c) -> p b c", b=B)
        maskb = ar(5120, 1024).bitcast(bf16).rearrange("p (b k) -> p b k", b=B)
        RT = ar(6144, 2048)
        SG = 8192
        uqT = ar(SG, H * QC).rearrange("p (h c) -> p h c", h=H)
        ukT = ar(SG + 1536, H * KVC).rearrange("p (h c) -> p h c", h=H)
        uvT = ar(SG + 2560, H * KVC).rearrange("p (h c) -> p h c", h=H)
        wo = ar(SG + 3584, H * D).rearrange("p (h d) -> p h d", h=H)
        xg = ar(SG, 4 * D).rearrange("p (u d) -> p u d", u=4)
        xgT = ar(SG + 1024, 2 * D).rearrange("p (u k t) -> p u k t", u=2, k=DK)
        sg = ar(SG + 1536, 2 * I).rearrange("p (u d) -> p u d", u=2)
        hh = ar(SG + 1792, 2 * I).rearrange("p (u d) -> p u d", u=2)
        hT = ar(SG + 2048, 2 * I).rearrange("p (u d) -> p u d", u=2)
        yb = ar(SG + 2304, 4 * D).rearrange("p (u d) -> p u d", u=4)
        gb = ar(SG + 3328, 8 * D).rearrange("p (u s d) -> p u s d", u=4, s=2)
        shs = RT[:, 1024:2048].rearrange("p (u n) -> p u n", u=2)
        Q = WE[:, 0:2048].rearrange("p (u h n) -> p u h n", u=2, h=2)
        P = WE[:, 2048:4096].rearrange("p (u i k) -> p u i k", u=2, i=8)
        PT = WE[:, 4096:6144].rearrange("p (u i k) -> p u i k", u=2, i=8)
        ra = WE[:, 6144:7168].rearrange("p (u n) -> p u n", u=2)
        rbm = WE[:, 7168:8192].rearrange("p (u n) -> p u n", u=2)
        O = WE[:, 8192:9216].rearrange("p (u b h c) -> p u b h c", u=2, b=4, h=2)
        OT = CT[:, :, :, :].rearrange("p k t n -> p (k t n)").rearrange("p (m b q) -> p m b q", m=H // 2, b=4)
        XNf = XN[:, :, :].rearrange("p t d -> p (t d)")
        qc = XNf[0:QC, 0:2048]
        w1f = ar(SG, DK * HID).rearrange("p (k n) -> p k n", k=DK)
        w3f = ar(SG + DK * HID, DK * HID).rearrange("p (k n) -> p k n", k=DK)
        w2f = ar(SG + 2 * DK * HID, NC * D).rearrange("p (c d) -> p c d", c=NC)
        o = SG + 2 * DK * HID + NC * D
        w1q = ar(o, HID).bitcast(bf16).rearrange("p (k n) -> p k n", k=DK)
        w3q = ar(o + HID, HID).bitcast(bf16).rearrange("p (k n) -> p k n", k=DK)
        w2q = ar(o + 2 * HID, NC * D // 2).bitcast(bf16).rearrange("p (c d) -> p c d", c=NC)
        CTf = CT[:, :, :, :].rearrange("p k t n -> p (k t n)")
        QTf = QT[:, :, :, :].rearrange("p k t n -> p (k t n)")
        ghi = CTf[:, 0:1536].bitcast(bf16).rearrange("p (c n) -> p c n", c=NC)
        gmid = CTf[:, 1536:3072].bitcast(bf16).rearrange("p (c n) -> p c n", c=NC)
        glo = QTf[:, 0:1536].bitcast(bf16).rearrange("p (c n) -> p c n", c=NC)
        x3n = CTf[:, 3072:4096].rearrange("p (b d) -> p b d", b=4)
        xp = [QTf[:, 1536 + 512 * i:2048 + 512 * i].bitcast(bf16).rearrange("p (k n) -> p k n", k=DK) for i in range(3)]
        xr = QTf[:, 3072:4096].rearrange("p (k n) -> p k n", k=DK)
        sl = XNf[:, 2048:3072].rearrange("p (u n) -> p u n", u=2)
        gg = XNf[:, 3072:4096].rearrange("p (u n) -> p u n", u=2)
        gr = WE[:, 0:1024].rearrange("p (u n) -> p u n", u=2)
        rs = RT[:, 0:16].rearrange("p (u i) -> p u i", u=2)
        nm = RT[:, 16:32].rearrange("p (u i) -> p u i", u=2)
        mx = RT[:, 32:48].rearrange("p (u i) -> p u i", u=2)
        ri = RT[:, 48:64].rearrange("p (u i) -> p u i", u=2)

        PSt = ctx.enter_context(nc.psum_tensor("PS", [128, 8, 512], f32))

        def bank(k, n=1):
            return PSt[:, k, :] if n == 1 else PSt[:, k:k + n, :]

        XG = nc.dram_tensor("XG", [NB * 128, D], f32, kind="Internal").ap()
        YG = nc.dram_tensor("YG", [NB * 128, D], f32, kind="Internal").ap()
        Z = nc.dram_tensor("Z", [NH0, 384], f32, kind="Internal").ap()
        Xm = nc.dram_tensor("Xm", [B, S, D], f32, kind="Internal").ap()

        class Signals:
            pass

        s = Signals()
        s.qr_w = sem("qr_w")
        s.const = sem("const")
        s.small = sem("small")
        s.ssm = sem("ssm")
        s.zinit = sem("zinit")
        s.zk_set = sem("zk_set")
        s.zk_d = sem("zk_d")
        s.zk_out = sem("zk_out")
        s.ctx0 = sem("ctx0")
        s.ctx1 = sem("ctx1")
        s.ctx2 = sem("ctx2")
        s.ctx3 = sem("ctx3")
        s.x0 = sem("x0")
        s.x1 = sem("x1")
        s.x2 = sem("x2")
        s.x3 = sem("x3")
        s.moe_w = sem("moe_w")
        s.shared_w = sem("shared_w")
        s.tg_ready = sem("tg_ready")
        s.memsets = sem("memsets")
        s.ln1_stats = sem("ln1_stats")
        s.rstd1 = sem("rstd1")
        s.xn1 = sem("xn1")
        s.ctx_xp = sem("ctx_xp")
        s.x_xp = sem("x_xp")
        s.ctx_T = sem("ctx_T")
        s.x_T = sem("x_T")
        s.kv_ready = sem("kv_ready")
        s.y_ready = sem("y_ready")
        s.prod_raw = sem("prod_raw")
        s.prod_ready = sem("prod_ready")
        s.out_ready = sem("out_ready")
        s.ln2_stats = sem("ln2_stats")
        s.rstd2 = sem("rstd2")
        s.xn2 = sem("xn2")
        s.xn2_xp = sem("xn2_xp")
        s.xn2_T = sem("xn2_T")
        s.lg_ready = sem("lg_ready")
        s.lg_sb = sem("lg_sb")
        s.dve = sem("dve")
        s.pool = sem("pool")
        s.ab_w = sem("ab_w")
        s.ab_ready = sem("ab_ready")
        s.ab_sb = sem("ab_sb")
        s.cw_ready = sem("cw_ready")
        s.cw_sb = sem("cw_sb")
        s.kc_ready = sem("kc_ready")
        s.kc_sb = sem("kc_sb")
        s.kr_ready = sem("kr_ready")
        s.kr_mul = sem("kr_mul")
        s.kr_sb = sem("kr_sb")
        s.kt_ready = sem("kt_ready")
        s.kt_sb = sem("kt_sb")
        s.mask = sem("mask")
        s.seg = sem("seg")
        s.max_sub = sem("max_sub")
        s.exp_r = sem("exp_r")
        s.onehot = sem("onehot")
        s.counts = sem("counts")
        s.cnt_read = sem("cnt_read")
        s.slots = sem("slots")
        s.sh_up = sem("sh_up")
        s.sh_silu = sem("sh_silu")
        s.sh_h = sem("sh_h")
        s.sh_dn = sem("sh_dn")
        s.sh_res = sem("sh_res")
        s.scat = sem("scat")
        s.xg_xp = sem("xg_xp")
        s.xg_T = sem("xg_T")
        s.gu_ready = sem("gu_ready")
        s.silu = sem("silu")
        s.h_ready = sem("h_ready")
        s.h_xp = sem("h_xp")
        s.h_T = sem("h_T")
        s.y_blk = sem("y_blk")
        s.y_sb = sem("y_sb")
        s.yg0 = sem("yg0")
        s.yg1 = sem("yg1")
        s.yg2 = sem("yg2")
        s.yg3 = sem("yg3")
        s.res2 = sem("res2")
        s.ln3_stats = sem("ln3_stats")
        s.rstd3 = sem("rstd3")
        s.xn3 = sem("xn3")
        s.xm_out = sem("xm_out")
        s.xn3_xp = sem("xn3_xp")
        s.xn3_T = sem("xn3_T")
        s.qc_ready = sem("qc_ready")
        s.qc_sb = sem("qc_sb")
        s.xin = sem("xin")
        s.proj = sem("proj")
        s.rope_mul = sem("rope_mul")
        s.q_n = sem("q_n")
        s.q_r = sem("q_r")
        s.s_ready = sem("s_ready")
        s.max_ready = sem("max_ready")
        s.exp_done = sem("exp_done")
        s.p_xp = sem("p_xp")
        s.pt_a = sem("pt_a")
        s.pt_d = sem("pt_d")
        s.pv_ready = sem("pv_ready")
        s.o_ready = sem("o_ready")
        s.o_xp = sem("o_xp")
        s.ot_ready = sem("ot_ready")
        s.op_ready = sem("op_ready")
        s.res3 = sem("res3")
        s.w_ffn = sem("w_ffn")
        s.w_abs = sem("w_abs")
        s.abs_sum = sem("abs_sum")
        s.scale_r = sem("scale_r")
        s.ternary = sem("ternary")
        s.d_stats = sem("d_stats")
        s.rstd4 = sem("rstd4")
        s.xn4 = sem("xn4")
        s.xn4_xp = sem("xn4_xp")
        s.split_hi = sem("split_hi")
        s.split_r = sem("split_r")
        s.split_mid = sem("split_mid")
        s.split_lo = sem("split_lo")
        s.up_ready = sem("up_ready")
        s.up_silu = sem("up_silu")
        s.g_ready = sem("g_ready")
        s.g_hi = sem("g_hi")
        s.g_r = sem("g_r")
        s.g_mid = sem("g_mid")
        s.g_lo = sem("g_lo")
        s.dn_ready = sem("dn_ready")
        s.yout = sem("yout")
        s.out_dma = sem("out_dma")
        xg_in = [sem(f"xg_in{i}") for i in range(4)]
        toep = [sem(f"toep{i}") for i in range(4)]
        gat = [sem(f"gat{i}") for i in range(4)]
        ctx_in = [s.ctx0, s.ctx1, s.ctx2, s.ctx3]
        x_in = [s.x0, s.x1, s.x2, s.x3]
        yg_out = [s.yg0, s.yg1, s.yg2, s.yg3]
        block = ctx.enter_context(nc.Block())

        @block.sync
        def _(sp):
            sp.dma_start(cf[:, :], constf).then_inc(s.const, 16)
            for c in range(4):
                for j in range(HD0):
                    src = x.rearrange("b (h j) d -> j b h d", j=HD0)[j]
                    sp.dma_start(X[j * B:(j + 1) * B, 4 * c:4 * c + 4, :], src[:, 4 * c:4 * c + 4, :]).then_inc(x_in[c], 16)
            for dst, src in ((rb[:, :], rbias.unsqueeze(0).to_broadcast([128, E])),
                             (Wr[:, :, :], WrT.rearrange("(k p) e -> p k e", p=128)),
                             (sWgu[:, :, 0, :], sWg.rearrange("(k p) c -> p k c", p=128)),
                             (sWgu[:, :, 1, :], sWu.rearrange("(k p) c -> p k c", p=128)),
                             (sWdn[:, :], sWd)):
                sp.dma_start(dst, src).then_inc(s.shared_w, 16)
            for k in range(DK):
                for c, w in ((0, Wg), (1, Wu)):
                    sp.dma_start(WGU[:, k, :, c * I:(c + 1) * I],
                                 w.rearrange("e (k p) c -> k p e c", p=128)[k]).then_inc(s.moe_w, 16)
            sp.dma_start(WD, Wd.rearrange("e p d -> p e d")).then_inc(s.moe_w, 16)
            sp.wait_ge(s.memsets, 1)
            XGz = XG.rearrange("(n p) d -> p n d", p=128)
            for c in range(0, NB, 12):
                n = min(12, NB - c)
                sp.dma_start(XGz[:, c:c + n, :], zero[:, :].unsqueeze(1).to_broadcast([128, n, D])).then_inc(s.zinit, 16)
            for a in range(2):
                sp.dma_start(Wk2[:, :, a, :], Wkvc.rearrange("(k p) c -> p k c", p=128)).then_inc(s.ab_w, 16)
                sp.dma_start(Wkr2[:, 0, a, :], Wkr).then_inc(s.ab_w, 16)
                for z in range(2):
                    sp.dma_start(Wkr2[:, 1, a, z * 32:z * 32 + 32], Wkr[:, (1 - z) * 32:(1 - z) * 32 + 32]).then_inc(s.ab_w, 16)
            sp.dma_start(Wdqs[:, :, :], Wdq.rearrange("(k p) c -> p k c", p=128)).then_inc(s.ab_w, 16)
            sp.dma_start(segi[:, :], segT).then_inc(s.seg, 16)
            sp.wait_ge(s.out_ready, NT)
            for dst, src in ((uqT, WuqT), (ukT, WukT), (uvT, WuvT), (wo, Wo)):
                sp.dma_start(dst, src.rearrange("(h p) c -> p h c", p=128)).then_inc(s.ab_w, 16)
            sp.wait_ge(s.scat, 2 * NT * 16)
            sp.wait_ge(s.cw_ready, 4)
            sp.wait_ge(s.ab_ready, 2)
            for n in range(NB):
                if n >= 4:
                    sp.wait_ge(s.xg_xp, n - 3)
                sp.dma_start(xg[:, n % 4, :], XG[n * 128:(n + 1) * 128, :]).then_inc(xg_in[n % 4], 16)
            sp.wait_ge(s.y_blk, NB)
            for a in range(2):
                src = Wqr.rearrange("q (m a c) -> q m a c", a=2, c=R)[:, :, 1 - a, :]
                sp.dma_start(WRA[:, :, a, :], src).then_inc(s.qr_w, 16)
                for z in range(2):
                    sp.dma_start(WRB[:, :, a, z * 32:z * 32 + 32], src[:, :, (1 - z) * 32:(1 - z) * 32 + 32]).then_inc(s.qr_w, 16)
            for c in range(4):
                sp.wait_ge(s.res2, 4 * (c + 1))
                for j in range(HD0):
                    dst = Xm.rearrange("b (h j) d -> j b h d", j=HD0)[j]
                    sp.dma_start(dst[:, 4 * c:4 * c + 4, :], X[j * B:(j + 1) * B, 4 * c:4 * c + 4, :]).then_inc(s.xm_out, 16)
            sp.dma_start(w1f, w1T.rearrange("(k p) n -> p k n", p=128)).then_inc(s.w_ffn, 16)
            sp.dma_start(w3f, w3T.rearrange("(k p) n -> p k n", p=128)).then_inc(s.w_ffn, 16)
            sp.wait_ge(s.w_abs, 1)
            sp.dma_start(w2f[:, 0:NC - 1, :], w2T[0:(NC - 1) * 128, :].rearrange("(c p) d -> p c d", p=128)).then_inc(s.w_ffn, 16)
            sp.dma_start(w2f[0:HID - (NC - 1) * 128, NC - 1, :], w2T[(NC - 1) * 128:HID, :]).then_inc(s.w_ffn, 16)
            sp.wait_ge(s.xm_out, 4 * HD0 * 16)
            sp.wait_ge(s.xn3, NT)
            sp.dma_start(X[:, :, :], Xm.rearrange("b s d -> s b d")).then_inc(s.xin, 16)
            for b in range(B):
                sp.wait_ge(s.yout, b + 1)
                sp.dma_start(out[b], X[:, b, :]).then_inc(s.out_dma, 16)
            sp.wait_ge(s.out_dma, B * 16)

        @block.scalar
        def _(act):
            act.dma_start(gt[:, :], gates.unsqueeze(0).to_broadcast([128, 4])).then_inc(s.small, 16)
            act.wait_ge(s.zk_set, 1)
            act.dma_start(zk[:, 127:383], ssm).then_inc(s.ssm, 16)
            act.dma_start(dsb[:, :], ssmD.unsqueeze(1)).then_inc(s.ssm, 16)
            for c in range(4):
                for j in range(HD0):
                    src = ctxd.rearrange("b (h j) d -> j b h d", j=HD0)[j]
                    act.dma_start(CS[j * B:(j + 1) * B, 4 * c:4 * c + 4, :], src[:, 4 * c:4 * c + 4, :]).then_inc(ctx_in[c], 16)
            act.wait_ge(s.zk_d, 1)
            act.dma_start(Z, zk[:, :]).then_inc(s.zk_out, 16)
            act.wait_ge(s.zk_out, 16)
            for h in range(0, NH0, 4):
                src = bass.AP(Z.tensor, 384 * h, [[1, 128], [384, 4], [1, 256]])
                act.dma_start(T[:, h:h + 4, :], src).then_inc(toep[h // 4], 16)
            act.wait_ge(s.small, 16)
            nc.scalar.activation(tg[:, :], gt[:, :], ACT.Tanh).then_inc(s.tg_ready, 1)
            for u in range(NT // 2):
                act.wait_ge(s.ctx_xp, u + 1)
                nc.scalar.activation(CT[:, :, 2 * u:2 * u + 2, :],
                                     bank(2 * (u % 2)).rearrange("p (t k n) -> p k t n", t=2, k=DK), ACT.Copy).then_inc(s.ctx_T, 1)
            for u in range(NT // 2):
                act.wait_ge(s.xn2_xp, u + 1)
                nc.scalar.activation(QT[:, :, 2 * u:2 * u + 2, :],
                                     bank(u % 4).rearrange("p (t k n) -> p k t n", t=2, k=DK), ACT.Copy).then_inc(s.xn2_T, 1)
            act.wait_ge(s.max_sub, 1)
            L = RT[:, 0:256]
            nc.scalar.activation(L, L, ACT.Exp).then_inc(s.exp_r, 1)
            for g in range(4):
                act.wait_ge(s.sh_up, g + 1)
                if g >= 2:
                    act.wait_ge(s.sh_h, g - 1)
                nc.scalar.activation(shs[:, g % 2, :], bank(2 * (g % 2)), ACT.Silu).then_inc(s.sh_silu, 1)
            for c in range(2):
                act.wait_ge(s.ab_ready, c + 1)
                nc.scalar.activation(WN[:, 4 * c:4 * c + 4, :, :], bank(4 + c)[0:QC, :].rearrange("p (m a c) -> p m a c", a=2, c=KVC),
                                     ACT.Copy).then_inc(s.ab_sb, 1)
            for c in range(4):
                act.wait_ge(s.cw_ready, c + 1)
                nc.scalar.activation(CW[:, 2 * c:2 * c + 2, :], bank(6 + c % 2).rearrange("p (m d) -> p m d", m=2),
                                     ACT.Copy).then_inc(s.cw_sb, 1)
            for c in range(4):
                act.wait_ge(s.kc_ready, c + 1)
                for lo, dst in ((0, K01), (64, K10)):
                    for j4 in range(4):
                        h = 4 * c + j4
                        ins = nc.scalar.activation(
                            dst[lo:lo + 64, :, h * HD0:(h + 1) * HD0].rearrange("p b j -> p j b"),
                            bank(c % 2)[lo:lo + 64, j4 * 128:(j4 + 1) * 128].rearrange("p (j b) -> p j b", j=HD0), ACT.Copy)
                ins.then_inc(s.kc_sb, 1)
            for c in range(2):
                act.wait_ge(s.kt_ready, c + 1)
                nc.scalar.activation(KVr[:, 8 * c:8 * c + 8, :], bank(6 + c).rearrange("p (b c) -> p b c", b=8), ACT.Copy).then_inc(s.kt_sb, 1)
            for n in range(NB + 4):
                if n < NB:
                    act.wait_ge(s.xg_xp, n + 1)
                    if n >= 2:
                        act.wait_ge(s.gu_ready, n - 1)
                    nc.scalar.activation(xgT[:, n % 2, :, :], bank(n % 2)[:, 0:256].rearrange("p (k t) -> p k t", k=DK),
                                         ACT.Copy).then_inc(s.xg_T, 1)
                m = n - 1
                if 0 <= m < NB:
                    act.wait_ge(s.gu_ready, m + 1)
                    if m >= 2:
                        act.wait_ge(s.h_ready, m - 1)
                    nc.scalar.activation(sg[:, m % 2, :], bank(2 + m % 2)[:, 0:I], ACT.Silu).then_inc(s.silu, 1)
                m = n - 4
                if m >= 0:
                    act.wait_ge(s.y_sb, m + 1)
                    act.dma_start(YG[m * 128:(m + 1) * 128, :], yb[:, m % 4, :]).then_inc(yg_out[m % 4], 16)
            QTp = QT[:, :, :, :].rearrange("p k t n -> p k (t n)").rearrange("p k (b s) -> p k b s", b=B)
            for t in range(NT):
                act.wait_ge(s.xn3_xp, t + 1)
                for k in range(DK):
                    ins = nc.scalar.activation(QTp[:, k, :, t * HD0:(t + 1) * HD0].rearrange("p b j -> p j b"),
                                               bank(t % 4)[:, k * 128:(k + 1) * 128].rearrange("p (j b) -> p j b", j=HD0), ACT.Copy)
                ins.then_inc(s.xn3_T, 1)
            for c in range(4):
                act.wait_ge(s.qc_ready, c + 1)
                nc.scalar.activation(qc[:, c * 512:(c + 1) * 512], bank(4 + c)[0:QC, :], ACT.Copy).then_inc(s.qc_sb, 1)

            def q_nope(u):
                act.wait_ge(s.proj, u + 1)
                if u >= 2:
                    act.wait_ge(s.s_ready, u - 1)
                nc.scalar.activation(Q[0:64, u % 2, 0, :], bank(2)[0:64, :], ACT.Copy)
                nc.scalar.activation(Q[64:128, u % 2, 1, :], bank(2)[64:128, :], ACT.Copy).then_inc(s.q_n, 1)

            q_nope(0)
            for u in range(33):
                if u < 32:
                    act.wait_ge(s.max_ready, u + 1)
                    if u >= 2:
                        act.wait_ge(s.p_xp, u - 1)
                        act.wait_ge(s.o_ready, u - 1)
                    for i in range(8):
                        ins = nc.scalar.activation(P[:, u % 2, i, :], bank(i // 4)[:, (i % 4) * 128:(i % 4 + 1) * 128], ACT.Exp,
                                                   bias=nm[:, u % 2, i:i + 1], scale=SCALE, accum_out=rs[:, u % 2, i:i + 1])
                    ins.then_inc(s.exp_done, 1)
                    if u + 1 < 32:
                        q_nope(u + 1)
                if u >= 1:
                    act.wait_ge(s.o_xp, u)
                    if u - 1 >= 8:
                        act.wait_ge(s.op_ready, 2 * ((u - 1) // 8))
                    nc.scalar.activation(OT[:, (u - 1) % 8, :, :], bank(7).rearrange("p (b q) -> p b q", b=4), ACT.Copy).then_inc(s.ot_ready, 1)
                if u < 32:
                    act.wait_ge(s.p_xp, u + 1)
                    if u >= 2:
                        act.wait_ge(s.pv_ready, u - 1)
                    nc.scalar.activation(PT[:, u % 2, 0:4, :], bank(5).rearrange("p (i q) -> p i q", i=4), ACT.Copy).then_inc(s.pt_a, 1)
            act.wait_ge(s.w_ffn, 64)
            for i, w in enumerate((w1f, w3f, w2f)):
                w = w.rearrange("p k n -> p (k n)")
                ins = nc.scalar.activation(WE[:, 1024:1024 + w.shape[1]], w, ACT.Abs, accum_out=small[:, 32 + i:33 + i])
                ins.then_inc(s.abs_sum, 1)
                act.wait_ge(s.abs_sum, i + 1)
            for g in range(4):
                for t in range(2):
                    act.wait_ge(s.xn4_xp, 2 * g + t + 1)
                    if g >= 1:
                        act.wait_ge(s.up_ready, NC * g)
                    nc.scalar.activation(xp[0][:, :, t * 256:(t + 1) * 256],
                                         bank(t).rearrange("p (k n) -> p k n", k=DK), ACT.Copy).then_inc(s.split_hi, 1)
                for c in range(NC):
                    n = NC * g + c
                    m = min(128, HID - c * 128)
                    act.wait_ge(s.up_ready, n + 1)
                    if n >= 2:
                        act.wait_ge(s.g_ready, n - 1)
                    nc.scalar.activation(sl[0:m, n % 2, :], bank(2 + 2 * (n % 2))[0:m, :], ACT.Silu,
                                         scale=small[0:m, 40:41]).then_inc(s.up_silu, 1)
                    act.wait_ge(s.g_ready, n + 1)
                    if g >= 1:
                        act.wait_ge(s.dn_ready, 4 * g)
                    nc.scalar.activation(ghi[0:m, c, :], gg[0:m, n % 2, :], ACT.Copy).then_inc(s.g_hi, 1)

        @block.tensor
        def _(pe):
            mm = nc.tensor.matmul
            tr = nc.tensor.transpose
            pe.wait_ge(s.const, 16)
            for u in range(NT // 2):
                pe.wait_ge(ctx_in[u // 2], HD0 * 16)
                if u >= 2:
                    pe.wait_ge(s.ctx_T, u - 1)
                for t in range(2):
                    for k in range(DK):
                        ins = tr(bank(2 * (u % 2))[:, (2 * t + k) * 128:(2 * t + k + 1) * 128],
                                 CS[:, 2 * u + t, k * 128:(k + 1) * 128], ident)
                ins.then_inc(s.ctx_xp, 1)
                pe.wait_ge(s.xn1, 2 * u + 2)
                if u >= 2:
                    pe.wait_ge(s.x_T, u - 1)
                for t in range(2):
                    for k in range(DK):
                        ins = tr(bank(2 * (u % 2) + 1)[:, (2 * t + k) * 128:(2 * t + k + 1) * 128],
                                 XN[:, 2 * u + t, k * 128:(k + 1) * 128], ident)
                ins.then_inc(s.x_xp, 1)

            def conv(h):
                pe.wait_ge(s.kv_ready, h + 1)
                if h % 4 == 0:
                    pe.wait_ge(toep[h // 4], 16)
                if h == 0:
                    pe.wait_ge(s.ctx_T, NT // 2)
                    pe.wait_ge(s.x_T, NT // 2)
                if h >= 2:
                    pe.wait_ge(s.prod_raw, h - 1)
                p = 3 * (h % 2)
                for lo, dst, n0, n in ((0, bank(p)[:, 0:PA * B], 0, PA * B), (0, bank(p + 2)[:, 0:PB * B], PA * B, PB * B),
                                       (1, bank(p + 1)[:, 0:PA * B], 0, PA * B),
                                       (1, bank(p + 2)[:, PB * B:2 * PB * B], PA * B, PB * B)):
                    for k in range(lo + 1):
                        ins = mm(dst, T[:, h, (lo - k) * 128:(lo - k + 1) * 128], kv[:, h % 2, k, n0:n0 + n],
                                 start=(k == 0), stop=(k == lo))
                ins.then_inc(s.y_ready, 1)

            def token_sum(t):
                pe.wait_ge(s.prod_ready, t + 1)
                if t >= 2:
                    pe.wait_ge(s.ln2_stats, t - 1)
                for k in range(DK):
                    for i in range(4):
                        ins = mm(bank(6 + t % 2)[:, k * 128:(k + 1) * 128], prod[:, t % 2, k, i * 128:(i + 1) * 128], ident,
                                 start=(i == 0), stop=(i == 3))
                ins.then_inc(s.out_ready, 1)

            for h in range(NT + 1):
                if h < NT:
                    conv(h)
                if h >= 1:
                    token_sum(h - 1)
            pe.wait_ge(s.prod_raw, NT)
            pe.wait_ge(s.shared_w, 5 * 16)
            for u in range(NT // 2 + 2):
                if u < NT // 2:
                    pe.wait_ge(s.xn2, 2 * u + 2)
                    if u >= 4:
                        pe.wait_ge(s.xn2_T, u - 3)
                    for t in range(2):
                        for k in range(DK):
                            ins = tr(bank(u % 4)[:, (2 * t + k) * 128:(2 * t + k + 1) * 128], XN[:, 2 * u + t, k * 128:(k + 1) * 128], ident)
                    ins.then_inc(s.xn2_xp, 1)
                if u >= 2:
                    pe.wait_ge(s.xn2_T, u - 1)
                    for t in range(2 * u - 4, 2 * u - 2):
                        for k in range(DK):
                            ins = mm(bank(4)[:, t * E:(t + 1) * E], QT[:, k, t, :], Wr[:, k, :], start=(k == 0), stop=(k == DK - 1))
            ins.then_inc(s.lg_ready, 1)

            def sh_down(g):
                pe.wait_ge(s.sh_h, g + 1)
                if g >= 1:
                    pe.wait_ge(s.sh_res, g)
                if g == 0:
                    pe.wait_ge(s.lg_sb, 1)
                for t in range(4):
                    ins = mm(bank(4 + t // 2)[:, (t % 2) * 256:(t % 2 + 1) * 256], shs[:, g % 2, t * 128:(t + 1) * 128], sWdn[:, :],
                             start=True, stop=True)
                ins.then_inc(s.sh_dn, 1)

            Mb = RT[:, 768:896].bitcast(bf16)
            pe.wait_ge(s.xn2_T, NT // 2)
            for g in range(4):
                if g >= 2:
                    pe.wait_ge(s.sh_h, g - 1)
                for c in range(2):
                    for k in range(DK):
                        ins = mm(bank(2 * (g % 2) + c), sWgu[:, k, c, :], QT[:, k, 4 * g:4 * g + 4, :].rearrange("p t n -> p (t n)"),
                                 start=(k == 0), stop=(k == DK - 1))
                ins.then_inc(s.sh_up, 1)
                if g == 1:
                    pe.wait_ge(s.onehot, 1)
                    mm(bank(6)[:, 0:256], trib, Mb, start=True, stop=True)
                    mm(bank(6)[:, 256:512], onesb[:, :], Mb, start=True, stop=True).then_inc(s.counts, 1)
                if g >= 1:
                    sh_down(g - 1)
            sh_down(3)
            pe.wait_ge(s.ab_w, 13 * 16)
            pe.wait_ge(s.sh_res, 4)
            for c in range(2):
                for i in range(8):
                    h = 8 * c + i
                    ins = mm(bank(4 + c)[0:QC, i * KVC:(i + 1) * KVC], uqT[:, h, :], ukT[:, h, :], start=True, stop=True)
                ins.then_inc(s.ab_ready, 1)
            pe.wait_ge(s.cnt_read, 1)
            for c in range(4):
                if c >= 2:
                    pe.wait_ge(s.cw_sb, c - 1)
                for i in range(4):
                    h = 4 * c + i
                    lo = 64 * (h % 2)
                    ins = mm(bank(6 + c % 2)[lo:lo + 64, (i // 2) * 256:(i // 2 + 1) * 256], uvT[:, h, :], wo[:, h, :],
                             start=True, stop=True)
                ins.then_inc(s.cw_ready, 1)
            for c in range(4):
                if c >= 2:
                    pe.wait_ge(s.kc_sb, c - 1)
                for k in range(DK):
                    ins = mm(bank(c % 2), Wk2[:, k, :, :].rearrange("p a c -> p (a c)"),
                             CT[:, k, 4 * c:4 * c + 4, :].rearrange("p t n -> p (t n)"), start=(k == 0), stop=(k == DK - 1))
                ins.then_inc(s.kc_ready, 1)
            pe.wait_ge(s.kc_sb, 4)
            for c in range(4):
                if c >= 1:
                    pe.wait_ge(s.kr_mul, c)
                for z in range(2):
                    ins = mm(bank(2 + z), Wkr2[:, z, :, :].rearrange("p a c -> p (a c)"),
                             K01[0:64, 4 * c:4 * c + 4, :].rearrange("p b s -> p (b s)"), start=True, stop=True)
                ins.then_inc(s.kr_ready, 1)
            pe.wait_ge(s.cw_sb, 4)
            for c in range(2):
                for i in range(8):
                    ins = tr(bank(6 + c)[:, i * 64:(i + 1) * 64], K01[0:64, 8 * c + i, :], ident[0:64, 0:64])
                ins.then_inc(s.kt_ready, 1)
            pe.wait_ge(s.slots, 1)
            pe.wait_ge(s.moe_w, 5 * 16)
            pe.wait_ge(s.kt_sb, 2)
            pe.wait_ge(s.kr_mul, 4)
            experts = {}
            for n in range(NB + 3):
                if n < NB:
                    pe.wait_ge(xg_in[n % 4], 16 * (n // 4 + 1))
                    if n >= 2:
                        pe.wait_ge(s.xg_T, n - 1)
                    for k in range(DK):
                        ins = tr(bank(n % 2)[:, k * 128:(k + 1) * 128], xg[:, n % 4, k * 128:(k + 1) * 128], ident)
                    ins.then_inc(s.xg_xp, 1)
                m = n - 1
                if 0 <= m < NB:
                    e = pe.value_load(eid[0:1, m:m + 1], min_val=0, max_val=E - 1)
                    experts[m] = e
                    pe.wait_ge(s.xg_T, m + 1)
                    if m >= 2:
                        pe.wait_ge(s.h_ready, m - 1)
                    for k in range(DK):
                        ins = mm(bank(2 + m % 2)[:, 0:2 * I], xgT[:, m % 2, k, :], WGU[:, k, bass.ds(e, 1), :].rearrange("p e c -> p (e c)"),
                                 start=(k == 0), stop=(k == DK - 1))
                    ins.then_inc(s.gu_ready, 1)
                m = n - 2
                if 0 <= m < NB:
                    pe.wait_ge(s.h_ready, m + 1)
                    if m >= 2:
                        pe.wait_ge(s.h_T, m - 1)
                    tr(bank(4 + m % 2)[:, 0:I], hh[:, m % 2, :], ident).then_inc(s.h_xp, 1)
                m = n - 3
                if 0 <= m < NB:
                    pe.wait_ge(s.h_T, m + 1)
                    if m >= 2:
                        pe.wait_ge(s.y_sb, m - 1)
                    mm(bank(6 + m % 2)[:, 0:D], hT[:, m % 2, :], WD[:, bass.ds(experts.pop(m), 1), :].rearrange("p e d -> p (e d)"),
                       start=True, stop=True).then_inc(s.y_blk, 1)
            for t in range(NT):
                pe.wait_ge(s.xn3, t + 1)
                if t >= 4:
                    pe.wait_ge(s.xn3_T, t - 3)
                for k in range(DK):
                    ins = tr(bank(t % 4)[:, k * 128:(k + 1) * 128], XN[:, t, k * 128:(k + 1) * 128], ident)
                ins.then_inc(s.xn3_xp, 1)
            pe.wait_ge(s.xn3_T, NT)
            QTc = QT[:, :, :, :].rearrange("p k t n -> p k (t n)")
            for c in range(4):
                for k in range(DK):
                    ins = mm(bank(4 + c)[0:QC, :], Wdqs[:, k, :], QTc[:, k, c * 512:(c + 1) * 512], start=(k == 0), stop=(k == DK - 1))
                ins.then_inc(s.qc_ready, 1)

            def project(u):
                g, m = u // 8, u % 8
                if u == 0:
                    pe.wait_ge(s.qc_sb, 4)
                else:
                    pe.wait_ge(s.q_n, u)
                    pe.wait_ge(s.rope_mul, u)
                if m == 2 and g >= 1:
                    pe.wait_ge(s.res3, 2 * g)
                for z, w in enumerate((WN, WRA, WRB)):
                    ins = mm(bank(2 + z), w[:, m, :, :].rearrange("p a c -> p (a c)"), qc[:, g * 512:(g + 1) * 512], start=True, stop=True)
                ins.then_inc(s.proj, 1)

            def scores(u):
                g = u // 8
                pe.wait_ge(s.q_n, u + 1)
                pe.wait_ge(s.q_r, 2 * u + 2)
                if u >= 1:
                    pe.wait_ge(s.exp_done, u)
                for a, keys in enumerate((K01, K10)):
                    mm(bank(a), identb, maskb[:, 4 * g:4 * g + 4, :].rearrange("p b k -> p (b k)"), start=True, stop=False)
                    for b in range(4):
                        ins = mm(bank(a)[:, b * 128:(b + 1) * 128], Q[:, u % 2, a, b * 128:(b + 1) * 128], keys[:, 4 * g + b, :],
                                 start=False, stop=(b == 3))
                ins.then_inc(s.s_ready, 1)

            def attend(u):
                g = u // 8
                pe.wait_ge(s.pt_a, u + 1)
                pe.wait_ge(s.pt_d, u + 1)
                if u >= 1:
                    pe.wait_ge(s.ot_ready, u)
                for i in range(8):
                    ins = mm(bank(7)[:, i * 64:(i + 1) * 64], PT[:, u % 2, i, :], KVr[:, 4 * g + i % 4, :], start=True, stop=True)
                ins.then_inc(s.pv_ready, 1)

            pe.wait_ge(s.mask, 2)
            pe.wait_ge(s.kr_sb, 4)
            pe.wait_ge(s.qr_w, 6 * 16)
            project(0)
            for u in range(33):
                if u < 32:
                    scores(u)
                if u >= 1:
                    attend(u - 1)
                if u + 1 < 32:
                    project(u + 1)
                if u >= 1:
                    pe.wait_ge(s.o_ready, u)
                    for b in range(4):
                        ins = tr(bank(7)[:, b * 128:(b + 1) * 128], O[:, (u - 1) % 2, b, :, :].rearrange("p h c -> p (h c)"), ident)
                    ins.then_inc(s.o_xp, 1)
                if u < 32:
                    pe.wait_ge(s.exp_done, u + 1)
                    if u >= 1:
                        pe.wait_ge(s.pt_a, u)
                        pe.wait_ge(s.pt_d, u)
                    for i in range(8):
                        ins = tr(bank(5 + i // 4)[:, (i % 4) * 128:(i % 4 + 1) * 128], P[:, u % 2, i, :], ident)
                    ins.then_inc(s.p_xp, 1)
                if u >= 1 and (u - 1) % 8 == 7:
                    pe.wait_ge(s.ot_ready, u)
                    pe.wait_ge(s.rope_mul, min(u + 2, 32))
                    for b in range(4):
                        for m in range(H // 2):
                            ins = mm(bank(3 + b // 2)[:, (b % 2) * 256:(b % 2 + 1) * 256], OT[:, m, b, :], CW[:, m, :],
                                     start=(m == 0), stop=(m == H // 2 - 1))
                        if b % 2:
                            ins.then_inc(s.op_ready, 1)
            pe.wait_ge(s.abs_sum, 3)
            pe.wait_ge(s.res3, 8)
            mm(bank(7)[:, 0:3], onesf[:, :], small[:, 32:35], start=True, stop=True).then_inc(s.scale_r, 1)
            for g in range(4):
                for t in range(2):
                    pe.wait_ge(s.xn4, 4 * g + 2 * t + 2)
                    if g >= 1:
                        pe.wait_ge(s.split_r, 2 * (g - 1) + t + 1)
                    for b in range(2):
                        for k in range(DK):
                            ins = tr(bank(t)[:, k * 256 + b * 128:k * 256 + (b + 1) * 128], x3n[:, 2 * t + b, k * 128:(k + 1) * 128], ident)
                    ins.then_inc(s.xn4_xp, 1)
                if g == 0:
                    pe.wait_ge(s.ternary, 3)
                pe.wait_ge(s.split_lo, 2 * g + 2)
                for c in range(NC):
                    n = NC * g + c
                    m = min(128, HID - c * 128)
                    if n >= 2:
                        pe.wait_ge(s.g_ready, n - 1)
                    for z, w in enumerate((w1q, w3q)):
                        for k in range(DK):
                            for q in range(3):
                                ins = mm(bank(2 + 2 * (n % 2) + z)[0:m, :], w[:, k, c * 128:c * 128 + m], xp[q][:, k, :],
                                         start=(k == 0 and q == 0), stop=(k == DK - 1 and q == 2))
                    ins.then_inc(s.up_ready, 1)
                pe.wait_ge(s.g_lo, NC * (g + 1))
                for b in range(4):
                    if g >= 1 or b >= 2:
                        pe.wait_ge(s.yout, 4 * g + b - 1)
                    for c in range(NC):
                        m = min(128, HID - c * 128)
                        for q, part in enumerate((ghi, gmid, glo)):
                            ins = mm(bank(6 + b % 2)[:, 0:D], part[0:m, c, b * 128:(b + 1) * 128], w2q[0:m, c, :],
                                     start=(c == 0 and q == 0), stop=(c == NC - 1 and q == 2))
                    ins.then_inc(s.dn_ready, 1)

        @block.gpsimd
        def _(pool):
            tt = nc.gpsimd.tensor_tensor
            nc.gpsimd.memset(zero[:, :], 0.0).then_inc(s.memsets, 1)
            nc.gpsimd.memset(mhalf[:, :], -0.5)
            nc.gpsimd.memset(onesb[:, :], 1.0)
            nc.gpsimd.memset(onesf[:, :], 1.0).then_inc(s.memsets, 1)
            pool.wait_ge(s.memsets, 2)
            done = [0]

            def rsqrt(lo, n, wait, value, signal):
                pool.wait_ge(wait, value)
                nc.gpsimd.tensor_scalar(rstd[:, lo:lo + n], mv[:, lo:lo + n, 1], LN_EPS, None, ALU.add).then_inc(s.pool, 1)
                done[0] += 1
                pool.wait_ge(s.pool, done[0])
                tt(rstd[:, lo:lo + n], rstd[:, lo:lo + n], mhalf[:, lo:lo + n], ALU.pow).then_inc(signal, 1)

            for c in range(4):
                rsqrt(4 * c, 4, s.ln1_stats, c + 1, s.rstd1)

            def products(h):
                pool.wait_ge(s.ctx_T, h // 2 + 1)
                if h >= 2:
                    pool.wait_ge(s.y_ready, h - 1)
                for i in range(HD0):
                    n = i + 1
                    c = CT[:, :, h, :]
                    ins = tt(kv[:, h % 2, :, pair(i) * B:(pair(i) + n) * B].rearrange("p k (j b) -> p k j b", b=B),
                             c[:, :, 0:n * B].rearrange("p k (j b) -> p k j b", b=B),
                             c[:, :, i * B:(i + 1) * B].unsqueeze(2).to_broadcast([128, DK, n, B]), ALU.mult)
                ins.then_inc(s.kv_ready, 1)

            products(0)
            products(1)
            for h in range(NT):
                if h + 2 < NT:
                    products(h + 2)
                rsqrt(h, 1, s.ln2_stats, h + 1, s.rstd2)
            pool.wait_ge(s.zinit, 4 * 16)
            pool.wait_ge(s.slots, 1)
            pool.wait_ge(s.xn2, NT)
            for t in range(NT):
                for q in range(2):
                    pool.indirect_dma_start(out=XG, out_offset=bass.IndirectOffsetOnAxis(ap=slot[:, q, t:t + 1], axis=0),
                                            in_=XN[:, t, :], in_offset=None).then_inc(s.scat, 16)
            for i in range(4):
                pool.wait_ge(yg_out[i], 16 * ((NB - i + 3) // 4))
            for t in range(NT):
                if t >= 4:
                    pool.wait_ge(s.res2, t - 3)
                for q in range(2):
                    pool.indirect_dma_start(out=gb[:, t % 4, q, :], out_offset=None, in_=YG,
                                            in_offset=bass.IndirectOffsetOnAxis(ap=slot[:, q, t:t + 1], axis=0)).then_inc(gat[t % 4], 16)
                if t >= 4:
                    rsqrt(t - 4, 1, s.ln3_stats, t - 3, s.rstd3)
            for t in range(NT - 4, NT):
                rsqrt(t, 1, s.ln3_stats, t + 1, s.rstd3)
            for u in range(32):
                pool.wait_ge(s.rope_mul, u + 1)
                if u >= 2:
                    pool.wait_ge(s.s_ready, u - 1)
                tt(Q[64:128, u % 2, 0, :], ra[64:128, u % 2, :], rbm[64:128, u % 2, :], ALU.add).then_inc(s.q_r, 1)
                pool.wait_ge(s.q_r, 2 * u + 1)
                tt(Q[0:64, u % 2, 1, :], ra[0:64, u % 2, :], rbm[0:64, u % 2, :], ALU.add).then_inc(s.q_r, 1)
                pool.wait_ge(s.q_r, 2 * u + 2)
            for g in range(4):
                rsqrt(4 * g, 4, s.d_stats, g + 1, s.rstd4)
                for t in range(2):
                    pool.wait_ge(s.split_r, 2 * g + t + 1)
                    nc.gpsimd.tensor_copy(xp[1][:, :, t * 256:(t + 1) * 256], xr[:, :, t * 256:(t + 1) * 256]).then_inc(s.split_mid, 1)
                for c in range(NC):
                    m = min(128, HID - c * 128)
                    pool.wait_ge(s.g_r, NC * g + c + 1)
                    nc.gpsimd.tensor_copy(gmid[0:m, c, :], gr[0:m, c % 2, :]).then_inc(s.g_mid, 1)

        @block.vector
        def _(dve):
            tt = nc.vector.tensor_tensor
            ts = nc.vector.tensor_scalar
            stt = nc.vector.scalar_tensor_tensor
            red = nc.vector.tensor_reduce
            steps = [0]

            def link(ins):
                steps[0] += 1
                ins.then_inc(s.dve, 1)
                dve.wait_ge(s.dve, steps[0])

            def stats(t, wait_last, signal):
                link(nc.vector.bn_stats(st[:, t, :], X[:, t, :]))
                ins = nc.vector.bn_aggr(mv[:, t, :], st[:, t, :])
                if signal is not None:
                    ins.then_inc(signal, 1)

            def normalise(t, dst):
                return ts(dst, X[:, t, :], mv[:, t, 0:1], rstd[:, t:t + 1], ALU.subtract, ALU.mult)

            link(nc.vector.memset(zk[:, :], 0.0))
            nc.vector.tensor_copy(dsb[:, :], zk[:, 0:1]).then_inc(s.zk_set, 1)
            dve.wait_ge(s.ssm, 32)
            tt(zk[:, 127:128], zk[:, 127:128], dsb[:, :], ALU.add).then_inc(s.zk_d, 1)
            for c in range(5):
                if c < 4:
                    dve.wait_ge(x_in[c], HD0 * 16)
                    for t in range(4 * c, 4 * c + 4):
                        stats(t, None, s.ln1_stats if t == 4 * c + 3 else None)
                if c >= 1:
                    dve.wait_ge(s.rstd1, c)
                    for t in range(4 * c - 4, 4 * c):
                        normalise(t, XN[:, t, :]).then_inc(s.xn1, 1)
            for u in range(NT // 2):
                dve.wait_ge(s.x_xp, u + 1)
                nc.vector.tensor_copy(QT[:, :, 2 * u:2 * u + 2, :].rearrange("p k t n -> p t k n"),
                                      bank(2 * (u % 2) + 1).rearrange("p (t k n) -> p t k n", t=2, k=DK)).then_inc(s.x_T, 1)
            dve.wait_ge(s.x_T, NT // 2)
            dve.wait_ge(s.tg_ready, 1)
            dve.wait_ge(s.const, 16)
            link(nc.vector.tensor_copy(identb, ident))
            link(nc.vector.tensor_copy(trib, cf[:, C_UP:C_UP + 128]))
            L = RT[:, 0:256].rearrange("p (t e) -> p t e", t=NT)
            for h in range(NT + 2):
                if h < NT:
                    dve.wait_ge(s.y_ready, h + 1)
                    if h >= 2:
                        dve.wait_ge(s.out_ready, h - 1)
                    pr = prod[:, h % 2, :, :].rearrange("p k (i j b) -> p k i j b", i=HD0, j=HD0)
                    q = QT[:, :, h, :].rearrange("p k (i b) -> p k i b", b=B)
                    p = 3 * (h % 2)
                    for i in range(HD0):
                        if i <= 5:
                            y = bank(p, 2)[:, :, pair(i) * B:(pair(i) + i + 1) * B]
                        else:
                            o = (pair(i) - PA) * B
                            y = bank(p + 2)[:, 0:2 * PB * B].rearrange("p (k n) -> p k n", k=2)[:, :, o:o + (i + 1) * B]
                        y = y.rearrange("p k (j b) -> p k j b", b=B)
                        ins = tt(pr[:, :, i, 0:i + 1, :], y, q[:, :, i, :].unsqueeze(2).to_broadcast([128, DK, i + 1, B]), ALU.mult)
                        if i:
                            ins = tt(pr[:, :, 0:i, i, :], y[:, :, 0:i, :], q[:, :, 0:i, :], ALU.mult)
                    ins.then_inc(s.prod_raw, 1)
                    dve.wait_ge(s.prod_raw, h + 1)
                    tt(prod[:, h % 2, :, 0:512], prod[:, h % 2, :, 0:512], prod[:, h % 2, :, 512:1024], ALU.add).then_inc(s.prod_ready, 1)
                t = h - 1
                if 0 <= t < NT:
                    dve.wait_ge(s.out_ready, t + 1)
                    link(stt(X[:, t, :], bank(6 + t % 2)[:, 0:256], tg[:, 0:1], X[:, t, :], ALU.mult, ALU.add))
                    stats(t, None, s.ln2_stats)
                t = h - 2
                if 0 <= t < NT:
                    dve.wait_ge(s.rstd2, t + 1)
                    normalise(t, XN[:, t, :]).then_inc(s.xn2, 1)
            dve.wait_ge(s.lg_ready, 1)
            dve.wait_ge(s.shared_w, 5 * 16)
            tt(L, bank(4)[:, 0:256].rearrange("p (t e) -> p t e", t=NT), rb[:, :].unsqueeze(1).to_broadcast([128, NT, E]),
               ALU.add).then_inc(s.lg_sb, 1)
            dve.wait_ge(s.lg_sb, 1)

            def ob(ap):
                return ap.unsqueeze(2).to_broadcast([128, 16, 16])

            def mb(ap):
                return ap.unsqueeze(1).to_broadcast([128, 16, 16])

            m16, s16 = small[:, 0:16], small[:, 16:32]
            link(red(m16, L, AX, ALU.max))
            tt(L, L, ob(m16), ALU.subtract).then_inc(s.max_sub, 1)
            dve.wait_ge(s.exp_r, 1)
            link(red(s16, L, AX, ALU.add))
            link(nc.vector.reciprocal(s16, s16))
            link(tt(L, L, ob(s16), ALU.mult))
            top = R2[:, 0:128].rearrange("p (t v) -> p t v", t=NT)
            idx = R2[:, 128:256].bitcast(u32).rearrange("p (t v) -> p t v", t=NT)
            for t in range(NT):
                ins = nc.vector.max(top[:, t, :], L[:, t, :])
            link(ins)
            for t in range(NT):
                ins = nc.vector.max_index(idx[:, t, :], top[:, t, :], L[:, t, :])
            link(ins)
            idf = R2[:, 256:288].rearrange("p (v t) -> p v t", v=2)
            link(nc.vector.tensor_copy(idf.rearrange("p v t -> p t v"), idx[:, :, 0:2]))
            oh = RT[:, 256:768].rearrange("p (v t e) -> p v t e", v=2, t=NT)
            for v in range(2):
                ins = tt(oh[:, v], ob(idf[:, v, :]), mb(cf[:, C_IOTA:C_IOTA + 16]), ALU.is_equal)
            link(ins)
            Mb = RT[:, 768:896].bitcast(bf16).rearrange("p (t e) -> p t e", t=NT)
            tt(Mb, oh[:, 0], oh[:, 1], ALU.add).then_inc(s.onehot, 1)
            link(tt(m16, top[:, :, 0], top[:, :, 1], ALU.add))
            link(ts(m16, m16, W_EPS, None, ALU.add))
            link(nc.vector.reciprocal(m16, m16))
            link(ts(m16, m16, tg[:, 2:3], None, ALU.mult))
            for v in range(2):
                ins = tt(wc[:, v, :], top[:, :, v], m16, ALU.mult)
            link(ins)
            dve.wait_ge(s.counts, 1)
            rank = bank(6)[:, 0:256].rearrange("p (t e) -> p t e", t=NT)
            Rb = R2[:, 320:592].rearrange("p (t e) -> p t e", t=NT + 1)
            link(nc.vector.memset(Rb[:, 0, :], 0.0))
            for t in range(NT):
                link(tt(Rb[:, t + 1, :], bank(6)[:, 256 + t * 16:272 + t * 16], Rb[:, t, :], ALU.add))
            tmp = R2[:, 640:896].rearrange("p (a b) -> p a b", a=16)
            nb_, sb_, en_ = small[:, 0:16], small[:, 16:32], small[:, 48:64]
            link(tt(tmp, ob(Rb[:, NT, :]), mb(cf[:, C_THR:C_THR + 16]), ALU.is_gt))
            link(red(nb_, tmp, AX, ALU.add))
            link(tt(tmp, cf[:, C_TRI:C_TRI + 256].rearrange("p (a b) -> p a b", a=16), mb(nb_), ALU.mult))
            link(red(sb_, tmp, AX, ALU.add))
            link(tt(en_, sb_, nb_, ALU.add))
            link(stt(Rb[:, 0:NT, :], mb(sb_), 128.0, Rb[:, 0:NT, :], ALU.mult, ALU.add))
            tt(Rb[:, 0:NT, :], rank, Rb[:, 0:NT, :], ALU.add).then_inc(s.cnt_read, 1)
            dve.wait_ge(s.cnt_read, 1)
            slf = R2[:, 288:320].rearrange("p (v t) -> p v t", v=2)
            for v in range(2):
                link(tt(tmp, oh[:, v], Rb[:, 0:NT, :], ALU.mult))
                link(red(slf[:, v, :], tmp, AX, ALU.add))
            link(nc.vector.tensor_copy(slot[:, :, :], slf))
            tb = R2[:, 0:NB * E].rearrange("p (n e) -> p n e", e=E)
            ef = R2[:, 768:768 + NB]
            link(tt(tb, en_.unsqueeze(1).to_broadcast([128, NB, E]), cf[:, C_BLK:C_BLK + NB].unsqueeze(2).to_broadcast([128, NB, E]), ALU.is_le))
            link(red(ef, tb, AX, ALU.add))
            link(ts(ef, ef, float(E - 1), None, ALU.min))
            nc.vector.tensor_copy(eid[:, :], ef).then_inc(s.slots, 1)
            dve.wait_ge(s.slots, 1)

            for g in range(5):
                if g < 4:
                    dve.wait_ge(s.sh_silu, g + 1)
                    if g >= 2:
                        dve.wait_ge(s.sh_dn, g - 1)
                    tt(shs[:, g % 2, :], shs[:, g % 2, :], bank(2 * (g % 2) + 1), ALU.mult).then_inc(s.sh_h, 1)
                if g >= 1:
                    dve.wait_ge(s.sh_dn, g)
                    for c in range(2):
                        t = 4 * (g - 1) + 2 * c
                        ins = stt(X[:, t:t + 2, :], bank(4 + c).rearrange("p (t d) -> p t d", t=2), tg[:, 2:3], X[:, t:t + 2, :], ALU.mult, ALU.add)
                    ins.then_inc(s.sh_res, 1)
            dve.wait_ge(s.sh_res, 4)
            dve.wait_ge(s.seg, 16)
            link(nc.vector.tensor_copy(segf[:, :], segi[:, :]))
            for c in range(2):
                d = R2[:, 0:1024].rearrange("p (b k) -> p b k", b=8)
                link(tt(d, cf[:, C_K4:C_K4 + 128].unsqueeze(1).to_broadcast([128, 8, 128]),
                        segf[:, 8 * c:8 * c + 8].unsqueeze(2).to_broadcast([128, 8, 128]), ALU.subtract))
                link(tt(d, d, d, ALU.mult))
                ts(maskb[:, 8 * c:8 * c + 8, :], d, (LOOKBACK / 2.0) ** 2, NEG, ALU.is_gt, ALU.mult).then_inc(s.mask, 1)
                dve.wait_ge(s.mask, c + 1)
            for c in range(4):
                dve.wait_ge(s.kr_ready, c + 1)
                for z, w in enumerate((cosT, sinT)):
                    ins = tt(R2[:, z * 512:(z + 1) * 512].rearrange("p (b s) -> p b s", b=4),
                             bank(2 + z).rearrange("p (b s) -> p b s", b=4), w.unsqueeze(1).to_broadcast([128, 4, 128]), ALU.mult)
                ins.then_inc(s.kr_mul, 1)
                dve.wait_ge(s.kr_mul, c + 1)
                for lo, dst in ((64, K01), (0, K10)):
                    ins = tt(dst[lo:lo + 64, 4 * c:4 * c + 4, :].rearrange("p b s -> p (b s)"), R2[lo:lo + 64, 0:512],
                             R2[lo:lo + 64, 512:1024], ALU.add)
                ins.then_inc(s.kr_sb, 1)
                dve.wait_ge(s.kr_sb, c + 1)

            for n in range(NB + 2):
                if n < NB:
                    dve.wait_ge(s.silu, n + 1)
                    if n >= 2:
                        dve.wait_ge(s.h_xp, n - 1)
                    tt(hh[:, n % 2, :], sg[:, n % 2, :], bank(2 + n % 2)[:, I:2 * I], ALU.mult).then_inc(s.h_ready, 1)
                m = n - 1
                if 0 <= m < NB:
                    dve.wait_ge(s.h_xp, m + 1)
                    if m >= 2:
                        dve.wait_ge(s.y_blk, m - 1)
                    nc.vector.tensor_copy(hT[:, m % 2, :], bank(4 + m % 2)[:, 0:I]).then_inc(s.h_T, 1)
                m = n - 2
                if 0 <= m < NB:
                    dve.wait_ge(s.y_blk, m + 1)
                    if m >= 4:
                        dve.wait_ge(yg_out[m % 4], 16 * (m // 4))
                    nc.vector.tensor_copy(yb[:, m % 4, :], bank(6 + m % 2)[:, 0:D]).then_inc(s.y_sb, 1)
            for t in range(NT + 1):
                if t < NT:
                    dve.wait_ge(gat[t % 4], 32 * (t // 4 + 1))
                    link(stt(X[:, t, :], gb[:, t % 4, 0, :], wc[:, 0, t:t + 1], X[:, t, :], ALU.mult, ALU.add))
                    stt(X[:, t, :], gb[:, t % 4, 1, :], wc[:, 1, t:t + 1], X[:, t, :], ALU.mult, ALU.add).then_inc(s.res2, 1)
                    dve.wait_ge(s.res2, t + 1)
                    stats(t, None, s.ln3_stats)
                if t >= 1:
                    dve.wait_ge(s.rstd3, t)
                    normalise(t - 1, XN[:, t - 1, :]).then_inc(s.xn3, 1)

            nc.vector.memset(w2f[:, NC - 1, :], 0.0).then_inc(s.w_abs, 1)

            def rope(u):
                dve.wait_ge(s.proj, u + 1)
                if u >= 2:
                    dve.wait_ge(s.q_r, 2 * u - 2)
                for z, (dst, w) in enumerate(((ra, cosT), (rbm, sinT))):
                    ins = tt(dst[:, u % 2, :].rearrange("p (b s) -> p b s", b=4), bank(3 + z).rearrange("p (b s) -> p b s", b=4),
                             w.unsqueeze(1).to_broadcast([128, 4, 128]), ALU.mult)
                ins.then_inc(s.rope_mul, 1)

            rope(0)
            for u in range(33):
                if u < 32:
                    dve.wait_ge(s.s_ready, u + 1)
                    link(red(mx[:, u % 2, :], bank(0, 2).rearrange("p a (i k) -> p (a i) k", i=4), AX, ALU.max))
                    if u >= 2:
                        dve.wait_ge(s.exp_done, u - 1)
                    ts(nm[:, u % 2, :], mx[:, u % 2, :], -SCALE, None, ALU.mult).then_inc(s.max_ready, 1)
                if u >= 1:
                    dve.wait_ge(s.pv_ready, u)
                    dve.wait_ge(s.exp_done, u)
                    if u >= 3:
                        dve.wait_ge(s.o_xp, u - 2)
                    link(nc.vector.reciprocal(ri[:, (u - 1) % 2, :], rs[:, (u - 1) % 2, :]))
                    tt(O[:, (u - 1) % 2].rearrange("p b h c -> p h b c"), bank(7).rearrange("p (h b c) -> p h b c", h=2, b=4),
                       ri[:, (u - 1) % 2, :].rearrange("p (h b) -> p h b", h=2).unsqueeze(3).to_broadcast([128, 2, 4, KVC]),
                       ALU.mult).then_inc(s.o_ready, 1)
                if u + 1 < 32:
                    rope(u + 1)
                if u < 32:
                    dve.wait_ge(s.p_xp, u + 1)
                    if u >= 2:
                        dve.wait_ge(s.pv_ready, u - 1)
                    nc.vector.tensor_copy(PT[:, u % 2, 4:8, :], bank(6).rearrange("p (i q) -> p i q", i=4)).then_inc(s.pt_d, 1)
                if u >= 1 and (u - 1) % 8 == 7:
                    g = (u - 1) // 8
                    if g == 0:
                        dve.wait_ge(s.xin, 16)
                    for c in range(2):
                        dve.wait_ge(s.op_ready, 2 * g + c + 1)
                        b = 4 * g + 2 * c
                        stt(X[:, b:b + 2, :], bank(3 + c).rearrange("p (b d) -> p b d", b=2), tg[:, 1:2], X[:, b:b + 2, :],
                            ALU.mult, ALU.add).then_inc(s.res3, 1)

            dve.wait_ge(s.res3, 8)
            dve.wait_ge(s.scale_r, 1)
            sc = small[:, 40:43]
            link(ts(sc, bank(7)[:, 0:3], 1.0 / (HID * D), None, ALU.mult))
            link(ts(small[:, 43:46], sc, 0.5, None, ALU.mult))
            link(ts(small[:, 46:49], sc, -0.5, None, ALU.mult))
            link(tt(small[:, 49:50], sc[:, 2:3], tg[:, 3:4], ALU.mult))
            for i, (w, q, n) in enumerate(((w1f, w1q, DK * HID), (w3f, w3q, DK * HID), (w2f, w2q, NC * D))):
                w, q = w.rearrange("p k n -> p (k n)"), q.rearrange("p k n -> p (k n)")
                low = WE[:, 1024:1024 + n]
                link(ts(low, w, small[:, 46 + i:47 + i], None, ALU.is_lt))
                stt(q, w, small[:, 43 + i:44 + i], low, ALU.is_gt, ALU.subtract).then_inc(s.ternary, 1)
                dve.wait_ge(s.ternary, i + 1)

            def rows(g):
                for b in range(4 * g, 4 * g + 4):
                    stats(b, None, s.d_stats if b == 4 * g + 3 else None)
                dve.wait_ge(s.rstd4, g + 1)
                if g >= 1:
                    dve.wait_ge(s.xn4_xp, 2 * g)
                for b in range(4):
                    normalise(4 * g + b, x3n[:, b, :]).then_inc(s.xn4, 1)

            rows(0)
            for g in range(4):
                for t in range(2):
                    h = slice(t * 256, (t + 1) * 256)
                    dve.wait_ge(s.split_hi, 2 * g + t + 1)
                    tt(xr[:, :, h], bank(t).rearrange("p (k n) -> p k n", k=DK), xp[0][:, :, h], ALU.subtract).then_inc(s.split_r, 1)
                for t in range(2):
                    h = slice(t * 256, (t + 1) * 256)
                    dve.wait_ge(s.split_mid, 2 * g + t + 1)
                    tt(xp[2][:, :, h], xr[:, :, h], xp[1][:, :, h], ALU.subtract).then_inc(s.split_lo, 1)
                for c in range(NC + 1):
                    n = NC * g + c
                    if c < NC:
                        m = min(128, HID - c * 128)
                        dve.wait_ge(s.up_silu, n + 1)
                        if n >= 2:
                            dve.wait_ge(s.g_r, n - 1)
                        stt(gg[0:m, n % 2, :], bank(3 + 2 * (n % 2))[0:m, :], sc[0:m, 1:2], sl[0:m, n % 2, :], ALU.mult, ALU.mult).then_inc(s.g_ready, 1)
                        dve.wait_ge(s.g_hi, n + 1)
                        if c >= 2:
                            dve.wait_ge(s.g_lo, n - 1)
                        tt(gr[0:m, c % 2, :], gg[0:m, n % 2, :], ghi[0:m, c, :], ALU.subtract).then_inc(s.g_r, 1)
                    if c >= 1:
                        m = min(128, HID - (c - 1) * 128)
                        dve.wait_ge(s.g_mid, n)
                        tt(glo[0:m, c - 1, :], gr[0:m, (c - 1) % 2, :], gmid[0:m, c - 1, :], ALU.subtract).then_inc(s.g_lo, 1)
                if g < 3:
                    rows(g + 1)
                for b in range(4):
                    dve.wait_ge(s.dn_ready, 4 * g + b + 1)
                    stt(X[:, 4 * g + b, :], bank(6 + b % 2)[:, 0:D], small[:, 49:50], X[:, 4 * g + b, :], ALU.mult, ALU.add).then_inc(s.yout, 1)


_OUT = (B, S, D)


def _constants():
    import numpy as np
    p = np.arange(128)
    cf = np.zeros((128, NCF), np.float32)
    cf[:, C_ID:C_ID + 128] = np.eye(128)
    half = R // 2
    inv = (1.0 / np.float32(10000.0) ** (np.arange(half, dtype=np.float32) / np.float32(half))).astype(np.float32)
    ang = np.arange(128, dtype=np.float32)[None, :] * inv[p % half][:, None]
    cf[:, C_COS:C_COS + 128] = np.cos(ang)
    cf[:, C_SIN:C_SIN + 128] = np.sin(ang) * np.where(p % R < half, -1.0, 1.0)[:, None]
    cf[:, C_K4:C_K4 + 128] = p[None, :] + LOOKBACK // 2
    cf[:, C_TRI:C_TRI + 256] = np.tril(np.ones((16, 16)), -1).reshape(1, 256)
    cf[:, C_THR:C_THR + 16] = 128 * np.arange(16)
    cf[:, C_IOTA:C_IOTA + 16] = np.arange(16)
    cf[:, C_BLK:C_BLK + NB] = np.arange(NB)
    cf[:, C_UP:C_UP + 128] = np.triu(np.ones((128, 128)), 1)
    return cf


def kernel(x, ctx_2048, itok_BxS_0_1023, g_xattn, g_ffn, L0_xattn_ssm_kernel, L0_xattn_D, L0_ffn_Wr, L0_ffn_bias,
           L0_ffn_Wg, L0_ffn_Wu, L0_ffn_Wd, L0_ffn_sWg, L0_ffn_sWu, L0_ffn_sWd, L1_xattn_W_kvc, L1_xattn_W_dq,
           L1_xattn_W_uq, L1_xattn_W_qr, L1_xattn_W_uk, L1_xattn_W_kr, L1_xattn_W_uv, L1_xattn_W_o,
           L1_ffn_w1, L1_ffn_w3, L1_ffn_w2):
    import numpy as np
    import concourse.bacc as bacc
    from concourse import mybir
    from concourse.bass_utils import run_bass_kernel_spmd

    def t(a):
        return np.ascontiguousarray(np.asarray(a).T)

    def back(a, axis):
        a = np.asarray(a)
        halves = a.reshape(a.shape[:axis] + (DK, 128) + a.shape[axis + 1:])
        return np.ascontiguousarray(np.flip(halves, axis + 1)).reshape(a.shape)

    cf = _constants()
    given = {
        "x": x, "ctxd": back(ctx_2048, 2), "segT": t(itok_BxS_0_1023), "gates": np.concatenate([np.asarray(g_xattn), np.asarray(g_ffn)]),
        "ssm": L0_xattn_ssm_kernel, "ssmD": L0_xattn_D, "WrT": t(L0_ffn_Wr), "rbias": L0_ffn_bias,
        "Wg": L0_ffn_Wg, "Wu": L0_ffn_Wu, "Wd": L0_ffn_Wd, "sWg": L0_ffn_sWg, "sWu": L0_ffn_sWu, "sWd": L0_ffn_sWd,
        "Wkvc": back(L1_xattn_W_kvc, 0), "Wdq": L1_xattn_W_dq, "WuqT": t(L1_xattn_W_uq), "Wqr": L1_xattn_W_qr,
        "WukT": t(L1_xattn_W_uk), "Wkr": L1_xattn_W_kr, "WuvT": t(L1_xattn_W_uv), "Wo": L1_xattn_W_o,
        "w1T": t(L1_ffn_w1), "w3T": t(L1_ffn_w3), "w2T": t(L1_ffn_w2), "constf": cf,
    }
    nc = bacc.Bacc("TRN2", target_bir_lowering=False, num_devices=1)
    arrays, args = {}, []
    for name, a in given.items():
        a = np.ascontiguousarray(a)
        arrays[f"in_{name}"] = a
        args.append(nc.dram_tensor(f"in_{name}", a.shape, mybir.dt.from_np(a.dtype), kind="ExternalInput").ap())
    args.append(nc.dram_tensor("out_0", _OUT, mybir.dt.float32, kind="ExternalOutput").ap())
    flamingo_kernel(nc, *args)
    r = run_bass_kernel_spmd(nc, [arrays], core_ids=[0])
    return r.results[0]["out_0"]
```

```python
import concourse.bass as bass
from concourse import mybir
from contextlib import ExitStack

B, S, D = 16, 128, 256
NT = 16
DK = D // 128
E, I = 16, 128
NH0, HD0 = 16, 8
NB = 47
H, HD, KVC, QC, R = 16, 128, 64, 96, 64
HID = 682
NC = (HID + 127) // 128
NPAIR = HD0 * (HD0 + 1) // 2
PA = 21
PB = NPAIR - PA
LN_EPS = 1e-5
W_EPS = 1e-9
NEG = -1e30
LOOKBACK = 8
SCALE = 1.0 / (HD + R) ** 0.5

C_ID, C_COS, C_SIN, C_K4 = 0, 128, 256, 384
C_TRI, C_THR, C_IOTA, C_BLK, C_UP = 512, 768, 784, 800, 800 + NB
C_J = C_UP + 128
C_B = C_J + HD0
NCF = C_B + B


def flamingo_kernel(nc, x, ctxd, segT, gates, ssm, ssmD, WrT, rbias, Wg, Wu, Wd, sWg, sWu, sWd,
                    Wkvc, Wdq, WuqT, Wqr, WukT, Wkr, WuvT, Wo, w1T, w3T, w2T, constf, out):
    f32, bf16, i32, u32 = mybir.dt.float32, mybir.dt.bfloat16, mybir.dt.int32, mybir.dt.uint32
    ALU = mybir.AluOpType
    ACT = mybir.ActivationFunctionType
    AX = mybir.AxisListType.X

    def pair(i):
        return i * (i + 1) // 2

    ctx = ExitStack()
    with ctx:
        def sb(name, shape, dt=f32):
            return ctx.enter_context(nc.sbuf_tensor(name, shape, dt))

        def sem(name):
            return ctx.enter_context(nc.semaphore(name))

        cf = sb("cf", [128, NCF])
        cb = sb("cb", [128, 256], bf16)
        ident, cosT, sinT = cf[:, C_ID:C_ID + 128], cf[:, C_COS:C_COS + 128], cf[:, C_SIN:C_SIN + 128]
        identb, trib = cb[:, 0:128], cb[:, 128:256]
        onesb = sb("onesb", [128, 128], bf16)
        onesf = sb("onesf", [128, 128])
        X = sb("X", [128, NT, D])
        XN = sb("XN", [128, NT, D])
        CT = sb("CT", [128, DK, NT, 128])
        QT = sb("QT", [128, DK, NT, 128])
        WE = sb("WE", [128, (DK * E * 2 * I) + E * D])
        WGU = WE[:, 0:DK * E * 2 * I].rearrange("p (k e c) -> p k e c", k=DK, e=E)
        WD = WE[:, DK * E * 2 * I:].rearrange("p (e d) -> p e d", e=E)
        sWgu = sb("sWgu", [128, DK, 2, I])
        sWdn = sb("sWdn", [128, D])
        Wr = sb("Wr", [128, DK, E])
        rb = sb("rb", [128, E])
        gt = sb("gt", [128, 4])
        tg = sb("tg", [128, 4])
        WN = sb("WN", [QC, H // 2, 2, KVC])
        WRA = WE[0:QC, 9216:10240].rearrange("p (m a c) -> p m a c", m=H // 2, a=2)
        WRB = WE[0:QC, 10240:11264].rearrange("p (m a c) -> p m a c", m=H // 2, a=2)
        R2 = sb("R2", [128, 1536])
        CW = sb("CW", [128, H // 2, D])
        Wk2 = sb("Wk2", [128, DK, 2, KVC])
        Wkr2 = sb("Wkr2", [KVC, 2, 2, R])
        Wdqs = sb("Wdqs", [128, DK, QC])
        st = sb("st", [128, NT, 6])
        mv = sb("mv", [128, NT, 2])
        rstd = sb("rstd", [128, NT])
        mhalf = sb("mhalf", [128, NT])
        zero = sb("zero", [128, D])
        zk = sb("zk", [NH0, 384])
        dsb = sb("dsb", [NH0, 1])
        small = sb("small", [128, 64])
        wc = sb("wc", [128, 2, NT])
        slot = sb("slot", [128, 2, NT], i32)
        slotB = sb("slotB", [128, 2, B], i32)
        wcB = sb("wcB", [128, 2, B])
        eid = sb("eid", [128, NB], i32)
        segi = sb("segi", [128, B], i32)
        segf = sb("segf", [128, B])

        AR = sb("AR", [128, 15872])

        def ar(lo, n):
            return AR[:, lo:lo + n]

        T = ar(0, 4096).rearrange("p (h l) -> p h l", h=NH0)
        CS = ar(4096, 4096).rearrange("p (t d) -> p t d", t=NT)
        kv = ar(8192, 2 * DK * NPAIR * B).rearrange("p (u k n) -> p u k n", u=2, k=DK)
        o = 8192 + 2 * DK * NPAIR * B
        prod = ar(o, 2 * DK * 64 * B).rearrange("p (u k n) -> p u k n", u=2, k=DK)
        K01 = ar(0, 2048).rearrange("p (b s) -> p b s", b=B)
        K10 = ar(2048, 2048).rearrange("p (b s) -> p b s", b=B)
        KVr = ar(4096, 1024).rearrange("p (b c) -> p b c", b=B)
        maskb = ar(5120, 1024).bitcast(bf16).rearrange("p (b k) -> p b k", b=B)
        RT = ar(6144, 2048)
        SG = 8192
        uqT = ar(SG, H * QC).rearrange("p (h c) -> p h c", h=H)
        ukT = ar(SG + 1536, H * KVC).rearrange("p (h c) -> p h c", h=H)
        uvT = ar(SG + 2560, H * KVC).rearrange("p (h c) -> p h c", h=H)
        wo = ar(SG + 3584, H * D).rearrange("p (h d) -> p h d", h=H)
        xg = ar(SG, 4 * D).rearrange("p (u d) -> p u d", u=4)
        xgT = ar(SG + 1024, 2 * D).rearrange("p (u k t) -> p u k t", u=2, k=DK)
        sg = ar(SG + 1536, 2 * I).rearrange("p (u d) -> p u d", u=2)
        hh = ar(SG + 1792, 2 * I).rearrange("p (u d) -> p u d", u=2)
        hT = ar(SG + 2048, 2 * I).rearrange("p (u d) -> p u d", u=2)
        yb = ar(SG + 2304, 4 * D).rearrange("p (u d) -> p u d", u=4)
        gb = ar(SG + 3328, 8 * D).rearrange("p (u s d) -> p u s d", u=4, s=2)
        SP4 = R2[:, 1024:1536].rearrange("p (v n) -> p v n", v=4)
        shs = RT[:, 1024:2048].rearrange("p (u n) -> p u n", u=2)
        Q = WE[:, 0:2048].rearrange("p (u h n) -> p u h n", u=2, h=2)
        P = WE[:, 2048:4096].rearrange("p (u i k) -> p u i k", u=2, i=8)
        PT = WE[:, 4096:6144].rearrange("p (u i k) -> p u i k", u=2, i=8)
        ra = WE[:, 6144:7168].rearrange("p (u n) -> p u n", u=2)
        rbm = WE[:, 7168:8192].rearrange("p (u n) -> p u n", u=2)
        O = WE[:, 8192:9216].rearrange("p (u b h c) -> p u b h c", u=2, b=4, h=2)
        CTf = CT[:, :, :, :].rearrange("p k t n -> p (k t n)")
        QTf = QT[:, :, :, :].rearrange("p k t n -> p (k t n)")
        XNf = XN[:, :, :].rearrange("p t d -> p (t d)")
        OT = [v.rearrange("p (m b q) -> p m b q", m=H // 2, b=4) for v in (CTf, QTf)]
        xb = XNf[:, 0:1024].rearrange("p (b d) -> p b d", b=4)
        xbT = XNf[:, 1024:2048].rearrange("p (k n) -> p k n", k=DK)
        qc = [XNf[0:QC, 2048 + 512 * i:2560 + 512 * i] for i in range(2)]
        w1f = ar(SG, DK * HID).rearrange("p (k n) -> p k n", k=DK)
        w3f = ar(SG + DK * HID, DK * HID).rearrange("p (k n) -> p k n", k=DK)
        w2f = ar(SG + 2 * DK * HID, NC * D).rearrange("p (c d) -> p c d", c=NC)
        o = SG + 2 * DK * HID + NC * D
        w1q = ar(o, HID).bitcast(bf16).rearrange("p (k n) -> p k n", k=DK)
        w3q = ar(o + HID, HID).bitcast(bf16).rearrange("p (k n) -> p k n", k=DK)
        w2q = ar(o + 2 * HID, NC * D // 2).bitcast(bf16).rearrange("p (c d) -> p c d", c=NC)
        f16 = mybir.dt.float16
        gs = [[WE[:, 4608 * i + 1536 * j:4608 * i + 1536 * (j + 1)].bitcast(bf16).rearrange("p (c n) -> p c n", c=NC)
               for j in range(3)] for i in range(2)]
        sl = WE[:, 9216:10240].rearrange("p (u n) -> p u n", u=2)
        gg = WE[:, 10240:11264].rearrange("p (u n) -> p u n", u=2)
        gr = WE[:, 11264:12288].rearrange("p (u n) -> p u n", u=2)
        x3n = XNf[:, 3072:4096].rearrange("p (b d) -> p b d", b=4)
        xp = [[XNf[:, 1024 * i + 512 * j:1024 * i + 512 * (j + 1)].bitcast(f16).rearrange("p (k n) -> p k n", k=DK)
               for j in range(2)] for i in range(2)]
        wtmp = XNf[:, 0:1536]
        rs = RT[:, 0:16].rearrange("p (u i) -> p u i", u=2)
        nm = RT[:, 16:32].rearrange("p (u i) -> p u i", u=2)
        mx = RT[:, 32:48].rearrange("p (u i) -> p u i", u=2)
        ri = RT[:, 48:64].rearrange("p (u i) -> p u i", u=2)

        PSt = ctx.enter_context(nc.psum_tensor("PS", [128, 8, 512], f32))

        def bank(k, n=1):
            return PSt[:, k, :] if n == 1 else PSt[:, k:k + n, :]

        XG = nc.dram_tensor("XG", [NB * 128, D], f32, kind="Internal").ap()
        YG = nc.dram_tensor("YG", [NB * 128, D], f32, kind="Internal").ap()
        Z = nc.dram_tensor("Z", [NH0, 384], f32, kind="Internal").ap()
        Xm = nc.dram_tensor("Xm", [B, S, D], f32, kind="Internal").ap()

        class Signals:
            pass

        s = Signals()
        s.ctx0 = sem("ctx0")
        s.ctx1 = sem("ctx1")
        s.ctx2 = sem("ctx2")
        s.ctx3 = sem("ctx3")
        s.x0 = sem("x0")
        s.x1 = sem("x1")
        s.x2 = sem("x2")
        s.x3 = sem("x3")
        s.yg0 = sem("yg0")
        s.yg1 = sem("yg1")
        s.yg2 = sem("yg2")
        s.yg3 = sem("yg3")
        s.const = sem("const")
        s.shared_w = sem("shared_w")
        s.moe_w = sem("moe_w")
        s.memsets = sem("memsets")
        s.zinit = sem("zinit")
        s.ab_w = sem("ab_w")
        s.seg = sem("seg")
        s.out_ready = sem("out_ready")
        s.sh_res = sem("sh_res")
        s.xm_out = sem("xm_out")
        s.xin = sem("xin")
        s.scat = sem("scat")
        s.cw_ready = sem("cw_ready")
        s.ab_ready = sem("ab_ready")
        s.xg_xp = sem("xg_xp")
        s.y_blk = sem("y_blk")
        s.qr_w = sem("qr_w")
        s.res2 = sem("res2")
        s.w_ffn = sem("w_ffn")
        s.w_abs = sem("w_abs")
        s.yout = sem("yout")
        s.out_dma = sem("out_dma")
        s.small = sem("small")
        s.zk_set = sem("zk_set")
        s.ssm = sem("ssm")
        s.zk_d = sem("zk_d")
        s.zk_out = sem("zk_out")
        s.tg_ready = sem("tg_ready")
        s.ctx_xp = sem("ctx_xp")
        s.ctx_T = sem("ctx_T")
        s.xn2_xp = sem("xn2_xp")
        s.xn2_T = sem("xn2_T")
        s.max_sub = sem("max_sub")
        s.exp_r = sem("exp_r")
        s.sh_up = sem("sh_up")
        s.sh_h = sem("sh_h")
        s.sh_silu = sem("sh_silu")
        s.ab_sb = sem("ab_sb")
        s.cw_sb = sem("cw_sb")
        s.kc_ready = sem("kc_ready")
        s.kc_sb = sem("kc_sb")
        s.kt_ready = sem("kt_ready")
        s.kt_sb = sem("kt_sb")
        s.gu_ready = sem("gu_ready")
        s.xg_T = sem("xg_T")
        s.h_ready = sem("h_ready")
        s.silu = sem("silu")
        s.y_sb = sem("y_sb")
        s.xn3_xp = sem("xn3_xp")
        s.xn3_T = sem("xn3_T")
        s.qc_ready = sem("qc_ready")
        s.qc_sb = sem("qc_sb")
        s.proj_n = sem("proj_n")
        s.s_ready = sem("s_ready")
        s.q_n = sem("q_n")
        s.max_ready = sem("max_ready")
        s.p_xp = sem("p_xp")
        s.o_ready = sem("o_ready")
        s.exp_done = sem("exp_done")
        s.o_xp = sem("o_xp")
        s.op_ready = sem("op_ready")
        s.ot_ready = sem("ot_ready")
        s.pv_ready = sem("pv_ready")
        s.pt_a = sem("pt_a")
        s.abs_sum = sem("abs_sum")
        s.xn4_xp = sem("xn4_xp")
        s.up_ready = sem("up_ready")
        s.split_hi = sem("split_hi")
        s.g_ready = sem("g_ready")
        s.up_silu = sem("up_silu")
        s.dn_ready = sem("dn_ready")
        s.g_hi = sem("g_hi")
        s.xn1 = sem("xn1")
        s.x_T = sem("x_T")
        s.x_xp = sem("x_xp")
        s.kv_ready = sem("kv_ready")
        s.prod_raw = sem("prod_raw")
        s.y_ready = sem("y_ready")
        s.prod_ready = sem("prod_ready")
        s.ln2_stats = sem("ln2_stats")
        s.xn2 = sem("xn2")
        s.lg_ready = sem("lg_ready")
        s.lg_sb = sem("lg_sb")
        s.sh_dn = sem("sh_dn")
        s.onehot = sem("onehot")
        s.counts = sem("counts")
        s.cnt_read = sem("cnt_read")
        s.spread = sem("spread")
        s.spread_ps = sem("spread_ps")
        s.slotsB = sem("slotsB")
        s.kr_mul = sem("kr_mul")
        s.kr_ready = sem("kr_ready")
        s.slots = sem("slots")
        s.h_T = sem("h_T")
        s.h_xp = sem("h_xp")
        s.xn3 = sem("xn3")
        s.rope_mul = sem("rope_mul")
        s.res3 = sem("res3")
        s.proj = sem("proj")
        s.q_r = sem("q_r")
        s.pt_d = sem("pt_d")
        s.mask = sem("mask")
        s.kr_sb = sem("kr_sb")
        s.scale_r = sem("scale_r")
        s.scale_sb = sem("scale_sb")
        s.xn4 = sem("xn4")
        s.split_lo = sem("split_lo")
        s.g_lo = sem("g_lo")
        s.ternary = sem("ternary")
        s.pool = sem("pool")
        s.ln1_stats = sem("ln1_stats")
        s.rstd1 = sem("rstd1")
        s.rstd2 = sem("rstd2")
        s.ln3_stats = sem("ln3_stats")
        s.rstd3 = sem("rstd3")
        s.d_stats = sem("d_stats")
        s.rstd4 = sem("rstd4")
        s.g_r = sem("g_r")
        s.g_mid = sem("g_mid")
        s.dve = sem("dve")
        xg_in = [sem(f"xg_in{i}") for i in range(4)]
        toep = [sem(f"toep{i}") for i in range(4)]
        gat = [sem(f"gat{i}") for i in range(4)]
        ctx_in = [s.ctx0, s.ctx1, s.ctx2, s.ctx3]
        x_in = [s.x0, s.x1, s.x2, s.x3]
        yg_out = [s.yg0, s.yg1, s.yg2, s.yg3]
        block = ctx.enter_context(nc.Block())

        @block.sync
        def _(sp):
            sp.dma_start(cf[:, :], constf).then_inc(s.const, 16)
            for c in range(4):
                for j in range(HD0):
                    src = x.rearrange("b (h j) d -> j b h d", j=HD0)[j]
                    sp.dma_start(X[j * B:(j + 1) * B, 4 * c:4 * c + 4, :], src[:, 4 * c:4 * c + 4, :]).then_inc(x_in[c], 16)
            for dst, src in ((rb[:, :], rbias.unsqueeze(0).to_broadcast([128, E])),
                             (Wr[:, :, :], WrT.rearrange("(k p) e -> p k e", p=128)),
                             (sWgu[:, :, 0, :], sWg.rearrange("(k p) c -> p k c", p=128)),
                             (sWgu[:, :, 1, :], sWu.rearrange("(k p) c -> p k c", p=128)),
                             (sWdn[:, :], sWd)):
                sp.dma_start(dst, src).then_inc(s.shared_w, 16)
            for k in range(DK):
                for c, w in ((0, Wg), (1, Wu)):
                    sp.dma_start(WGU[:, k, :, c * I:(c + 1) * I],
                                 w.rearrange("e (k p) c -> k p e c", p=128)[k]).then_inc(s.moe_w, 16)
            sp.dma_start(WD, Wd.rearrange("e p d -> p e d")).then_inc(s.moe_w, 16)
            sp.wait_ge(s.memsets, 1)
            XGz = XG.rearrange("(n p) d -> p n d", p=128)
            for c in range(0, NB, 12):
                n = min(12, NB - c)
                sp.dma_start(XGz[:, c:c + n, :], zero[:, :].unsqueeze(1).to_broadcast([128, n, D])).then_inc(s.zinit, 16)
            for a in range(2):
                sp.dma_start(Wk2[:, :, a, :], Wkvc.rearrange("(k p) c -> p k c", p=128)).then_inc(s.ab_w, 16)
                sp.dma_start(Wkr2[:, 0, a, :], Wkr).then_inc(s.ab_w, 16)
                for z in range(2):
                    sp.dma_start(Wkr2[:, 1, a, z * 32:z * 32 + 32], Wkr[:, (1 - z) * 32:(1 - z) * 32 + 32]).then_inc(s.ab_w, 16)
            sp.dma_start(Wdqs[:, :, :], Wdq.rearrange("(k p) c -> p k c", p=128)).then_inc(s.ab_w, 16)
            sp.dma_start(segi[:, :], segT).then_inc(s.seg, 16)
            sp.wait_ge(s.out_ready, NT)
            for dst, src in ((uqT, WuqT), (ukT, WukT), (uvT, WuvT), (wo, Wo)):
                sp.dma_start(dst, src.rearrange("(h p) c -> p h c", p=128)).then_inc(s.ab_w, 16)
            for c in range(4):
                sp.wait_ge(s.sh_res, c + 1)
                for j in range(HD0):
                    dst = Xm.rearrange("b (h j) d -> j b h d", j=HD0)[j]
                    sp.dma_start(dst[:, 4 * c:4 * c + 4, :], X[j * B:(j + 1) * B, 4 * c:4 * c + 4, :]).then_inc(s.xm_out, 16)
            sp.wait_ge(s.xm_out, 4 * HD0 * 16)
            sp.dma_start(X[:, :, :], Xm.rearrange("b s d -> s b d")).then_inc(s.xin, 16)
            sp.wait_ge(s.scat, 2 * NT * 16)
            sp.wait_ge(s.cw_ready, 4)
            sp.wait_ge(s.ab_ready, 2)
            for n in range(NB):
                if n >= 4:
                    sp.wait_ge(s.xg_xp, n - 3)
                sp.dma_start(xg[:, n % 4, :], XG[n * 128:(n + 1) * 128, :]).then_inc(xg_in[n % 4], 16)
            sp.wait_ge(s.y_blk, NB)
            for a in range(2):
                src = Wqr.rearrange("q (m a c) -> q m a c", a=2, c=R)[:, :, 1 - a, :]
                sp.dma_start(WRA[:, :, a, :], src).then_inc(s.qr_w, 16)
                for z in range(2):
                    sp.dma_start(WRB[:, :, a, z * 32:z * 32 + 32], src[:, :, (1 - z) * 32:(1 - z) * 32 + 32]).then_inc(s.qr_w, 16)
            sp.wait_ge(s.res2, B)
            sp.dma_start(w1f, w1T.rearrange("(k p) n -> p k n", p=128)).then_inc(s.w_ffn, 16)
            sp.dma_start(w3f, w3T.rearrange("(k p) n -> p k n", p=128)).then_inc(s.w_ffn, 16)
            sp.wait_ge(s.w_abs, 1)
            sp.dma_start(w2f[:, 0:NC - 1, :], w2T[0:(NC - 1) * 128, :].rearrange("(c p) d -> p c d", p=128)).then_inc(s.w_ffn, 16)
            sp.dma_start(w2f[0:HID - (NC - 1) * 128, NC - 1, :], w2T[(NC - 1) * 128:HID, :]).then_inc(s.w_ffn, 16)
            for b in range(B):
                sp.wait_ge(s.yout, b + 1)
                sp.dma_start(out[b], X[:, b, :]).then_inc(s.out_dma, 16)
            sp.wait_ge(s.out_dma, B * 16)

        @block.scalar
        def _(act):
            act.dma_start(gt[:, :], gates.unsqueeze(0).to_broadcast([128, 4])).then_inc(s.small, 16)
            act.wait_ge(s.zk_set, 1)
            act.dma_start(zk[:, 127:383], ssm).then_inc(s.ssm, 16)
            act.dma_start(dsb[:, :], ssmD.unsqueeze(1)).then_inc(s.ssm, 16)
            for c in range(4):
                for j in range(HD0):
                    src = ctxd.rearrange("b (h j) d -> j b h d", j=HD0)[j]
                    act.dma_start(CS[j * B:(j + 1) * B, 4 * c:4 * c + 4, :], src[:, 4 * c:4 * c + 4, :]).then_inc(ctx_in[c], 16)
            act.wait_ge(s.zk_d, 1)
            act.dma_start(Z, zk[:, :]).then_inc(s.zk_out, 16)
            act.wait_ge(s.zk_out, 16)
            for h in range(0, NH0, 4):
                src = bass.AP(Z.tensor, 384 * h, [[1, 128], [384, 4], [1, 256]])
                act.dma_start(T[:, h:h + 4, :], src).then_inc(toep[h // 4], 16)
            act.wait_ge(s.small, 16)
            nc.scalar.activation(tg[:, :], gt[:, :], ACT.Tanh).then_inc(s.tg_ready, 1)
            for u in range(NT // 2):
                act.wait_ge(s.ctx_xp, u + 1)
                nc.scalar.activation(CT[:, :, 2 * u:2 * u + 2, :],
                                     bank(2 * (u % 2)).rearrange("p (t k n) -> p k t n", t=2, k=DK), ACT.Copy).then_inc(s.ctx_T, 1)
            for u in range(NT // 2):
                act.wait_ge(s.xn2_xp, u + 1)
                nc.scalar.activation(QT[:, :, 2 * u:2 * u + 2, :],
                                     bank(u % 4).rearrange("p (t k n) -> p k t n", t=2, k=DK), ACT.Copy).then_inc(s.xn2_T, 1)
            act.wait_ge(s.max_sub, 1)
            L = RT[:, 0:256]
            nc.scalar.activation(L, L, ACT.Exp).then_inc(s.exp_r, 1)
            for g in range(4):
                act.wait_ge(s.sh_up, g + 1)
                if g >= 2:
                    act.wait_ge(s.sh_h, g - 1)
                nc.scalar.activation(shs[:, g % 2, :], bank(2 * (g % 2)), ACT.Silu).then_inc(s.sh_silu, 1)
            for c in range(2):
                act.wait_ge(s.ab_ready, c + 1)
                nc.scalar.activation(WN[:, 4 * c:4 * c + 4, :, :], bank(4 + c)[0:QC, :].rearrange("p (m a c) -> p m a c", a=2, c=KVC),
                                     ACT.Copy).then_inc(s.ab_sb, 1)
            for c in range(4):
                act.wait_ge(s.cw_ready, c + 1)
                nc.scalar.activation(CW[:, 2 * c:2 * c + 2, :], bank(6 + c % 2).rearrange("p (m d) -> p m d", m=2),
                                     ACT.Copy).then_inc(s.cw_sb, 1)
            for c in range(4):
                act.wait_ge(s.kc_ready, c + 1)
                for lo, dst in ((0, K01), (64, K10)):
                    for j4 in range(4):
                        h = 4 * c + j4
                        ins = nc.scalar.activation(
                            dst[lo:lo + 64, :, h * HD0:(h + 1) * HD0].rearrange("p b j -> p j b"),
                            bank(c % 2)[lo:lo + 64, j4 * 128:(j4 + 1) * 128].rearrange("p (j b) -> p j b", j=HD0), ACT.Copy)
                ins.then_inc(s.kc_sb, 1)
            for c in range(2):
                act.wait_ge(s.kt_ready, c + 1)
                nc.scalar.activation(KVr[:, 8 * c:8 * c + 8, :], bank(6 + c).rearrange("p (b c) -> p b c", b=8), ACT.Copy).then_inc(s.kt_sb, 1)
            for n in range(NB + 4):
                if n < NB:
                    act.wait_ge(s.xg_xp, n + 1)
                    if n >= 2:
                        act.wait_ge(s.gu_ready, n - 1)
                    nc.scalar.activation(xgT[:, n % 2, :, :], bank(n % 2)[:, 0:256].rearrange("p (k t) -> p k t", k=DK),
                                         ACT.Copy).then_inc(s.xg_T, 1)
                m = n - 1
                if 0 <= m < NB:
                    act.wait_ge(s.gu_ready, m + 1)
                    if m >= 2:
                        act.wait_ge(s.h_ready, m - 1)
                    nc.scalar.activation(sg[:, m % 2, :], bank(2 + m % 2)[:, 0:I], ACT.Silu).then_inc(s.silu, 1)
                m = n - 4
                if m >= 0:
                    act.wait_ge(s.y_sb, m + 1)
                    act.dma_start(YG[m * 128:(m + 1) * 128, :], yb[:, m % 4, :]).then_inc(yg_out[m % 4], 16)
            def latent(g, c):
                if c < 2:
                    act.wait_ge(s.xn3_xp, 2 * g + c + 1)
                    nc.scalar.activation(xbT[:, :, c * 256:(c + 1) * 256], bank(4).rearrange("p (k n) -> p k n", k=DK),
                                         ACT.Copy).then_inc(s.xn3_T, 1)
                else:
                    act.wait_ge(s.qc_ready, g + 1)
                    nc.scalar.activation(qc[g % 2], bank(4)[0:QC, :], ACT.Copy).then_inc(s.qc_sb, 1)

            def q_nope(u):
                act.wait_ge(s.proj_n, u + 1)
                if u >= 2:
                    act.wait_ge(s.s_ready, u - 1)
                nc.scalar.activation(Q[0:64, u % 2, 0, :], bank(2)[0:64, :], ACT.Copy)
                nc.scalar.activation(Q[64:128, u % 2, 1, :], bank(2)[64:128, :], ACT.Copy).then_inc(s.q_n, 1)

            for c in range(3):
                latent(0, c)
            q_nope(0)
            q_nope(1)
            for u in range(33):
                g, m = u // 8, u % 8
                if u < 32:
                    act.wait_ge(s.max_ready, u + 1)
                    if u >= 2:
                        act.wait_ge(s.p_xp, u - 1)
                        act.wait_ge(s.o_ready, u - 1)
                    for i in range(8):
                        ins = nc.scalar.activation(P[:, u % 2, i, :], bank(i // 4)[:, (i % 4) * 128:(i % 4 + 1) * 128], ACT.Exp,
                                                   bias=nm[:, u % 2, i:i + 1], scale=SCALE, accum_out=rs[:, u % 2, i:i + 1])
                    ins.then_inc(s.exp_done, 1)
                if g < 3 and m in (2, 4, 5):
                    latent(g + 1, (2, 4, 5).index(m))
                if u + 2 < 32:
                    q_nope(u + 2)
                if u >= 1:
                    act.wait_ge(s.o_xp, u)
                    if u - 1 >= 16:
                        act.wait_ge(s.op_ready, 8 * ((u - 1) // 8 - 1))
                    nc.scalar.activation(OT[(u - 1) // 8 % 2][:, (u - 1) % 8, :, :], bank(7).rearrange("p (b q) -> p b q", b=4),
                                         ACT.Copy).then_inc(s.ot_ready, 1)
                if u < 32:
                    act.wait_ge(s.p_xp, u + 1)
                    if u >= 2:
                        act.wait_ge(s.pv_ready, u - 1)
                    nc.scalar.activation(PT[:, u % 2, 0:4, :], bank(5).rearrange("p (i q) -> p i q", i=4), ACT.Copy).then_inc(s.pt_a, 1)
                if 25 <= u < 28:
                    i, w = u - 25, (w1f, w3f, w2f)[u - 25]
                    act.wait_ge(s.w_ffn, 64)
                    w = w.rearrange("p k n -> p (k n)")
                    nc.scalar.activation(wtmp[:, 0:w.shape[1]], w, ACT.Abs, accum_out=small[:, 32 + i:33 + i]).then_inc(s.abs_sum, 1)
                    act.wait_ge(s.abs_sum, i + 1)

            def split_rows(g):
                for t in range(2):
                    act.wait_ge(s.xn4_xp, 2 * g + t + 1)
                    if g >= 2:
                        act.wait_ge(s.up_ready, NC * (g - 1))
                    nc.scalar.activation(xp[g % 2][0][:, :, t * 256:(t + 1) * 256],
                                         bank(t).rearrange("p (k n) -> p k n", k=DK), ACT.Copy).then_inc(s.split_hi, 1)

            split_rows(0)
            for g in range(4):
                for c in range(NC):
                    n = NC * g + c
                    m = min(128, HID - c * 128)
                    act.wait_ge(s.up_ready, n + 1)
                    if n >= 2:
                        act.wait_ge(s.g_ready, n - 1)
                    nc.scalar.activation(sl[0:m, n % 2, :], bank(2 + 2 * (n % 2))[0:m, :], ACT.Silu,
                                         scale=small[0:m, 40:41]).then_inc(s.up_silu, 1)
                    act.wait_ge(s.g_ready, n + 1)
                    if g >= 2 and c == 0:
                        act.wait_ge(s.dn_ready, 4 * (g - 1))
                    nc.scalar.activation(gs[g % 2][0][0:m, c, :], gg[0:m, n % 2, :], ACT.Copy).then_inc(s.g_hi, 1)
                    if c == 3 and g < 3:
                        split_rows(g + 1)

        @block.tensor
        def _(pe):
            mm = nc.tensor.matmul
            tr = nc.tensor.transpose
            pe.wait_ge(s.const, 16)
            for u in range(NT // 2):
                pe.wait_ge(ctx_in[u // 2], HD0 * 16)
                if u >= 2:
                    pe.wait_ge(s.ctx_T, u - 1)
                for t in range(2):
                    for k in range(DK):
                        ins = tr(bank(2 * (u % 2))[:, (2 * t + k) * 128:(2 * t + k + 1) * 128],
                                 CS[:, 2 * u + t, k * 128:(k + 1) * 128], ident)
                ins.then_inc(s.ctx_xp, 1)
                pe.wait_ge(s.xn1, 2 * u + 2)
                if u >= 2:
                    pe.wait_ge(s.x_T, u - 1)
                for t in range(2):
                    for k in range(DK):
                        ins = tr(bank(2 * (u % 2) + 1)[:, (2 * t + k) * 128:(2 * t + k + 1) * 128],
                                 XN[:, 2 * u + t, k * 128:(k + 1) * 128], ident)
                ins.then_inc(s.x_xp, 1)

            def conv(h):
                pe.wait_ge(s.kv_ready, h + 1)
                if h % 4 == 0:
                    pe.wait_ge(toep[h // 4], 16)
                if h == 0:
                    pe.wait_ge(s.ctx_T, NT // 2)
                    pe.wait_ge(s.x_T, NT // 2)
                if h >= 2:
                    pe.wait_ge(s.prod_raw, h - 1)
                p = 3 * (h % 2)
                for lo, dst, n0, n in ((0, bank(p)[:, 0:PA * B], 0, PA * B), (0, bank(p + 2)[:, 0:PB * B], PA * B, PB * B),
                                       (1, bank(p + 1)[:, 0:PA * B], 0, PA * B),
                                       (1, bank(p + 2)[:, PB * B:2 * PB * B], PA * B, PB * B)):
                    for k in range(lo + 1):
                        ins = mm(dst, T[:, h, (lo - k) * 128:(lo - k + 1) * 128], kv[:, h % 2, k, n0:n0 + n],
                                 start=(k == 0), stop=(k == lo))
                ins.then_inc(s.y_ready, 1)

            def token_sum(t):
                pe.wait_ge(s.prod_ready, t + 1)
                if t >= 2:
                    pe.wait_ge(s.ln2_stats, t - 1)
                for k in range(DK):
                    for i in range(4):
                        ins = mm(bank(6 + t % 2)[:, k * 128:(k + 1) * 128], prod[:, t % 2, k, i * 128:(i + 1) * 128], ident,
                                 start=(i == 0), stop=(i == 3))
                ins.then_inc(s.out_ready, 1)

            for h in range(NT + 1):
                if h < NT:
                    conv(h)
                if h >= 1:
                    token_sum(h - 1)
            pe.wait_ge(s.prod_raw, NT)
            pe.wait_ge(s.shared_w, 5 * 16)
            for u in range(NT // 2 + 2):
                if u < NT // 2:
                    pe.wait_ge(s.xn2, 2 * u + 2)
                    if u >= 4:
                        pe.wait_ge(s.xn2_T, u - 3)
                    for t in range(2):
                        for k in range(DK):
                            ins = tr(bank(u % 4)[:, (2 * t + k) * 128:(2 * t + k + 1) * 128], XN[:, 2 * u + t, k * 128:(k + 1) * 128], ident)
                    ins.then_inc(s.xn2_xp, 1)
                if u >= 2:
                    pe.wait_ge(s.xn2_T, u - 1)
                    for t in range(2 * u - 4, 2 * u - 2):
                        for k in range(DK):
                            ins = mm(bank(4)[:, t * E:(t + 1) * E], QT[:, k, t, :], Wr[:, k, :], start=(k == 0), stop=(k == DK - 1))
            ins.then_inc(s.lg_ready, 1)

            def sh_down(g):
                pe.wait_ge(s.sh_h, g + 1)
                if g >= 1:
                    pe.wait_ge(s.sh_res, g)
                if g == 0:
                    pe.wait_ge(s.lg_sb, 1)
                for t in range(4):
                    ins = mm(bank(4 + t // 2)[:, (t % 2) * 256:(t % 2 + 1) * 256], shs[:, g % 2, t * 128:(t + 1) * 128], sWdn[:, :],
                             start=True, stop=True)
                ins.then_inc(s.sh_dn, 1)

            Mb = RT[:, 768:896].bitcast(bf16)
            pe.wait_ge(s.xn2_T, NT // 2)
            for g in range(4):
                if g >= 2:
                    pe.wait_ge(s.sh_h, g - 1)
                for c in range(2):
                    for k in range(DK):
                        ins = mm(bank(2 * (g % 2) + c), sWgu[:, k, c, :], QT[:, k, 4 * g:4 * g + 4, :].rearrange("p t n -> p (t n)"),
                                 start=(k == 0), stop=(k == DK - 1))
                ins.then_inc(s.sh_up, 1)
                if g == 1:
                    pe.wait_ge(s.onehot, 1)
                    mm(bank(6)[:, 0:256], trib, Mb, start=True, stop=True)
                    mm(bank(6)[:, 256:512], onesb[:, :], Mb, start=True, stop=True).then_inc(s.counts, 1)
                if g >= 1:
                    sh_down(g - 1)
            sh_down(3)
            pe.wait_ge(s.ab_w, 13 * 16)
            pe.wait_ge(s.sh_res, 4)
            for c in range(2):
                for i in range(8):
                    h = 8 * c + i
                    ins = mm(bank(4 + c)[0:QC, i * KVC:(i + 1) * KVC], uqT[:, h, :], ukT[:, h, :], start=True, stop=True)
                ins.then_inc(s.ab_ready, 1)
            pe.wait_ge(s.cnt_read, 1)
            pe.wait_ge(s.spread, 1)
            for v in range(4):
                ins = mm(bank(7)[:, v * B:(v + 1) * B], SP4[:, v, :], cf[:, C_B:C_B + B], start=True, stop=True)
            ins.then_inc(s.spread_ps, 1)
            pe.wait_ge(s.slotsB, 1)
            for c in range(4):
                if c >= 2:
                    pe.wait_ge(s.cw_sb, c - 1)
                for i in range(4):
                    h = 4 * c + i
                    lo = 64 * (h % 2)
                    ins = mm(bank(6 + c % 2)[lo:lo + 64, (i // 2) * 256:(i // 2 + 1) * 256], uvT[:, h, :], wo[:, h, :],
                             start=True, stop=True)
                ins.then_inc(s.cw_ready, 1)
            for c in range(4):
                if c >= 2:
                    pe.wait_ge(s.kc_sb, c - 1)
                for k in range(DK):
                    ins = mm(bank(c % 2), Wk2[:, k, :, :].rearrange("p a c -> p (a c)"),
                             CT[:, k, 4 * c:4 * c + 4, :].rearrange("p t n -> p (t n)"), start=(k == 0), stop=(k == DK - 1))
                ins.then_inc(s.kc_ready, 1)
            pe.wait_ge(s.kc_sb, 4)
            for c in range(4):
                if c >= 1:
                    pe.wait_ge(s.kr_mul, c)
                for z in range(2):
                    ins = mm(bank(2 + z), Wkr2[:, z, :, :].rearrange("p a c -> p (a c)"),
                             K01[0:64, 4 * c:4 * c + 4, :].rearrange("p b s -> p (b s)"), start=True, stop=True)
                ins.then_inc(s.kr_ready, 1)
            pe.wait_ge(s.cw_sb, 4)
            for c in range(2):
                for i in range(8):
                    ins = tr(bank(6 + c)[:, i * 64:(i + 1) * 64], K01[0:64, 8 * c + i, :], ident[0:64, 0:64])
                ins.then_inc(s.kt_ready, 1)
            pe.wait_ge(s.slots, 1)
            pe.wait_ge(s.moe_w, 5 * 16)
            pe.wait_ge(s.kt_sb, 2)
            pe.wait_ge(s.kr_mul, 4)
            experts = {}
            for n in range(NB + 3):
                if n < NB:
                    pe.wait_ge(xg_in[n % 4], 16 * (n // 4 + 1))
                    if n >= 2:
                        pe.wait_ge(s.xg_T, n - 1)
                    for k in range(DK):
                        ins = tr(bank(n % 2)[:, k * 128:(k + 1) * 128], xg[:, n % 4, k * 128:(k + 1) * 128], ident)
                    ins.then_inc(s.xg_xp, 1)
                m = n - 1
                if 0 <= m < NB:
                    e = pe.value_load(eid[0:1, m:m + 1], min_val=0, max_val=E - 1)
                    experts[m] = e
                    pe.wait_ge(s.xg_T, m + 1)
                    if m >= 2:
                        pe.wait_ge(s.h_ready, m - 1)
                    for k in range(DK):
                        ins = mm(bank(2 + m % 2)[:, 0:2 * I], xgT[:, m % 2, k, :], WGU[:, k, bass.ds(e, 1), :].rearrange("p e c -> p (e c)"),
                                 start=(k == 0), stop=(k == DK - 1))
                    ins.then_inc(s.gu_ready, 1)
                m = n - 2
                if 0 <= m < NB:
                    pe.wait_ge(s.h_ready, m + 1)
                    if m >= 2:
                        pe.wait_ge(s.h_T, m - 1)
                    tr(bank(4 + m % 2)[:, 0:I], hh[:, m % 2, :], ident).then_inc(s.h_xp, 1)
                m = n - 3
                if 0 <= m < NB:
                    pe.wait_ge(s.h_T, m + 1)
                    if m >= 2:
                        pe.wait_ge(s.y_sb, m - 1)
                    mm(bank(6 + m % 2)[:, 0:D], hT[:, m % 2, :], WD[:, bass.ds(experts.pop(m), 1), :].rearrange("p e d -> p (e d)"),
                       start=True, stop=True).then_inc(s.y_blk, 1)
            def latent(g, c):
                if c < 2:
                    pe.wait_ge(s.xn3, 4 * g + 2 * c + 2)
                    if g or c:
                        pe.wait_ge(s.rope_mul, rope_seen(g, c))
                    if c:
                        pe.wait_ge(s.xn3_T, 2 * g + c)
                    elif g:
                        pe.wait_ge(s.qc_ready, g)
                    for b in range(2):
                        for k in range(DK):
                            ins = tr(bank(4)[:, k * 256 + b * 128:k * 256 + (b + 1) * 128], xb[:, 2 * c + b, k * 128:(k + 1) * 128], ident)
                    ins.then_inc(s.xn3_xp, 1)
                else:
                    pe.wait_ge(s.xn3_T, 2 * g + 2)
                    if g:
                        pe.wait_ge(s.rope_mul, rope_seen(g, c))
                    for k in range(DK):
                        ins = mm(bank(4)[0:QC, :], Wdqs[:, k, :], xbT[:, k, :], start=(k == 0), stop=(k == DK - 1))
                    ins.then_inc(s.qc_ready, 1)

            def rope_seen(g, c):
                return 8 * (g - 1) + (2, 4, 5)[c] + 2 if g else 0

            def project(u, piece, side):
                g, m = u // 8, u % 8
                if m == 0:
                    pe.wait_ge(s.qc_sb, g + 1)
                if u:
                    pe.wait_ge(s.q_n, u)
                mm(bank(2), WN[:, m, :, :].rearrange("p a c -> p (a c)"), qc[g % 2], start=True, stop=True).then_inc(s.proj_n, 1)
                if u:
                    pe.wait_ge(s.rope_mul, u)
                if piece:
                    pe.wait_ge(s.res3, piece)
                mm(bank(3), WRA[:, m, :, :].rearrange("p a c -> p (a c)"), qc[g % 2], start=True, stop=True)
                if side is not None:
                    pe.wait_ge(*side)
                mm(bank(4), WRB[:, m, :, :].rearrange("p a c -> p (a c)"), qc[g % 2], start=True, stop=True).then_inc(s.proj, 1)

            def scores(u):
                g = u // 8
                pe.wait_ge(s.q_n, u + 1)
                pe.wait_ge(s.q_r, 2 * u + 2)
                if u >= 1:
                    pe.wait_ge(s.exp_done, u)
                for a, keys in enumerate((K01, K10)):
                    mm(bank(a), identb, maskb[:, 4 * g:4 * g + 4, :].rearrange("p b k -> p (b k)"), start=True, stop=False)
                    for b in range(4):
                        ins = mm(bank(a)[:, b * 128:(b + 1) * 128], Q[:, u % 2, a, b * 128:(b + 1) * 128], keys[:, 4 * g + b, :],
                                 start=False, stop=(b == 3))
                ins.then_inc(s.s_ready, 1)

            def attend(u):
                g = u // 8
                pe.wait_ge(s.pt_a, u + 1)
                pe.wait_ge(s.pt_d, u + 1)
                if u >= 1:
                    pe.wait_ge(s.ot_ready, u)
                for i in range(8):
                    ins = mm(bank(7)[:, i * 64:(i + 1) * 64], PT[:, u % 2, i, :], KVr[:, 4 * g + i % 4, :], start=True, stop=True)
                ins.then_inc(s.pv_ready, 1)

            def out_piece(i, b3):
                g, b, half = i // 8, i % 8 // 2, i % 2
                pe.wait_ge(s.ot_ready, 8 * (g + 1))
                for m in range(H // 2):
                    ins = mm(bank(b3)[:, 0:128], OT[g % 2][:, m, b, :], CW[:, m, half * 128:(half + 1) * 128],
                             start=(m == 0), stop=(m == H // 2 - 1))
                ins.then_inc(s.op_ready, 1)

            pe.wait_ge(s.mask, 2)
            pe.wait_ge(s.kr_sb, 4)
            pe.wait_ge(s.qr_w, 6 * 16)
            for c in range(3):
                latent(0, c)
            project(0, 0, (s.qc_sb, 1))
            project(1, 0, None)
            for u in range(33):
                g, m = u // 8, u % 8
                if u < 32:
                    scores(u)
                if u >= 1:
                    attend(u - 1)
                piece, side = 0, None
                if u >= 9:
                    pe.wait_ge(s.rope_mul, min(u + 2, 32))
                    out_piece(u - 9, 3)
                    piece = u - 8
                if g < 3 and m in (2, 4, 5):
                    c = (2, 4, 5).index(m)
                    latent(g + 1, c)
                    side = (s.xn3_T, 2 * (g + 1) + c + 1) if c < 2 else (s.qc_sb, g + 2)
                if u == 29:
                    pe.wait_ge(s.abs_sum, 3)
                    pe.wait_ge(s.rope_mul, u + 2)
                    mm(bank(4)[:, 0:3], onesf[:, :], small[:, 32:35], start=True, stop=True).then_inc(s.scale_r, 1)
                    side = (s.scale_sb, 1)
                if u + 2 < 32:
                    project(u + 2, piece, side)
                if u >= 1:
                    pe.wait_ge(s.o_ready, u)
                    for b in range(4):
                        ins = tr(bank(7)[:, b * 128:(b + 1) * 128], O[:, (u - 1) % 2, b, :, :].rearrange("p h c -> p (h c)"), ident)
                    ins.then_inc(s.o_xp, 1)
                if u < 32:
                    pe.wait_ge(s.exp_done, u + 1)
                    if u >= 1:
                        pe.wait_ge(s.pt_a, u)
                        pe.wait_ge(s.pt_d, u)
                    for i in range(8):
                        ins = tr(bank(5 + i // 4)[:, (i % 4) * 128:(i % 4 + 1) * 128], P[:, u % 2, i, :], ident)
                    ins.then_inc(s.p_xp, 1)

            def rows(g):
                for t in range(2):
                    pe.wait_ge(s.xn4, 4 * g + 2 * t + 2)
                    if g >= 1:
                        pe.wait_ge(s.split_lo, 2 * (g - 1) + t + 1)
                    else:
                        pe.wait_ge(s.exp_done, 32)
                    for b in range(2):
                        for k in range(DK):
                            ins = tr(bank(t)[:, k * 256 + b * 128:k * 256 + (b + 1) * 128], x3n[:, 2 * t + b, k * 128:(k + 1) * 128], ident)
                    ins.then_inc(s.xn4_xp, 1)

            def up(n):
                g, c = n // NC, n % NC
                m = min(128, HID - c * 128)
                if n >= 2:
                    pe.wait_ge(s.g_ready, n - 1)
                for z, w in enumerate((w1q, w3q)):
                    for k in range(DK):
                        for q in range(2):
                            ins = mm(bank(2 + 2 * (n % 2) + z)[0:m, :], w[:, k, c * 128:c * 128 + m], xp[g % 2][q][:, k, :],
                                     start=(k == 0 and q == 0), stop=(k == DK - 1 and q == 1))
                ins.then_inc(s.up_ready, 1)

            def down(g):
                pe.wait_ge(s.g_lo, NC * (g + 1))
                for b in range(4):
                    if g >= 1 or b >= 2:
                        pe.wait_ge(s.yout, 4 * g + b - 1)
                    for c in range(NC):
                        m = min(128, HID - c * 128)
                        for q, part in enumerate(gs[g % 2]):
                            ins = mm(bank(6 + b % 2)[:, 0:D], part[0:m, c, b * 128:(b + 1) * 128], w2q[0:m, c, :],
                                     start=(c == 0 and q == 0), stop=(c == NC - 1 and q == 2))
                    ins.then_inc(s.dn_ready, 1)

            for i in range(24, 32):
                pe.wait_ge(s.res3, max(24, i - 1))
                out_piece(i, 3 + i % 2)
                if i == 26:
                    rows(0)
            pe.wait_ge(s.ternary, 3)
            pe.wait_ge(s.split_lo, 2)
            pe.wait_ge(s.res3, 32)
            for n in range(4 * NC):
                if n % NC == 0 and n:
                    pe.wait_ge(s.split_lo, 2 * (n // NC) + 2)
                up(n)
                if n % NC == 2 and n // NC < 3:
                    rows(n // NC + 1)
                if n % NC == 1 and n > NC:
                    down(n // NC - 1)
            down(3)

        @block.gpsimd
        def _(pool):
            tt = nc.gpsimd.tensor_tensor
            nc.gpsimd.memset(zero[:, :], 0.0).then_inc(s.memsets, 1)
            nc.gpsimd.memset(mhalf[:, :], -0.5)
            nc.gpsimd.memset(onesb[:, :], 1.0)
            nc.gpsimd.memset(onesf[:, :], 1.0).then_inc(s.memsets, 1)
            pool.wait_ge(s.memsets, 2)
            done = [0]

            def rsqrt(lo, n, wait, value, signal):
                pool.wait_ge(wait, value)
                nc.gpsimd.tensor_scalar(rstd[:, lo:lo + n], mv[:, lo:lo + n, 1], LN_EPS, None, ALU.add).then_inc(s.pool, 1)
                done[0] += 1
                pool.wait_ge(s.pool, done[0])
                tt(rstd[:, lo:lo + n], rstd[:, lo:lo + n], mhalf[:, lo:lo + n], ALU.pow).then_inc(signal, 1)

            for c in range(4):
                rsqrt(4 * c, 4, s.ln1_stats, c + 1, s.rstd1)

            def products(h):
                pool.wait_ge(s.ctx_T, h // 2 + 1)
                if h >= 2:
                    pool.wait_ge(s.y_ready, h - 1)
                for i in range(HD0):
                    n = i + 1
                    c = CT[:, :, h, :]
                    ins = tt(kv[:, h % 2, :, pair(i) * B:(pair(i) + n) * B].rearrange("p k (j b) -> p k j b", b=B),
                             c[:, :, 0:n * B].rearrange("p k (j b) -> p k j b", b=B),
                             c[:, :, i * B:(i + 1) * B].unsqueeze(2).to_broadcast([128, DK, n, B]), ALU.mult)
                ins.then_inc(s.kv_ready, 1)

            products(0)
            products(1)
            for h in range(NT):
                if h + 2 < NT:
                    products(h + 2)
                rsqrt(h, 1, s.ln2_stats, h + 1, s.rstd2)
            pool.wait_ge(s.zinit, 4 * 16)
            pool.wait_ge(s.slots, 1)
            pool.wait_ge(s.xn2, NT)
            for t in range(NT):
                for q in range(2):
                    pool.indirect_dma_start(out=XG, out_offset=bass.IndirectOffsetOnAxis(ap=slot[:, q, t:t + 1], axis=0),
                                            in_=XN[:, t, :], in_offset=None).then_inc(s.scat, 16)
            for i in range(4):
                pool.wait_ge(yg_out[i], 16 * ((NB - i + 3) // 4))
            pool.wait_ge(s.slotsB, 1)

            def gather(b):
                if b >= 4:
                    pool.wait_ge(s.res2, b - 3)
                for q in range(2):
                    pool.indirect_dma_start(out=gb[:, b % 4, q, :], out_offset=None, in_=YG,
                                            in_offset=bass.IndirectOffsetOnAxis(ap=slotB[:, q, b:b + 1], axis=0)).then_inc(gat[b % 4], 16)

            for b in range(4):
                gather(b)
            for b in range(4):
                rsqrt(b, 1, s.ln3_stats, b + 1, s.rstd3)
            for u in range(32):
                pool.wait_ge(s.rope_mul, u + 1)
                if u >= 2:
                    pool.wait_ge(s.s_ready, u - 1)
                tt(Q[64:128, u % 2, 0, :], ra[64:128, u % 2, :], rbm[64:128, u % 2, :], ALU.add).then_inc(s.q_r, 1)
                pool.wait_ge(s.q_r, 2 * u + 1)
                tt(Q[0:64, u % 2, 1, :], ra[0:64, u % 2, :], rbm[0:64, u % 2, :], ALU.add).then_inc(s.q_r, 1)
                pool.wait_ge(s.q_r, 2 * u + 2)
                v = u - 2
                if 0 <= v < 24 and v % 8 < 4:
                    b = 4 * (v // 8 + 1) + v % 8
                    rsqrt(b, 1, s.ln3_stats, b + 1, s.rstd3)
                if 0 <= v + 1 < 24 and (v + 1) % 8 < 4:
                    gather(4 * ((v + 1) // 8 + 1) + (v + 1) % 8)
            rsqrt(0, 4, s.d_stats, 1, s.rstd4)
            for n in range(4 * NC):
                g, c = n // NC, n % NC
                m = min(128, HID - c * 128)
                pool.wait_ge(s.g_r, n + 1)
                nc.gpsimd.tensor_copy(gs[g % 2][1][0:m, c, :], gr[0:m, c % 2, :]).then_inc(s.g_mid, 1)
                if c == 0 and g < 3:
                    rsqrt(4 * (g + 1), 4, s.d_stats, g + 2, s.rstd4)

        @block.vector
        def _(dve):
            tt = nc.vector.tensor_tensor
            ts = nc.vector.tensor_scalar
            stt = nc.vector.scalar_tensor_tensor
            red = nc.vector.tensor_reduce
            steps = [0]

            def link(ins):
                steps[0] += 1
                ins.then_inc(s.dve, 1)
                dve.wait_ge(s.dve, steps[0])

            def stats(t, wait_last, signal):
                link(nc.vector.bn_stats(st[:, t, :], X[:, t, :]))
                ins = nc.vector.bn_aggr(mv[:, t, :], st[:, t, :])
                if signal is not None:
                    ins.then_inc(signal, 1)

            def normalise(t, dst):
                return ts(dst, X[:, t, :], mv[:, t, 0:1], rstd[:, t:t + 1], ALU.subtract, ALU.mult)

            link(nc.vector.memset(zk[:, :], 0.0))
            nc.vector.tensor_copy(dsb[:, :], zk[:, 0:1]).then_inc(s.zk_set, 1)
            dve.wait_ge(s.ssm, 32)
            tt(zk[:, 127:128], zk[:, 127:128], dsb[:, :], ALU.add).then_inc(s.zk_d, 1)
            for c in range(5):
                if c < 4:
                    dve.wait_ge(x_in[c], HD0 * 16)
                    for t in range(4 * c, 4 * c + 4):
                        stats(t, None, s.ln1_stats if t == 4 * c + 3 else None)
                if c >= 1:
                    dve.wait_ge(s.rstd1, c)
                    for t in range(4 * c - 4, 4 * c):
                        normalise(t, XN[:, t, :]).then_inc(s.xn1, 1)
            for u in range(NT // 2):
                dve.wait_ge(s.x_xp, u + 1)
                nc.vector.tensor_copy(QT[:, :, 2 * u:2 * u + 2, :].rearrange("p k t n -> p t k n"),
                                      bank(2 * (u % 2) + 1).rearrange("p (t k n) -> p t k n", t=2, k=DK)).then_inc(s.x_T, 1)
            dve.wait_ge(s.x_T, NT // 2)
            dve.wait_ge(s.tg_ready, 1)
            dve.wait_ge(s.const, 16)
            link(nc.vector.tensor_copy(identb, ident))
            link(nc.vector.tensor_copy(trib, cf[:, C_UP:C_UP + 128]))
            L = RT[:, 0:256].rearrange("p (t e) -> p t e", t=NT)
            for h in range(NT + 2):
                if h < NT:
                    dve.wait_ge(s.y_ready, h + 1)
                    if h >= 2:
                        dve.wait_ge(s.out_ready, h - 1)
                    pr = prod[:, h % 2, :, :].rearrange("p k (i j b) -> p k i j b", i=HD0, j=HD0)
                    q = QT[:, :, h, :].rearrange("p k (i b) -> p k i b", b=B)
                    p = 3 * (h % 2)
                    for i in range(HD0):
                        if i <= 5:
                            y = bank(p, 2)[:, :, pair(i) * B:(pair(i) + i + 1) * B]
                        else:
                            o = (pair(i) - PA) * B
                            y = bank(p + 2)[:, 0:2 * PB * B].rearrange("p (k n) -> p k n", k=2)[:, :, o:o + (i + 1) * B]
                        y = y.rearrange("p k (j b) -> p k j b", b=B)
                        ins = tt(pr[:, :, i, 0:i + 1, :], y, q[:, :, i, :].unsqueeze(2).to_broadcast([128, DK, i + 1, B]), ALU.mult)
                        if i:
                            ins = tt(pr[:, :, 0:i, i, :], y[:, :, 0:i, :], q[:, :, 0:i, :], ALU.mult)
                    ins.then_inc(s.prod_raw, 1)
                    dve.wait_ge(s.prod_raw, h + 1)
                    tt(prod[:, h % 2, :, 0:512], prod[:, h % 2, :, 0:512], prod[:, h % 2, :, 512:1024], ALU.add).then_inc(s.prod_ready, 1)
                t = h - 1
                if 0 <= t < NT:
                    dve.wait_ge(s.out_ready, t + 1)
                    link(stt(X[:, t, :], bank(6 + t % 2)[:, 0:256], tg[:, 0:1], X[:, t, :], ALU.mult, ALU.add))
                    stats(t, None, s.ln2_stats)
                t = h - 2
                if 0 <= t < NT:
                    dve.wait_ge(s.rstd2, t + 1)
                    normalise(t, XN[:, t, :]).then_inc(s.xn2, 1)
            dve.wait_ge(s.lg_ready, 1)
            dve.wait_ge(s.shared_w, 5 * 16)
            tt(L, bank(4)[:, 0:256].rearrange("p (t e) -> p t e", t=NT), rb[:, :].unsqueeze(1).to_broadcast([128, NT, E]),
               ALU.add).then_inc(s.lg_sb, 1)
            dve.wait_ge(s.lg_sb, 1)

            def ob(ap):
                return ap.unsqueeze(2).to_broadcast([128, 16, 16])

            def mb(ap):
                return ap.unsqueeze(1).to_broadcast([128, 16, 16])

            m16, s16 = small[:, 0:16], small[:, 16:32]
            link(red(m16, L, AX, ALU.max))
            tt(L, L, ob(m16), ALU.subtract).then_inc(s.max_sub, 1)
            dve.wait_ge(s.exp_r, 1)
            link(red(s16, L, AX, ALU.add))
            link(nc.vector.reciprocal(s16, s16))
            link(tt(L, L, ob(s16), ALU.mult))
            top = R2[:, 0:128].rearrange("p (t v) -> p t v", t=NT)
            idx = R2[:, 128:256].bitcast(u32).rearrange("p (t v) -> p t v", t=NT)
            for t in range(NT):
                ins = nc.vector.max(top[:, t, :], L[:, t, :])
            link(ins)
            for t in range(NT):
                ins = nc.vector.max_index(idx[:, t, :], top[:, t, :], L[:, t, :])
            link(ins)
            idf = R2[:, 256:288].rearrange("p (v t) -> p v t", v=2)
            link(nc.vector.tensor_copy(idf.rearrange("p v t -> p t v"), idx[:, :, 0:2]))
            oh = RT[:, 256:768].rearrange("p (v t e) -> p v t e", v=2, t=NT)
            for v in range(2):
                ins = tt(oh[:, v], ob(idf[:, v, :]), mb(cf[:, C_IOTA:C_IOTA + 16]), ALU.is_equal)
            link(ins)
            Mb = RT[:, 768:896].bitcast(bf16).rearrange("p (t e) -> p t e", t=NT)
            tt(Mb, oh[:, 0], oh[:, 1], ALU.add).then_inc(s.onehot, 1)
            link(tt(m16, top[:, :, 0], top[:, :, 1], ALU.add))
            link(ts(m16, m16, W_EPS, None, ALU.add))
            link(nc.vector.reciprocal(m16, m16))
            link(ts(m16, m16, tg[:, 2:3], None, ALU.mult))
            for v in range(2):
                ins = tt(wc[:, v, :], top[:, :, v], m16, ALU.mult)
            link(ins)
            dve.wait_ge(s.counts, 1)
            rank = bank(6)[:, 0:256].rearrange("p (t e) -> p t e", t=NT)
            Rb = R2[:, 320:592].rearrange("p (t e) -> p t e", t=NT + 1)
            link(nc.vector.memset(Rb[:, 0, :], 0.0))
            for t in range(NT):
                link(tt(Rb[:, t + 1, :], bank(6)[:, 256 + t * 16:272 + t * 16], Rb[:, t, :], ALU.add))
            tmp = R2[:, 640:896].rearrange("p (a b) -> p a b", a=16)
            nb_, sb_, en_ = small[:, 0:16], small[:, 16:32], small[:, 48:64]
            link(tt(tmp, ob(Rb[:, NT, :]), mb(cf[:, C_THR:C_THR + 16]), ALU.is_gt))
            link(red(nb_, tmp, AX, ALU.add))
            link(tt(tmp, cf[:, C_TRI:C_TRI + 256].rearrange("p (a b) -> p a b", a=16), mb(nb_), ALU.mult))
            link(red(sb_, tmp, AX, ALU.add))
            link(tt(en_, sb_, nb_, ALU.add))
            link(stt(Rb[:, 0:NT, :], mb(sb_), 128.0, Rb[:, 0:NT, :], ALU.mult, ALU.add))
            tt(Rb[:, 0:NT, :], rank, Rb[:, 0:NT, :], ALU.add).then_inc(s.cnt_read, 1)
            dve.wait_ge(s.cnt_read, 1)
            slf = R2[:, 288:320].rearrange("p (v t) -> p v t", v=2)
            for v in range(2):
                link(tt(tmp, oh[:, v], Rb[:, 0:NT, :], ALU.mult))
                link(red(slf[:, v, :], tmp, AX, ALU.add))
            link(nc.vector.tensor_copy(slot[:, :, :], slf))
            for v in range(4):
                src = slf[:, v, :] if v < 2 else wc[:, v - 2, :]
                ins = tt(SP4[:, v, :].rearrange("p (h j) -> p h j", j=HD0), src.unsqueeze(2).to_broadcast([128, NT, HD0]),
                         cf[:, C_J:C_J + HD0].unsqueeze(1).to_broadcast([128, NT, HD0]), ALU.mult)
            ins.then_inc(s.spread, 1)
            dve.wait_ge(s.spread, 1)
            tb = R2[:, 0:NB * E].rearrange("p (n e) -> p n e", e=E)
            ef = R2[:, 768:768 + NB]
            link(tt(tb, en_.unsqueeze(1).to_broadcast([128, NB, E]), cf[:, C_BLK:C_BLK + NB].unsqueeze(2).to_broadcast([128, NB, E]), ALU.is_le))
            link(red(ef, tb, AX, ALU.add))
            link(ts(ef, ef, float(E - 1), None, ALU.min))
            nc.vector.tensor_copy(eid[:, :], ef).then_inc(s.slots, 1)
            dve.wait_ge(s.slots, 1)

            for g in range(5):
                if g < 4:
                    dve.wait_ge(s.sh_silu, g + 1)
                    if g >= 2:
                        dve.wait_ge(s.sh_dn, g - 1)
                    tt(shs[:, g % 2, :], shs[:, g % 2, :], bank(2 * (g % 2) + 1), ALU.mult).then_inc(s.sh_h, 1)
                if g >= 1:
                    dve.wait_ge(s.sh_dn, g)
                    for c in range(2):
                        t = 4 * (g - 1) + 2 * c
                        ins = stt(X[:, t:t + 2, :], bank(4 + c).rearrange("p (t d) -> p t d", t=2), tg[:, 2:3], X[:, t:t + 2, :], ALU.mult, ALU.add)
                    ins.then_inc(s.sh_res, 1)
            dve.wait_ge(s.sh_res, 4)
            dve.wait_ge(s.spread_ps, 1)
            nc.vector.tensor_copy(slotB[:, :, :], bank(7)[:, 0:2 * B].rearrange("p (v b) -> p v b", v=2))
            nc.vector.tensor_copy(wcB[:, :, :], bank(7)[:, 2 * B:4 * B].rearrange("p (v b) -> p v b", v=2)).then_inc(s.slotsB, 1)
            dve.wait_ge(s.slotsB, 1)
            dve.wait_ge(s.seg, 16)
            link(nc.vector.tensor_copy(segf[:, :], segi[:, :]))
            for c in range(2):
                d = R2[:, 0:1024].rearrange("p (b k) -> p b k", b=8)
                link(tt(d, cf[:, C_K4:C_K4 + 128].unsqueeze(1).to_broadcast([128, 8, 128]),
                        segf[:, 8 * c:8 * c + 8].unsqueeze(2).to_broadcast([128, 8, 128]), ALU.subtract))
                link(tt(d, d, d, ALU.mult))
                ts(maskb[:, 8 * c:8 * c + 8, :], d, (LOOKBACK / 2.0) ** 2, NEG, ALU.is_gt, ALU.mult).then_inc(s.mask, 1)
                dve.wait_ge(s.mask, c + 1)
            for c in range(4):
                dve.wait_ge(s.kr_ready, c + 1)
                for z, w in enumerate((cosT, sinT)):
                    ins = tt(R2[:, z * 512:(z + 1) * 512].rearrange("p (b s) -> p b s", b=4),
                             bank(2 + z).rearrange("p (b s) -> p b s", b=4), w.unsqueeze(1).to_broadcast([128, 4, 128]), ALU.mult)
                ins.then_inc(s.kr_mul, 1)
                dve.wait_ge(s.kr_mul, c + 1)
                for lo, dst in ((64, K01), (0, K10)):
                    ins = tt(dst[lo:lo + 64, 4 * c:4 * c + 4, :].rearrange("p b s -> p (b s)"), R2[lo:lo + 64, 0:512],
                             R2[lo:lo + 64, 512:1024], ALU.add)
                ins.then_inc(s.kr_sb, 1)
                dve.wait_ge(s.kr_sb, c + 1)

            for n in range(NB + 2):
                if n < NB:
                    dve.wait_ge(s.silu, n + 1)
                    if n >= 2:
                        dve.wait_ge(s.h_xp, n - 1)
                    tt(hh[:, n % 2, :], sg[:, n % 2, :], bank(2 + n % 2)[:, I:2 * I], ALU.mult).then_inc(s.h_ready, 1)
                m = n - 1
                if 0 <= m < NB:
                    dve.wait_ge(s.h_xp, m + 1)
                    if m >= 2:
                        dve.wait_ge(s.y_blk, m - 1)
                    nc.vector.tensor_copy(hT[:, m % 2, :], bank(4 + m % 2)[:, 0:I]).then_inc(s.h_T, 1)
                m = n - 2
                if 0 <= m < NB:
                    dve.wait_ge(s.y_blk, m + 1)
                    if m >= 4:
                        dve.wait_ge(yg_out[m % 4], 16 * (m // 4))
                    nc.vector.tensor_copy(yb[:, m % 4, :], bank(6 + m % 2)[:, 0:D]).then_inc(s.y_sb, 1)

            def combine(b):
                dve.wait_ge(gat[b % 4], 32 * (b // 4 + 1))
                if b == 0:
                    dve.wait_ge(s.xin, 16)
                link(stt(X[:, b, :], gb[:, b % 4, 0, :], wcB[:, 0, b:b + 1], X[:, b, :], ALU.mult, ALU.add))
                stt(X[:, b, :], gb[:, b % 4, 1, :], wcB[:, 1, b:b + 1], X[:, b, :], ALU.mult, ALU.add).then_inc(s.res2, 1)
                dve.wait_ge(s.res2, b + 1)
                stats(b, None, s.ln3_stats)

            def row(b):
                dve.wait_ge(s.rstd3, b + 1)
                if b >= 4:
                    dve.wait_ge(s.xn3_xp, 2 * (b // 4))
                normalise(b, xb[:, b % 4, :]).then_inc(s.xn3, 1)

            def rope(u):
                dve.wait_ge(s.proj, u + 1)
                if u >= 2:
                    dve.wait_ge(s.q_r, 2 * u - 2)
                for z, (dst, w) in enumerate(((ra, cosT), (rbm, sinT))):
                    ins = tt(dst[:, u % 2, :].rearrange("p (b s) -> p b s", b=4), bank(3 + z).rearrange("p (b s) -> p b s", b=4),
                             w.unsqueeze(1).to_broadcast([128, 4, 128]), ALU.mult)
                ins.then_inc(s.rope_mul, 1)

            def residual(i, b3):
                b, half = 4 * (i // 8) + i % 8 // 2, i % 2
                dve.wait_ge(s.op_ready, i + 1)
                x_ = X[:, b, half * 128:(half + 1) * 128]
                stt(x_, bank(b3)[:, 0:128], tg[:, 1:2], x_, ALU.mult, ALU.add).then_inc(s.res3, 1)

            sc = small[:, 40:43]

            def scales():
                dve.wait_ge(s.scale_r, 1)
                ts(sc, bank(4)[:, 0:3], 1.0 / (HID * D), None, ALU.mult).then_inc(s.scale_sb, 1)
                dve.wait_ge(s.scale_sb, 1)
                link(ts(small[:, 43:46], sc, 0.5, None, ALU.mult))
                link(ts(small[:, 46:49], sc, -0.5, None, ALU.mult))
                link(tt(small[:, 49:50], sc[:, 2:3], tg[:, 3:4], ALU.mult))

            def ternary(i):
                w, q, n = ((w1f, w1q, DK * HID), (w3f, w3q, DK * HID), (w2f, w2q, NC * D))[i]
                w, q = w.rearrange("p k n -> p (k n)"), q.rearrange("p k n -> p (k n)")
                low = wtmp[:, 0:n]
                link(ts(low, w, small[:, 46 + i:47 + i], None, ALU.is_lt))
                stt(q, w, small[:, 43 + i:44 + i], low, ALU.is_gt, ALU.subtract).then_inc(s.ternary, 1)
                dve.wait_ge(s.ternary, i + 1)

            for b in range(4):
                combine(b)
            for b in range(4):
                row(b)
            rope(0)
            rope(1)
            for u in range(33):
                if 0 <= u - 1 < 24 and (u - 1) % 8 < 4:
                    row(4 * ((u - 1) // 8 + 1) + (u - 1) % 8)
                if u < 32:
                    dve.wait_ge(s.s_ready, u + 1)
                    link(red(mx[:, u % 2, :], bank(0, 2).rearrange("p a (i k) -> p (a i) k", i=4), AX, ALU.max))
                    if u >= 2:
                        dve.wait_ge(s.exp_done, u - 1)
                    ts(nm[:, u % 2, :], mx[:, u % 2, :], -SCALE, None, ALU.mult).then_inc(s.max_ready, 1)
                if u >= 1:
                    dve.wait_ge(s.pv_ready, u)
                    dve.wait_ge(s.exp_done, u)
                    if u >= 3:
                        dve.wait_ge(s.o_xp, u - 2)
                    link(nc.vector.reciprocal(ri[:, (u - 1) % 2, :], rs[:, (u - 1) % 2, :]))
                    tt(O[:, (u - 1) % 2].rearrange("p b h c -> p h b c"), bank(7).rearrange("p (h b c) -> p h b c", h=2, b=4),
                       ri[:, (u - 1) % 2, :].rearrange("p (h b) -> p h b", h=2).unsqueeze(3).to_broadcast([128, 2, 4, KVC]),
                       ALU.mult).then_inc(s.o_ready, 1)
                if u < 24 and u % 8 < 4:
                    combine(4 * (u // 8 + 1) + u % 8)
                if u >= 9:
                    residual(u - 9, 3)
                if u == 29:
                    scales()
                if u + 2 < 32:
                    rope(u + 2)
                if u < 32:
                    dve.wait_ge(s.p_xp, u + 1)
                    if u >= 2:
                        dve.wait_ge(s.pv_ready, u - 1)
                    nc.vector.tensor_copy(PT[:, u % 2, 4:8, :], bank(6).rearrange("p (i q) -> p i q", i=4)).then_inc(s.pt_d, 1)
                if u == 19:
                    nc.vector.memset(w2f[:, NC - 1, :], 0.0).then_inc(s.w_abs, 1)
                if u >= 30:
                    ternary(u - 30)

            def rows(g):
                for b in range(4 * g, 4 * g + 4):
                    stats(b, None, s.d_stats if b == 4 * g + 3 else None)
                dve.wait_ge(s.rstd4, g + 1)
                if g >= 1:
                    dve.wait_ge(s.xn4_xp, 2 * g)
                for b in range(4):
                    normalise(4 * g + b, x3n[:, b, :]).then_inc(s.xn4, 1)

            def split_rows(g):
                for t in range(2):
                    h = slice(t * 256, (t + 1) * 256)
                    dve.wait_ge(s.split_hi, 2 * g + t + 1)
                    tt(xp[g % 2][1][:, :, h], bank(t).rearrange("p (k n) -> p k n", k=DK), xp[g % 2][0][:, :, h],
                       ALU.subtract).then_inc(s.split_lo, 1)

            def low_part(n):
                g, c = n // NC, n % NC
                m = min(128, HID - c * 128)
                dve.wait_ge(s.g_mid, n + 1)
                tt(gs[g % 2][2][0:m, c, :], gr[0:m, c % 2, :], gs[g % 2][1][0:m, c, :], ALU.subtract).then_inc(s.g_lo, 1)

            def output(g):
                for b in range(4):
                    dve.wait_ge(s.dn_ready, 4 * g + b + 1)
                    stt(X[:, 4 * g + b, :], bank(6 + b % 2)[:, 0:D], small[:, 49:50], X[:, 4 * g + b, :], ALU.mult, ALU.add).then_inc(s.yout, 1)

            rows(0)
            for i in range(24, 32):
                residual(i, 3 + i % 2)
                if i == 28:
                    split_rows(0)
            for n in range(4 * NC):
                g, c = n // NC, n % NC
                m = min(128, HID - c * 128)
                dve.wait_ge(s.up_silu, n + 1)
                stt(gg[0:m, n % 2, :], bank(3 + 2 * (n % 2))[0:m, :], sc[0:m, 1:2], sl[0:m, n % 2, :], ALU.mult, ALU.mult).then_inc(s.g_ready, 1)
                if n >= 1:
                    low_part(n - 1)
                dve.wait_ge(s.g_hi, n + 1)
                tt(gr[0:m, c % 2, :], gg[0:m, n % 2, :], gs[g % 2][0][0:m, c, :], ALU.subtract).then_inc(s.g_r, 1)
                if c == 0 and g < 3:
                    rows(g + 1)
                if c == 4 and g < 3:
                    split_rows(g + 1)
                if c == 1 and g >= 1:
                    output(g - 1)
            low_part(4 * NC - 1)
            output(3)


_OUT = (B, S, D)


def _constants():
    import numpy as np
    p = np.arange(128)
    cf = np.zeros((128, NCF), np.float32)
    cf[:, C_ID:C_ID + 128] = np.eye(128)
    half = R // 2
    inv = (1.0 / np.float32(10000.0) ** (np.arange(half, dtype=np.float32) / np.float32(half))).astype(np.float32)
    ang = np.arange(128, dtype=np.float32)[None, :] * inv[p % half][:, None]
    cf[:, C_COS:C_COS + 128] = np.cos(ang)
    cf[:, C_SIN:C_SIN + 128] = np.sin(ang) * np.where(p % R < half, -1.0, 1.0)[:, None]
    cf[:, C_K4:C_K4 + 128] = p[None, :] + LOOKBACK // 2
    cf[:, C_TRI:C_TRI + 256] = np.tril(np.ones((16, 16)), -1).reshape(1, 256)
    cf[:, C_THR:C_THR + 16] = 128 * np.arange(16)
    cf[:, C_IOTA:C_IOTA + 16] = np.arange(16)
    cf[:, C_BLK:C_BLK + NB] = np.arange(NB)
    cf[:, C_UP:C_UP + 128] = np.triu(np.ones((128, 128)), 1)
    cf[:, C_J:C_J + HD0] = p[:, None] // B == np.arange(HD0)
    cf[:, C_B:C_B + B] = p[:, None] % B == np.arange(B)
    return cf


def kernel(x, ctx_2048, itok_BxS_0_1023, g_xattn, g_ffn, L0_xattn_ssm_kernel, L0_xattn_D, L0_ffn_Wr, L0_ffn_bias,
           L0_ffn_Wg, L0_ffn_Wu, L0_ffn_Wd, L0_ffn_sWg, L0_ffn_sWu, L0_ffn_sWd, L1_xattn_W_kvc, L1_xattn_W_dq,
           L1_xattn_W_uq, L1_xattn_W_qr, L1_xattn_W_uk, L1_xattn_W_kr, L1_xattn_W_uv, L1_xattn_W_o,
           L1_ffn_w1, L1_ffn_w3, L1_ffn_w2):
    import numpy as np
    import concourse.bacc as bacc
    from concourse import mybir
    from concourse.bass_utils import run_bass_kernel_spmd

    def t(a):
        return np.ascontiguousarray(np.asarray(a).T)

    def back(a, axis):
        a = np.asarray(a)
        halves = a.reshape(a.shape[:axis] + (DK, 128) + a.shape[axis + 1:])
        return np.ascontiguousarray(np.flip(halves, axis + 1)).reshape(a.shape)

    cf = _constants()
    given = {
        "x": x, "ctxd": back(ctx_2048, 2), "segT": t(itok_BxS_0_1023), "gates": np.concatenate([np.asarray(g_xattn), np.asarray(g_ffn)]),
        "ssm": L0_xattn_ssm_kernel, "ssmD": L0_xattn_D, "WrT": t(L0_ffn_Wr), "rbias": L0_ffn_bias,
        "Wg": L0_ffn_Wg, "Wu": L0_ffn_Wu, "Wd": L0_ffn_Wd, "sWg": L0_ffn_sWg, "sWu": L0_ffn_sWu, "sWd": L0_ffn_sWd,
        "Wkvc": back(L1_xattn_W_kvc, 0), "Wdq": L1_xattn_W_dq, "WuqT": t(L1_xattn_W_uq), "Wqr": L1_xattn_W_qr,
        "WukT": t(L1_xattn_W_uk), "Wkr": L1_xattn_W_kr, "WuvT": t(L1_xattn_W_uv), "Wo": L1_xattn_W_o,
        "w1T": t(L1_ffn_w1), "w3T": t(L1_ffn_w3), "w2T": t(L1_ffn_w2), "constf": cf,
    }
    nc = bacc.Bacc("TRN2", target_bir_lowering=False, num_devices=1)
    arrays, args = {}, []
    for name, a in given.items():
        a = np.ascontiguousarray(a)
        arrays[f"in_{name}"] = a
        args.append(nc.dram_tensor(f"in_{name}", a.shape, mybir.dt.from_np(a.dtype), kind="ExternalInput").ap())
    args.append(nc.dram_tensor("out_0", _OUT, mybir.dt.float32, kind="ExternalOutput").ap())
    flamingo_kernel(nc, *args)
    r = run_bass_kernel_spmd(nc, [arrays], core_ids=[0])
    return r.results[0]["out_0"]
```

```python
import concourse.bass as bass
from concourse import mybir
from contextlib import ExitStack

B, S, D = 16, 128, 256
NT = 16
DK = D // 128
E, I = 16, 128
NH0, HD0 = 16, 8
NB = 47
H, HD, KVC, QC, R = 16, 128, 64, 96, 64
HID = 682
NC = (HID + 127) // 128
LAST = HID - (NC - 1) * 128
NPAIR = HD0 * (HD0 + 1) // 2
PA = 21
PB = NPAIR - PA
LN_EPS = 1e-5
W_EPS = 1e-9
NEG = -1e30
LOOKBACK = 8
FFN_ROWS = (26, 27)
FFN_SCALE = 24
POOL_SUM = 256
PARTNER = [(i + 16) % 32 for i in range(32)]
SCALE = 1.0 / (HD + R) ** 0.5

C_ID, C_COS, C_SIN, C_K4 = 0, 128, 256, 384
C_TRI, C_THR, C_IOTA, C_BLK, C_UP = 512, 768, 784, 800, 800 + NB
C_J = C_UP + 128
C_B = C_J + HD0
C_TOK = C_B + B
NCF = C_TOK + NT


def flamingo_kernel(nc, x, ctxd, segT, gates, ssm, ssmD, WrT, rbias, Wg, Wu, Wd, sWg, sWu, sWd,
                    Wkvc, Wdq, WuqT, Wqr, WukT, Wkr, WuvT, Wo, w1T, w3T, w2T, constf, out):
    f32, bf16, i32, u32 = mybir.dt.float32, mybir.dt.bfloat16, mybir.dt.int32, mybir.dt.uint32
    ALU = mybir.AluOpType
    ACT = mybir.ActivationFunctionType
    AX = mybir.AxisListType.X

    def pair(i):
        return i * (i + 1) // 2

    ctx = ExitStack()
    with ctx:
        def sb(name, shape, dt=f32):
            return ctx.enter_context(nc.sbuf_tensor(name, shape, dt))

        def sem(name):
            return ctx.enter_context(nc.semaphore(name))

        cf = sb("cf", [128, NCF])
        cb = sb("cb", [128, 384], bf16)
        ident, cosT, sinT = cf[:, C_ID:C_ID + 128], cf[:, C_COS:C_COS + 128], cf[:, C_SIN:C_SIN + 128]
        identb, trib, placeb = cb[:, 0:128], cb[:, 128:256], cb[:, 256:384]
        onesb = sb("onesb", [128, 128], bf16)
        onesf = sb("onesf", [128, 128])
        X = sb("X", [128, NT, D])
        XN = sb("XN", [128, NT, D])
        CT = sb("CT", [128, DK, NT, 128])
        QT = sb("QT", [128, DK, NT, 128])
        WE = sb("WE", [128, (DK * E * 2 * I) + E * D])
        WGU = WE[:, 0:DK * E * 2 * I].rearrange("p (k e c) -> p k e c", k=DK, e=E)
        WD = WE[:, DK * E * 2 * I:].rearrange("p (e d) -> p e d", e=E)
        sWgu = sb("sWgu", [128, DK, 2, I])
        sWdn = sb("sWdn", [128, D])
        Wr = sb("Wr", [128, DK, E])
        rb = sb("rb", [128, E])
        gt = sb("gt", [128, 4])
        tg = sb("tg", [128, 4])
        WN = sb("WN", [QC, H // 2, 2, KVC])
        WRA = WE[0:QC, 9216:10240].rearrange("p (m a c) -> p m a c", m=H // 2, a=2)
        R2 = sb("R2", [128, 1536])
        CW = sb("CW", [128, H // 2, D])
        Wk2 = sb("Wk2", [128, DK, 2, KVC])
        Wkrs = sb("Wkrs", [KVC, R])
        Wdqs = sb("Wdqs", [128, DK, QC])
        st = sb("st", [128, NT, 6])
        mv = sb("mv", [128, NT, 2])
        rstd = sb("rstd", [128, NT])
        shift = sb("shift", [128, NT])
        mhalf = sb("mhalf", [128, NT])
        tok = sb("tok", [128, NB], i32)
        zk = sb("zk", [NH0, 384])
        dsb = sb("dsb", [NH0, 1])
        small = sb("small", [128, 64])
        small2 = sb("small2", [128, 128])
        wc = sb("wc", [128, 2, NT])
        slot = sb("slot", [128, 2, NT], i32)
        slotB = sb("slotB", [128, 2, B], i32)
        wcB = sb("wcB", [128, 2, B])
        eid = sb("eid", [128, NB], i32)
        segi = sb("segi", [128, B], i32)
        segf = sb("segf", [128, B])

        AR = sb("AR", [128, 15872])

        def ar(lo, n):
            return AR[:, lo:lo + n]

        T = ar(0, 4096).rearrange("p (h l) -> p h l", h=NH0)
        kv = ar(8192, 2 * DK * NPAIR * B).rearrange("p (u k n) -> p u k n", u=2, k=DK)
        o = 8192 + 2 * DK * NPAIR * B
        prod = ar(o, 2 * DK * 64 * B).rearrange("p (u k n) -> p u k n", u=2, k=DK)
        K01 = ar(0, 2048).rearrange("p (b s) -> p b s", b=B)
        K10 = ar(2048, 2048).rearrange("p (b s) -> p b s", b=B)
        KVr = ar(4096, 1024).rearrange("p (b c) -> p b c", b=B)
        maskb = ar(5120, 1024).bitcast(bf16).rearrange("p (b k) -> p b k", b=B)
        RT = ar(6144, 2048)
        SG = 8192
        uqT = ar(SG, H * QC).rearrange("p (h c) -> p h c", h=H)
        ukT = ar(SG + 1536, H * KVC).rearrange("p (h c) -> p h c", h=H)
        uvT = ar(SG + 2560, H * KVC).rearrange("p (h c) -> p h c", h=H)
        wo = ar(SG + 3584, H * D).rearrange("p (h d) -> p h d", h=H)
        XNf = XN[:, :, :].rearrange("p t d -> p (t d)")
        xg = XNf[:, 0:1024].rearrange("p (u d) -> p u d", u=4)
        xgT = XNf[:, 1024:1536].rearrange("p (u k t) -> p u k t", u=2, k=DK)
        sg = XNf[:, 1536:1792].rearrange("p (u d) -> p u d", u=2)
        hh = XNf[:, 1792:2048].rearrange("p (u d) -> p u d", u=2)
        hT = XNf[:, 2048:2304].rearrange("p (u d) -> p u d", u=2)
        yb = XNf[:, 2304:3328].rearrange("p (u d) -> p u d", u=4)
        gb = RT.rearrange("p (u s d) -> p u s d", u=4, s=2)
        place = ar(0, 2048).bitcast(bf16).rearrange("p (v t n) -> p v t n", v=2, t=NT)
        shs = ar(2048, 2048).rearrange("p (u n) -> p u n", u=4)
        shu = ar(4096, 1024).rearrange("p (u n) -> p u n", u=2)
        CWf = CW[:, :, :].rearrange("p m d -> p (m d)")
        blkid = CWf[:, 0:16 * NB].bitcast(mybir.dt.float16).rearrange("p (v t n) -> p v t n", v=2, t=NT)
        blk1 = RT[:, 1024:1024 + 16 * NB].bitcast(bf16).rearrange("p (v t n) -> p v t n", v=2, t=NT)
        slf = R2[:, 288:320].rearrange("p (v t) -> p v t", v=2)
        posf = small2[:, 0:32].rearrange("p (v t) -> p v t", v=2)
        blkf = small2[:, 32:64].rearrange("p (v t) -> p v t", v=2)
        SP4 = R2[:, 1024:1536].rearrange("p (v n) -> p v n", v=4)
        Q = WE[:, 0:2048].rearrange("p (u h n) -> p u h n", u=2, h=2)
        P = WE[:, 2048:4096].rearrange("p (u i k) -> p u i k", u=2, i=8)
        PT = WE[:, 4096:6144].rearrange("p (u i k) -> p u i k", u=2, i=8)
        ra = WE[:, 6144:7168].rearrange("p (u n) -> p u n", u=2)
        rbm = WE[:, 7168:8192].rearrange("p (u n) -> p u n", u=2)
        CTf = CT[:, :, :, :].rearrange("p k t n -> p (k t n)")
        QTf = QT[:, :, :, :].rearrange("p k t n -> p (k t n)")
        OT = [v.rearrange("p (m b q) -> p m b q", m=H // 2, b=4) for v in (CTf, QTf)]
        xb = XNf[:, 0:1024].rearrange("p (b d) -> p b d", b=4)
        xbT = XNf[:, 1024:2048].rearrange("p (k n) -> p k n", k=DK)
        qc = [XNf[0:QC, 2048 + 512 * i:2560 + 512 * i] for i in range(2)]
        w1f = ar(SG, DK * HID).rearrange("p (k n) -> p k n", k=DK)
        w3f = ar(SG + DK * HID, DK * HID).rearrange("p (k n) -> p k n", k=DK)
        w2f = ar(SG + 2 * DK * HID, NC * D).rearrange("p (c d) -> p c d", c=NC)
        o = SG + 2 * DK * HID + NC * D
        w1q = ar(o, HID).bitcast(bf16).rearrange("p (k n) -> p k n", k=DK)
        w3q = ar(o + HID, HID).bitcast(bf16).rearrange("p (k n) -> p k n", k=DK)
        w2q = ar(o + 2 * HID, NC * D // 2).bitcast(bf16).rearrange("p (c d) -> p c d", c=NC)
        f16 = mybir.dt.float16
        wlast = RT[:, 1536:1536 + DK * 64].bitcast(bf16).rearrange("p (k n) -> p k n", k=DK)
        gs = [[WE[:, 4608 * i + 1536 * j:4608 * i + 1536 * (j + 1)].bitcast(f16).rearrange("p (c n) -> p c n", c=NC)
               for j in range(2)] for i in range(2)]
        sl = WE[:, 9216:10240].rearrange("p (u n) -> p u n", u=2)
        gg = WE[:, 10240:11264].rearrange("p (u n) -> p u n", u=2)
        x3n = XNf[:, 3072:4096].rearrange("p (b d) -> p b d", b=4)
        xp = [[XNf[:, 1024 * i + 512 * j:1024 * i + 512 * (j + 1)].bitcast(f16).rearrange("p (k n) -> p k n", k=DK)
               for j in range(2)] for i in range(2)]
        wtmp = RT[:, 0:1536]
        rs = R2[:, 0:16].rearrange("p (u i) -> p u i", u=2)
        nm = R2[:, 16:32].rearrange("p (u i) -> p u i", u=2)
        mx = R2[:, 32:48].rearrange("p (u i) -> p u i", u=2)
        ri = R2[:, 48:64].rearrange("p (u i) -> p u i", u=2)

        PSt = ctx.enter_context(nc.psum_tensor("PS", [128, 8, 512], f32))

        def bank(k, n=1):
            return PSt[:, k, :] if n == 1 else PSt[:, k:k + n, :]

        Xn = nc.dram_tensor("Xn", [NT * 128, D], f32, kind="Internal").ap()
        YG = nc.dram_tensor("YG", [NB * 128, D], f32, kind="Internal").ap()
        Z = nc.dram_tensor("Z", [NH0, 384], f32, kind="Internal").ap()
        Xm = nc.dram_tensor("Xm", [B, S, D], f32, kind="Internal").ap()

        class Signals:
            pass

        s = Signals()
        s.ctx0 = sem("ctx0")
        s.ctx1 = sem("ctx1")
        s.ctx2 = sem("ctx2")
        s.ctx3 = sem("ctx3")
        s.x0 = sem("x0")
        s.x1 = sem("x1")
        s.x2 = sem("x2")
        s.x3 = sem("x3")
        s.yg0 = sem("yg0")
        s.yg1 = sem("yg1")
        s.yg2 = sem("yg2")
        s.yg3 = sem("yg3")
        s.ssm = sem("ssm")
        s.zk_set = sem("zk_set")
        s.ident_in = sem("ident_in")
        s.zk_d = sem("zk_d")
        s.zk_out = sem("zk_out")
        s.const = sem("const")
        s.shared_w = sem("shared_w")
        s.moe_w = sem("moe_w")
        s.ab_w = sem("ab_w")
        s.seg = sem("seg")
        s.xn2 = sem("xn2")
        s.xn_out = sem("xn_out")
        s.out_ready = sem("out_ready")
        s.sh_res = sem("sh_res")
        s.xm_out = sem("xm_out")
        s.xg_xp = sem("xg_xp")
        s.xin = sem("xin")
        s.y_blk = sem("y_blk")
        s.qr_w = sem("qr_w")
        s.res2 = sem("res2")
        s.w_ffn = sem("w_ffn")
        s.w_abs = sem("w_abs")
        s.yout = sem("yout")
        s.out_dma = sem("out_dma")
        s.small = sem("small")
        s.rstd1 = sem("rstd1")
        s.xn1 = sem("xn1")
        s.x_xp = sem("x_xp")
        s.x_T = sem("x_T")
        s.tg_ready = sem("tg_ready")
        s.sh_up = sem("sh_up")
        s.sh_h = sem("sh_h")
        s.sh_copied = sem("sh_copied")
        s.rstd2 = sem("rstd2")
        s.res1 = sem("res1")
        s.xn2_T = sem("xn2_T")
        s.xn2_xp = sem("xn2_xp")
        s.max_sub = sem("max_sub")
        s.exp_r = sem("exp_r")
        s.gu_ready = sem("gu_ready")
        s.xg_T = sem("xg_T")
        s.h_ready = sem("h_ready")
        s.silu = sem("silu")
        s.y_sb = sem("y_sb")
        s.xn3_xp = sem("xn3_xp")
        s.xn3_T = sem("xn3_T")
        s.qc_ready = sem("qc_ready")
        s.qc_sb = sem("qc_sb")
        s.proj_n = sem("proj_n")
        s.s_ready = sem("s_ready")
        s.q_n = sem("q_n")
        s.kc_ready = sem("kc_ready")
        s.kc_sb = sem("kc_sb")
        s.ab_ready = sem("ab_ready")
        s.ab_sb = sem("ab_sb")
        s.cw_ready = sem("cw_ready")
        s.cw_sb = sem("cw_sb")
        s.kt_ready = sem("kt_ready")
        s.kt_sb = sem("kt_sb")
        s.xn4_xp = sem("xn4_xp")
        s.up_ready = sem("up_ready")
        s.split_hi = sem("split_hi")
        s.p_xp = sem("p_xp")
        s.pv_ready = sem("pv_ready")
        s.pt_sb = sem("pt_sb")
        s.max_ready = sem("max_ready")
        s.exp_done = sem("exp_done")
        s.op_ready = sem("op_ready")
        s.ot_ready = sem("ot_ready")
        s.abs_sum = sem("abs_sum")
        s.g_ready = sem("g_ready")
        s.up_silu = sem("up_silu")
        s.dn_ready = sem("dn_ready")
        s.g_hi = sem("g_hi")
        s.kv_first = sem("kv_first")
        s.kv_ready = sem("kv_ready")
        s.prod_raw = sem("prod_raw")
        s.y_ready = sem("y_ready")
        s.prod_ready = sem("prod_ready")
        s.prod_pool = sem("prod_pool")
        s.sh_dn = sem("sh_dn")
        s.lg_ready = sem("lg_ready")
        s.onehot = sem("onehot")
        s.counts = sem("counts")
        s.lg_sb = sem("lg_sb")
        s.places = sem("places")
        s.blocks2 = sem("blocks2")
        s.tok_ps = sem("tok_ps")
        s.spread = sem("spread")
        s.cnt_read = sem("cnt_read")
        s.spread_ps = sem("spread_ps")
        s.slots = sem("slots")
        s.h_T = sem("h_T")
        s.h_xp = sem("h_xp")
        s.slotsB = sem("slotsB")
        s.res3 = sem("res3")
        s.xn3 = sem("xn3")
        s.rope_read = sem("rope_read")
        s.proj = sem("proj")
        s.q_r = sem("q_r")
        s.p_norm = sem("p_norm")
        s.kr_mul = sem("kr_mul")
        s.kr_ready = sem("kr_ready")
        s.xn4 = sem("xn4")
        s.split_lo = sem("split_lo")
        s.g_lo = sem("g_lo")
        s.mask = sem("mask")
        s.kr_sb = sem("kr_sb")
        s.scale_sb = sem("scale_sb")
        s.ternary = sem("ternary")
        s.scale_r = sem("scale_r")
        s.w_last = sem("w_last")
        s.memsets = sem("memsets")
        s.pool = sem("pool")
        s.ln1_stats = sem("ln1_stats")
        s.ln2_stats = sem("ln2_stats")
        s.blocks = sem("blocks")
        s.pos = sem("pos")
        s.tokens = sem("tokens")
        s.ln3_stats = sem("ln3_stats")
        s.rstd3 = sem("rstd3")
        s.d_stats = sem("d_stats")
        s.rstd4 = sem("rstd4")
        s.rope_mul = sem("rope_mul")
        s.dve = sem("dve")
        xg_in = [sem(f"xg_in{i}") for i in range(4)]
        toep = [sem(f"toep{i}") for i in range(4)]
        gat = [sem(f"gat{i}") for i in range(4)]
        ctx_in = [s.ctx0, s.ctx1, s.ctx2, s.ctx3]
        x_in = [s.x0, s.x1, s.x2, s.x3]
        yg_out = [s.yg0, s.yg1, s.yg2, s.yg3]
        block = ctx.enter_context(nc.Block())

        @block.sync
        def _(sp):
            def rows_in(c):
                sp.dma_start(X[:, 4 * c:4 * c + 4, :], x[:, 4 * c:4 * c + 4, :]).then_inc(x_in[c], 16)

            def context_in(c):
                sp.dma_start(CT[:, :, 4 * c:4 * c + 4, :], ctxd[:, :, 4 * c:4 * c + 4, :]).then_inc(ctx_in[c], 16)

            def toeplitz_in(c):
                src = bass.AP(Z.tensor, 384 * 4 * c, [[1, 128], [384, 4], [1, 256]])
                sp.dma_start(T[:, 4 * c:4 * c + 4, :], src).then_inc(toep[c], 16)

            sp.dma_start(dsb[:, :], ssmD.unsqueeze(1)).then_inc(s.ssm, 16)
            sp.wait_ge(s.zk_set, 1)
            sp.dma_start(zk[:, 127:383], ssm).then_inc(s.ssm, 16)
            rows_in(0)
            sp.dma_start(ident, constf[:, C_ID:C_ID + 128]).then_inc(s.ident_in, 16)
            sp.wait_ge(s.zk_d, 1)
            sp.dma_start(Z, zk[:, :]).then_inc(s.zk_out, 16)
            rows_in(1)
            sp.wait_ge(s.zk_out, 16)
            toeplitz_in(0)
            rows_in(2)
            rows_in(3)
            context_in(1)
            toeplitz_in(1)
            context_in(2)
            sp.dma_start(cf[:, C_ID + 128:], constf[:, C_ID + 128:]).then_inc(s.const, 16)
            toeplitz_in(2)
            context_in(3)
            toeplitz_in(3)
            for dst, src in ((rb[:, :], rbias.unsqueeze(0).to_broadcast([128, E])),
                             (Wr[:, :, :], WrT.rearrange("(k p) e -> p k e", p=128)),
                             (sWgu[:, :, 0, :], sWg.rearrange("(k p) c -> p k c", p=128)),
                             (sWgu[:, :, 1, :], sWu.rearrange("(k p) c -> p k c", p=128)),
                             (sWdn[:, :], sWd)):
                sp.dma_start(dst, src).then_inc(s.shared_w, 16)
            for k in range(DK):
                for c, w in ((0, Wg), (1, Wu)):
                    sp.dma_start(WGU[:, k, :, c * I:(c + 1) * I],
                                 w.rearrange("e (k p) c -> k p e c", p=128)[k]).then_inc(s.moe_w, 16)
            sp.dma_start(WD, Wd.rearrange("e p d -> p e d")).then_inc(s.moe_w, 16)
            for a in range(2):
                sp.dma_start(Wk2[:, :, a, :], Wkvc.rearrange("(k p) c -> p k c", p=128)).then_inc(s.ab_w, 16)
            sp.dma_start(Wkrs[:, :], Wkr).then_inc(s.ab_w, 16)
            sp.dma_start(Wdqs[:, :, :], Wdq.rearrange("(k p) c -> p k c", p=128)).then_inc(s.ab_w, 16)
            sp.dma_start(segi[:, :], segT).then_inc(s.seg, 16)
            for t in range(NT):
                sp.wait_ge(s.xn2, t + 1)
                sp.dma_start(Xn[t * 128:(t + 1) * 128, :], XN[:, t, :]).then_inc(s.xn_out, 16)
            sp.wait_ge(s.out_ready, NT)
            for dst, src in ((uqT, WuqT), (ukT, WukT), (uvT, WuvT), (wo, Wo)):
                sp.dma_start(dst, src.rearrange("(h p) c -> p h c", p=128)).then_inc(s.ab_w, 16)
            for c in range(4):
                sp.wait_ge(s.sh_res, c + 1)
                for j in range(HD0):
                    dst = Xm.rearrange("b (h j) d -> j b h d", j=HD0)[j]
                    sp.dma_start(dst[:, 4 * c:4 * c + 4, :], X[j * B:(j + 1) * B, 4 * c:4 * c + 4, :]).then_inc(s.xm_out, 16)
            sp.wait_ge(s.xm_out, 4 * HD0 * 16)
            for c in range(8):
                sp.wait_ge(s.xg_xp, 12 + 3 * c)
                sp.dma_start(X[:, 2 * c:2 * c + 2, :], Xm[2 * c:2 * c + 2].rearrange("b s d -> s b d")).then_inc(s.xin, 16)
            sp.wait_ge(s.y_blk, NB)
            sp.dma_start(WRA, Wqr).then_inc(s.qr_w, 16)
            sp.wait_ge(s.res2, B)
            sp.dma_start(w1f, w1T.rearrange("(k p) n -> p k n", p=128)).then_inc(s.w_ffn, 16)
            sp.dma_start(w3f, w3T.rearrange("(k p) n -> p k n", p=128)).then_inc(s.w_ffn, 16)
            sp.wait_ge(s.w_abs, 1)
            sp.dma_start(w2f[:, 0:NC - 1, :], w2T[0:(NC - 1) * 128, :].rearrange("(c p) d -> p c d", p=128)).then_inc(s.w_ffn, 16)
            sp.dma_start(w2f[0:HID - (NC - 1) * 128, NC - 1, :], w2T[(NC - 1) * 128:HID, :]).then_inc(s.w_ffn, 16)
            for b in range(B):
                sp.wait_ge(s.yout, b + 1)
                sp.dma_start(out[b], X[:, b, :]).then_inc(s.out_dma, 16)
            sp.wait_ge(s.out_dma, B * 16)

        @block.scalar
        def _(act):
            act.dma_start(CT[:, :, 0:4, :], ctxd[:, :, 0:4, :]).then_inc(ctx_in[0], 16)
            act.dma_start(gt[:, :], gates.unsqueeze(0).to_broadcast([128, 4])).then_inc(s.small, 16)

            def normalise(t, signal):
                nc.scalar.activation(XN[:, t, :], X[:, t, :], ACT.Identity, bias=shift[:, t:t + 1],
                                     scale=rstd[:, t:t + 1]).then_inc(signal, 1)

            for c in range(5):
                if c < 4:
                    act.wait_ge(s.rstd1, 4 * c + 4)
                    for t in range(4 * c, 4 * c + 4):
                        normalise(t, s.xn1)
                if c >= 1:
                    for u in (2 * c - 2, 2 * c - 1):
                        act.wait_ge(s.x_xp, u + 1)
                        nc.scalar.activation(QT[:, :, 2 * u:2 * u + 2, :].rearrange("p k t n -> p t k n"),
                                             bank(6 + u % 2).rearrange("p (t k n) -> p t k n", t=2, k=DK), ACT.Copy).then_inc(s.x_T, 1)
            act.wait_ge(s.small, 16)
            nc.scalar.activation(tg[:, :], gt[:, :], ACT.Tanh).then_inc(s.tg_ready, 1)

            def shared_parts(g):
                act.wait_ge(s.sh_up, g + 1)
                nc.scalar.activation(shs[:, g, :], bank(2 * (g % 2)), ACT.Silu)
                if g >= 2:
                    act.wait_ge(s.sh_h, g - 1)
                nc.scalar.activation(shu[:, g % 2, :], bank(2 * (g % 2) + 1), ACT.Copy).then_inc(s.sh_copied, 1)

            for t in range(NT):
                act.wait_ge(s.rstd2, t + 1)
                normalise(t, s.xn2)
                if 2 <= t < NT - 2:
                    act.wait_ge(s.res1, t + 3)
                    nc.scalar.activation(QT[:, :, t - 2, :], bank(6 + t % 2)[:, 256:512].rearrange("p (k n) -> p k n", k=DK),
                                         ACT.Copy).then_inc(s.xn2_T, 1)
                if t == NT - 3:
                    shared_parts(0)
            for u in (6, 7):
                act.wait_ge(s.xn2_xp, u - 5)
                nc.scalar.activation(QT[:, :, 2 * u:2 * u + 2, :],
                                     bank(u - 1).rearrange("p (t k n) -> p k t n", t=2, k=DK), ACT.Copy).then_inc(s.xn2_T, 1)
            act.wait_ge(s.max_sub, 1)
            L = RT[:, 0:256]
            nc.scalar.activation(L, L, ACT.Exp).then_inc(s.exp_r, 1)
            for g in range(1, 4):
                shared_parts(g)
            for n in range(NB + 4):
                if n < NB:
                    act.wait_ge(s.xg_xp, n + 1)
                    if n >= 2:
                        act.wait_ge(s.gu_ready, n - 1)
                    nc.scalar.activation(xgT[:, n % 2, :, :], bank(n % 2)[:, 0:256].rearrange("p (k t) -> p k t", k=DK),
                                         ACT.Copy).then_inc(s.xg_T, 1)
                m = n - 1
                if 0 <= m < NB:
                    act.wait_ge(s.gu_ready, m + 1)
                    if m >= 2:
                        act.wait_ge(s.h_ready, m - 1)
                    nc.scalar.activation(sg[:, m % 2, :], bank(2 + m % 2)[:, 0:I], ACT.Silu).then_inc(s.silu, 1)
                m = n - 4
                if m >= 0:
                    act.wait_ge(s.y_sb, m + 1)
                    act.dma_start(YG[m * 128:(m + 1) * 128, :], yb[:, m % 4, :]).then_inc(yg_out[m % 4], 16)

            def latent(g, c):
                if c < 2:
                    act.wait_ge(s.xn3_xp, 2 * g + c + 1)
                    nc.scalar.activation(xbT[:, :, c * 256:(c + 1) * 256], bank(4).rearrange("p (k n) -> p k n", k=DK),
                                         ACT.Copy).then_inc(s.xn3_T, 1)
                else:
                    act.wait_ge(s.qc_ready, g + 1)
                    nc.scalar.activation(qc[g % 2], bank(4)[0:QC, :], ACT.Copy).then_inc(s.qc_sb, 1)

            def q_nope(u):
                act.wait_ge(s.proj_n, u + 1)
                if u >= 2:
                    act.wait_ge(s.s_ready, 2 * u - 2)
                nc.scalar.activation(Q[0:64, u % 2, 0, :], bank(2)[0:64, :], ACT.Copy)
                nc.scalar.activation(Q[64:128, u % 2, 1, :], bank(2)[64:128, :], ACT.Copy).then_inc(s.q_n, 1)

            for c in range(4):
                act.wait_ge(s.kc_ready, c + 1)
                for lo, dst in ((0, K01), (64, K10)):
                    for j4 in range(4):
                        h = 4 * c + j4
                        ins = nc.scalar.activation(
                            dst[lo:lo + 64, :, h * HD0:(h + 1) * HD0].rearrange("p b j -> p j b"),
                            bank(c % 2)[lo:lo + 64, j4 * 128:(j4 + 1) * 128].rearrange("p (j b) -> p j b", j=HD0), ACT.Copy)
                ins.then_inc(s.kc_sb, 1)
            for c in range(2):
                act.wait_ge(s.ab_ready, c + 1)
                nc.scalar.activation(WN[:, 4 * c:4 * c + 4, :, :], bank(4 + c)[0:QC, :].rearrange("p (m a c) -> p m a c", a=2, c=KVC),
                                     ACT.Copy).then_inc(s.ab_sb, 1)
            for c in range(4):
                act.wait_ge(s.cw_ready, c + 1)
                nc.scalar.activation(CW[:, 2 * c:2 * c + 2, :], bank(6 + c % 2).rearrange("p (m d) -> p m d", m=2),
                                     ACT.Copy).then_inc(s.cw_sb, 1)
            for c in range(2):
                act.wait_ge(s.kt_ready, c + 1)
                nc.scalar.activation(KVr[:, 8 * c:8 * c + 8, :], bank(6 + c).rearrange("p (b c) -> p b c", b=8), ACT.Copy).then_inc(s.kt_sb, 1)
            def split_rows(g, t):
                act.wait_ge(s.xn4_xp, 2 * g + t + 1)
                if g >= 2:
                    act.wait_ge(s.up_ready, NC * (g - 1))
                nc.scalar.activation(xp[g % 2][0][:, :, t * 256:(t + 1) * 256],
                                     bank(t if g else 4).rearrange("p (k n) -> p k n", k=DK), ACT.Copy).then_inc(s.split_hi, 1)

            for c in range(3):
                latent(0, c)
            q_nope(0)
            q_nope(1)
            for u in range(33):
                g, m = u // 8, u % 8
                if u >= 1:
                    act.wait_ge(s.p_xp, u)
                    if u >= 3:
                        act.wait_ge(s.pv_ready, u - 2)
                    nc.scalar.activation(PT[:, (u - 1) % 2], bank(5, 2).rearrange("p a (i q) -> p (a i) q", i=4), ACT.Copy).then_inc(s.pt_sb, 1)
                if u < 32:
                    if u >= 2:
                        act.wait_ge(s.p_xp, u - 1)
                    for a in range(2):
                        act.wait_ge(s.max_ready, 2 * u + a + 1)
                        for b in range(4):
                            i = 4 * a + b
                            ins = nc.scalar.activation(P[:, u % 2, i, :], bank(a)[:, b * 128:(b + 1) * 128], ACT.Exp,
                                                       bias=nm[:, u % 2, i:i + 1], scale=SCALE, accum_out=rs[:, u % 2, i:i + 1])
                        ins.then_inc(s.exp_done, 1)
                if u + 2 < 32:
                    q_nope(u + 2)
                if u >= 1:
                    act.wait_ge(s.pv_ready, u)
                    if u - 1 >= 16:
                        act.wait_ge(s.op_ready, 8 * ((u - 1) // 8 - 1))
                    nc.scalar.activation(OT[(u - 1) // 8 % 2][:, (u - 1) % 8, :, :], bank(7).rearrange("p (b q) -> p b q", b=4),
                                         ACT.Copy).then_inc(s.ot_ready, 1)
                if g < 3 and m in (2, 4, 5):
                    latent(g + 1, (2, 4, 5).index(m))
                if u in FFN_ROWS:
                    split_rows(0, FFN_ROWS.index(u))
                if 21 <= u < 24:
                    i, w = u - 21, (w1f, w3f, w2f)[u - 21]
                    act.wait_ge(s.w_ffn, 64)
                    w = w.rearrange("p k n -> p (k n)")
                    nc.scalar.activation(wtmp[:, 0:w.shape[1]], w, ACT.Abs, accum_out=small[:, 32 + i:33 + i]).then_inc(s.abs_sum, 1)
                    act.wait_ge(s.abs_sum, i + 1)

            for n in range(4 * NC):
                g, c = n // NC, n % NC
                m = min(128, HID - c * 128)
                act.wait_ge(s.up_ready, n + 1)
                if n >= 2:
                    act.wait_ge(s.g_ready, n - 1)
                nc.scalar.activation(sl[0:m, n % 2, :], bank(2 + 2 * (n % 2))[0:m, :], ACT.Silu,
                                     scale=small[0:m, 40:41]).then_inc(s.up_silu, 1)
                act.wait_ge(s.g_ready, n + 1)
                if g >= 2 and c == 0:
                    act.wait_ge(s.dn_ready, 4 * (g - 1))
                nc.scalar.activation(gs[g % 2][0][0:m, c, :], gg[0:m, n % 2, :], ACT.Copy).then_inc(s.g_hi, 1)
                if c in (1, 2) and g < 3:
                    split_rows(g + 1, c - 1)

        @block.tensor
        def _(pe):
            mm = nc.tensor.matmul
            tr = nc.tensor.transpose
            pe.wait_ge(s.ident_in, 16)

            def transpose_rows(u):
                pe.wait_ge(s.xn1, 2 * u + 2)
                if u >= 2:
                    pe.wait_ge(s.x_T, u - 1)
                for t in range(2):
                    for k in range(DK):
                        ins = tr(bank(6 + u % 2)[:, (2 * t + k) * 128:(2 * t + k + 1) * 128],
                                 XN[:, 2 * u + t, k * 128:(k + 1) * 128], ident)
                ins.then_inc(s.x_xp, 1)

            def conv(h):
                if h == 0:
                    pe.wait_ge(s.kv_first, 1)
                else:
                    pe.wait_ge(s.kv_ready, h)
                if h % 4 == 0:
                    pe.wait_ge(toep[h // 4], 16)
                if h >= 2:
                    pe.wait_ge(s.prod_raw, h - 1)
                p = 3 * (h % 2)
                for lo, dst, n0, n in ((0, bank(p)[:, 0:PA * B], 0, PA * B), (0, bank(p + 2)[:, 0:PB * B], PA * B, PB * B),
                                       (1, bank(p + 1)[:, 0:PA * B], 0, PA * B),
                                       (1, bank(p + 2)[:, PB * B:2 * PB * B], PA * B, PB * B)):
                    for k in range(lo + 1):
                        ins = mm(dst, T[:, h, (lo - k) * 128:(lo - k + 1) * 128], kv[:, h % 2, k, n0:n0 + n],
                                 start=(k == 0), stop=(k == lo))
                ins.then_inc(s.y_ready, 1)

            def token_sum(t):
                pe.wait_ge(s.prod_ready, t + 1)
                pe.wait_ge(s.prod_pool, t + 1)
                if t == 0:
                    pe.wait_ge(s.x_T, NT // 2)
                if t >= 2:
                    pe.wait_ge(s.res1, t - 1)
                if t >= 6:
                    pe.wait_ge(s.xn2_T, t - 5)
                if t >= 4:
                    pe.wait_ge(s.xn2, t - 3)
                    for k in range(DK):
                        tr(bank(6 + t % 2)[:, 256 + k * 128:256 + (k + 1) * 128], XN[:, t - 4, k * 128:(k + 1) * 128], ident)
                for k in range(DK):
                    for i in range(4):
                        ins = mm(bank(6 + t % 2)[:, k * 128:(k + 1) * 128], prod[:, t % 2, k, i * 128:(i + 1) * 128], ident,
                                 start=(i == 0), stop=(i == 3))
                ins.then_inc(s.out_ready, 1)

            def shared_up(g):
                if g >= 2:
                    pe.wait_ge(s.sh_copied, g - 1)
                for c in range(2):
                    for k in range(DK):
                        ins = mm(bank(2 * (g % 2) + c), sWgu[:, k, c, :], QT[:, k, 4 * g:4 * g + 4, :].rearrange("p t n -> p (t n)"),
                                 start=(k == 0), stop=(k == DK - 1))
                ins.then_inc(s.sh_up, 1)

            for h in range(NT + 1):
                if h < NT:
                    conv(h)
                else:
                    pe.wait_ge(s.shared_w, 5 * 16)
                    pe.wait_ge(s.xn2_T, 4)
                    pe.wait_ge(s.prod_raw, NT - 1)
                    shared_up(0)
                for u in ((0, 1, 2, 3), (4, 5, 6, 7))[h] if h < 2 else ():
                    transpose_rows(u)
                if h >= 1:
                    token_sum(h - 1)

            def logits(lo, hi):
                for t in range(lo, hi):
                    for k in range(DK):
                        ins = mm(bank(4)[:, t * E:(t + 1) * E], QT[:, k, t, :], Wr[:, k, :], start=(k == 0), stop=(k == DK - 1))
                return ins

            def shared_down(g):
                pe.wait_ge(s.sh_h, g + 1)
                pe.wait_ge(s.sh_copied, (1, 3, 4, 4)[g])
                for t in range(4):
                    b4 = (4, 0, 2, 4)[g] + t // 2
                    ins = mm(bank(b4)[:, (t % 2) * 256:(t % 2 + 1) * 256], shs[:, g, t * 128:(t + 1) * 128], sWdn[:, :],
                             start=True, stop=True)
                ins.then_inc(s.sh_dn, 1)

            pe.wait_ge(s.prod_raw, NT)
            pe.wait_ge(s.xn2_T, NT - 8)
            logits(0, NT - 8)
            shared_up(1)
            for u in (6, 7):
                pe.wait_ge(s.xn2, 2 * u + 2)
                if u == 7:
                    pe.wait_ge(s.res1, NT - 1)
                for t in range(2):
                    for k in range(DK):
                        ins = tr(bank(u - 1)[:, (2 * t + k) * 128:(2 * t + k + 1) * 128], XN[:, 2 * u + t, k * 128:(k + 1) * 128], ident)
                ins.then_inc(s.xn2_xp, 1)
            pe.wait_ge(s.xn2_T, NT - 2)
            logits(NT - 8, NT).then_inc(s.lg_ready, 1)
            shared_up(2)
            Mb = RT[:, 768:904].bitcast(bf16)
            pe.wait_ge(s.onehot, 1)
            mm(bank(6)[:, 0:(NT + 1) * E], trib, Mb, start=True, stop=False)
            for t in range(NT):
                ins = mm(bank(6)[:, (t + 1) * E:(NT + 1) * E].rearrange("p (n e) -> p n e", e=E), onesb[:, :],
                         Mb[:, t * E:(t + 1) * E].unsqueeze(1).to_broadcast([128, NT - t, E]), start=False, stop=(t == NT - 1))
            ins.then_inc(s.counts, 1)
            shared_up(3)
            pe.wait_ge(s.lg_sb, 1)
            for g in range(3):
                shared_down(g)
            pe.wait_ge(s.res1, NT)
            for v in range(2):
                pe.wait_ge(s.places, v + 1)
                if v:
                    pe.wait_ge(s.blocks2, 1)
                for t in range(NT):
                    ins = mm(bank(7)[:, 0:NB], place[:, v, t, :], blkid[:, v, t, :],
                             start=(v == 0 and t == 0), stop=(v == 1 and t == NT - 1))
            ins.then_inc(s.tok_ps, 1)
            pe.wait_ge(s.sh_res, 1)
            shared_down(3)
            pe.wait_ge(s.spread, 1)
            pe.wait_ge(s.cnt_read, 1)
            for v in range(4):
                ins = mm(bank(6)[:, v * B:(v + 1) * B], SP4[:, v, :], cf[:, C_B:C_B + B], start=True, stop=True)
            ins.then_inc(s.spread_ps, 1)
            pe.wait_ge(s.moe_w, 5 * 16)
            pe.wait_ge(s.sh_res, 2)
            experts = {}
            for n in range(NB + 3):
                if n < NB:
                    pe.wait_ge(xg_in[n % 4], 16 * (n // 4 + 1))
                    if n >= 2:
                        pe.wait_ge(s.xg_T, n - 1)
                    for k in range(DK):
                        ins = tr(bank(n % 2)[:, k * 128:(k + 1) * 128], xg[:, n % 4, k * 128:(k + 1) * 128], ident)
                    ins.then_inc(s.xg_xp, 1)
                m = n - 1
                if m == 0:
                    pe.wait_ge(s.slots, 1)
                    pe.wait_ge(s.sh_res, 3)
                if 0 <= m < NB:
                    e = pe.value_load(eid[0:1, m:m + 1], min_val=0, max_val=E - 1)
                    experts[m] = e
                    pe.wait_ge(s.xg_T, m + 1)
                    if m >= 2:
                        pe.wait_ge(s.h_ready, m - 1)
                    for k in range(DK):
                        ins = mm(bank(2 + m % 2)[:, 0:2 * I], xgT[:, m % 2, k, :], WGU[:, k, bass.ds(e, 1), :].rearrange("p e c -> p (e c)"),
                                 start=(k == 0), stop=(k == DK - 1))
                    ins.then_inc(s.gu_ready, 1)
                m = n - 2
                if 0 <= m < NB:
                    pe.wait_ge(s.h_ready, m + 1)
                    if m == 0:
                        pe.wait_ge(s.sh_res, 4)
                    if m >= 2:
                        pe.wait_ge(s.h_T, m - 1)
                    tr(bank(4 + m % 2)[:, 0:I], hh[:, m % 2, :], ident).then_inc(s.h_xp, 1)
                m = n - 3
                if 0 <= m < NB:
                    pe.wait_ge(s.h_T, m + 1)
                    if m == 0:
                        pe.wait_ge(s.slotsB, 1)
                    if m >= 2:
                        pe.wait_ge(s.y_sb, m - 1)
                    mm(bank(6 + m % 2)[:, 0:D], hT[:, m % 2, :], WD[:, bass.ds(experts.pop(m), 1), :].rearrange("p e d -> p (e d)"),
                       start=True, stop=True).then_inc(s.y_blk, 1)

            LATENT = (2, 4, 5)

            def latent(g, c):
                if g >= 2:
                    pe.wait_ge(s.res3, 8 * (g - 1) + LATENT[c] - 8)
                elif g == 1 and c == 0:
                    pe.wait_ge(s.qc_sb, 1)
                if c < 2:
                    pe.wait_ge(s.xn3, 4 * g + 2 * c + 2)
                    if c:
                        pe.wait_ge(s.xn3_T, 2 * g + c)
                    elif g:
                        pe.wait_ge(s.qc_ready, g)
                    for b in range(2):
                        for k in range(DK):
                            ins = tr(bank(4)[:, k * 256 + b * 128:k * 256 + (b + 1) * 128], xb[:, 2 * c + b, k * 128:(k + 1) * 128], ident)
                    ins.then_inc(s.xn3_xp, 1)
                else:
                    pe.wait_ge(s.xn3_T, 2 * g + 2)
                    for k in range(DK):
                        ins = mm(bank(4)[0:QC, :], Wdqs[:, k, :], xbT[:, k, :], start=(k == 0), stop=(k == DK - 1))
                    ins.then_inc(s.qc_ready, 1)

            def project(u):
                g, m = u // 8, u % 8
                if m == 0:
                    pe.wait_ge(s.qc_sb, g + 1)
                if u:
                    pe.wait_ge(s.q_n, u)
                mm(bank(2), WN[:, m, :, :].rearrange("p a c -> p (a c)"), qc[g % 2], start=True, stop=True).then_inc(s.proj_n, 1)
                if u:
                    pe.wait_ge(s.rope_read, u)
                mm(bank(3), WRA[:, m, :, :].rearrange("p a c -> p (a c)"), qc[g % 2], start=True, stop=True).then_inc(s.proj, 1)

            def scores(u):
                g = u // 8
                pe.wait_ge(s.q_n, u + 1)
                for a, keys in enumerate((K01, K10)):
                    pe.wait_ge(s.q_r, 2 * u + a + 1)
                    if u >= 1:
                        pe.wait_ge(s.exp_done, 2 * u - 1 + a)
                    mm(bank(a), identb, maskb[:, 4 * g:4 * g + 4, :].rearrange("p b k -> p (b k)"), start=True, stop=False)
                    for b in range(4):
                        ins = mm(bank(a)[:, b * 128:(b + 1) * 128], Q[:, u % 2, a, b * 128:(b + 1) * 128], keys[:, 4 * g + b, :],
                                 start=False, stop=(b == 3))
                    ins.then_inc(s.s_ready, 1)

            def transpose_probs(u):
                pe.wait_ge(s.p_norm, u + 1)
                if u == 0:
                    pe.wait_ge(s.kr_mul, 2)
                if u >= 1:
                    pe.wait_ge(s.pt_sb, u)
                for i in range(8):
                    ins = tr(bank(5 + i // 4)[:, (i % 4) * 128:(i % 4 + 1) * 128], P[:, u % 2, i, :], ident)
                ins.then_inc(s.p_xp, 1)

            def attend(u):
                g = u // 8
                pe.wait_ge(s.pt_sb, u + 1)
                if u >= 1:
                    pe.wait_ge(s.ot_ready, u)
                for b in range(4):
                    for a in range(2):
                        ins = mm(bank(7)[64 * a:64 * a + 64, b * 128:(b + 1) * 128], KVr[:, 4 * g + b, :], PT[:, u % 2, 4 * a + b, :],
                                 start=True, stop=True)
                ins.then_inc(s.pv_ready, 1)

            def out_piece(i, b3):
                g, b, half = i // 8, i % 8 // 2, i % 2
                pe.wait_ge(s.ot_ready, 8 * (g + 1))
                for m in range(H // 2):
                    ins = mm(bank(b3)[:, 0:128], OT[g % 2][:, m, b, :], CW[:, m, half * 128:(half + 1) * 128],
                             start=(m == 0), stop=(m == H // 2 - 1))
                ins.then_inc(s.op_ready, 1)

            pe.wait_ge(s.y_sb, NB)
            pe.wait_ge(s.ab_w, 8 * 16)
            for c in range(4):
                if c >= 2:
                    pe.wait_ge(s.kc_sb, c - 1)
                for k in range(DK):
                    ins = mm(bank(c % 2), Wk2[:, k, :, :].rearrange("p a c -> p (a c)"),
                             CT[:, k, 4 * c:4 * c + 4, :].rearrange("p t n -> p (t n)"), start=(k == 0), stop=(k == DK - 1))
                ins.then_inc(s.kc_ready, 1)
            for c in range(2):
                for i in range(8):
                    h = 8 * c + i
                    ins = mm(bank(4 + c)[0:QC, i * KVC:(i + 1) * KVC], uqT[:, h, :], ukT[:, h, :], start=True, stop=True)
                ins.then_inc(s.ab_ready, 1)
            for c in range(4):
                if c >= 2:
                    pe.wait_ge(s.cw_sb, c - 1)
                for i in range(4):
                    h = 4 * c + i
                    lo = 64 * (h % 2)
                    ins = mm(bank(6 + c % 2)[lo:lo + 64, (i // 2) * 256:(i // 2 + 1) * 256], uvT[:, h, :], wo[:, h, :],
                             start=True, stop=True)
                ins.then_inc(s.cw_ready, 1)
            pe.wait_ge(s.kc_sb, 4)
            pe.wait_ge(s.cw_sb, 4)
            for c in range(2):
                for i in range(8):
                    ins = tr(bank(6 + c)[:, i * 64:(i + 1) * 64], K01[0:64, 8 * c + i, :], ident[0:64, 0:64])
                ins.then_inc(s.kt_ready, 1)

            def keys_rope(c):
                for half in range(2):
                    b = 8 * c + 4 * half
                    ins = mm(bank((0, 5)[c])[64 * half:64 * half + 64, :], Wkrs[:, :], K01[0:64, b:b + 4, :].rearrange("p b s -> p (b s)"),
                             start=True, stop=True)
                ins.then_inc(s.kr_ready, 1)

            def rows(g, t):
                pe.wait_ge(s.xn4, 4 * g + 2 * t + 2)
                if g >= 2:
                    pe.wait_ge(s.split_lo, 2 * (g - 1) + t + 1)
                for b in range(2):
                    for k in range(DK):
                        ins = tr(bank(t if g else 4)[:, k * 256 + b * 128:k * 256 + (b + 1) * 128], x3n[:, 2 * t + b, k * 128:(k + 1) * 128], ident)
                ins.then_inc(s.xn4_xp, 1)

            def up(n):
                g, c = n // NC, n % NC
                m = min(128, HID - c * 128)
                if n >= 2:
                    pe.wait_ge(s.g_ready, n - 1)
                if c == NC - 1:
                    for k in range(DK):
                        for q in range(2):
                            ins = mm(bank(2 + 2 * (n % 2))[0:64 + LAST, :], wlast[:, k, 0:64 + LAST], xp[g % 2][q][:, k, :],
                                     start=(k == 0 and q == 0), stop=(k == DK - 1 and q == 1))
                    ins.then_inc(s.up_ready, 1)
                    return
                for z, w in enumerate((w1q, w3q)):
                    for k in range(DK):
                        for q in range(2):
                            ins = mm(bank(2 + 2 * (n % 2) + z)[0:m, :], w[:, k, c * 128:c * 128 + m], xp[g % 2][q][:, k, :],
                                     start=(k == 0 and q == 0), stop=(k == DK - 1 and q == 1))
                ins.then_inc(s.up_ready, 1)

            def down(g, b):
                pe.wait_ge(s.g_lo, NC * (g + 1))
                if g == 0 and b < 2:
                    pe.wait_ge(s.res3, 31 + b)
                else:
                    pe.wait_ge(s.yout, 4 * g + b - 1)
                for c in range(NC):
                    m = min(128, HID - c * 128)
                    for q, part in enumerate(gs[g % 2]):
                        ins = mm(bank(6 + b % 2)[:, 0:D], part[0:m, c, b * 128:(b + 1) * 128], w2q[0:m, c, :],
                                 start=(c == 0 and q == 0), stop=(c == NC - 1 and q == 1))
                ins.then_inc(s.dn_ready, 1)

            keys_rope(0)
            pe.wait_ge(s.ab_sb, 2)
            keys_rope(1)
            for c in range(3):
                latent(0, c)
            pe.wait_ge(s.qr_w, 16)
            project(0)
            project(1)
            pe.wait_ge(s.mask, 4)
            pe.wait_ge(s.kr_sb, 1)
            pe.wait_ge(s.kt_sb, 2)
            for u in range(33):
                g, m = u // 8, u % 8
                if u == 16:
                    pe.wait_ge(s.kr_sb, 2)
                if u < 32:
                    scores(u)
                if 1 <= u < 32:
                    transpose_probs(u - 1)
                if u >= 9:
                    v = u - 1
                    if v // 8 < 3 and v % 8 in LATENT[0:2]:
                        pe.wait_ge(s.xn3_T, 2 * (v // 8 + 1) + LATENT.index(v % 8) + 1)
                    elif v // 8 < 3 and v % 8 == LATENT[2]:
                        pe.wait_ge(s.qc_sb, v // 8 + 2)
                    elif v == FFN_SCALE:
                        pe.wait_ge(s.scale_sb, 1)
                    elif v in FFN_ROWS:
                        pe.wait_ge(s.split_lo, FFN_ROWS.index(v) + 1)
                    elif v >= 9:
                        pe.wait_ge(s.res3, u - 9)
                    out_piece(u - 9, 4)
                if u == 32:
                    pe.wait_ge(s.ternary, 3)
                    up(0)
                    transpose_probs(31)
                if u + 2 < 32:
                    project(u + 2)
                if u >= 1:
                    attend(u - 1)
                if g < 3 and m in LATENT:
                    latent(g + 1, LATENT.index(m))
                if u in FFN_ROWS:
                    pe.wait_ge(s.res3, u - 8)
                    rows(0, FFN_ROWS.index(u))
                if u == FFN_SCALE:
                    pe.wait_ge(s.abs_sum, 3)
                    pe.wait_ge(s.res3, u - 8)
                    mm(bank(4)[:, 0:3], onesf[:, :], small[:, 32:35], start=True, stop=True).then_inc(s.scale_r, 1)

            for n in range(4 * NC):
                g, c = n // NC, n % NC
                if n == 1:
                    pe.wait_ge(s.res3, 24)
                if c == 0 and g:
                    pe.wait_ge(s.split_lo, 2 * g + 2)
                if n == NC - 1:
                    pe.wait_ge(s.w_last, 1)
                if n:
                    up(n)
                if n < 4:
                    for i in (24 + 2 * n, 25 + 2 * n):
                        if n:
                            pe.wait_ge(s.res3, i - 1)
                        out_piece(i, 6 + i % 2)
                if g and 1 <= c < 5:
                    down(g - 1, c - 1)
                if c in (1, 2) and g < 3:
                    rows(g + 1, c - 1)
            for c in range(NC):
                pe.wait_ge(s.g_lo, 3 * NC + c + 1)
                m = min(128, HID - c * 128)
                for b in range(4):
                    if c == 0 and b >= 2:
                        pe.wait_ge(s.yout, 8 + b + 1)
                    for q, part in enumerate(gs[1]):
                        ins = mm(bank((0, 1, 6, 7)[b])[:, 0:D], part[0:m, c, b * 128:(b + 1) * 128], w2q[0:m, c, :],
                                 start=(c == 0 and q == 0), stop=(c == NC - 1 and q == 1))
                    if c == NC - 1:
                        ins.then_inc(s.dn_ready, 1)

        @block.gpsimd
        def _(pool):
            tt = nc.gpsimd.tensor_tensor
            nc.gpsimd.memset(mhalf[:, :], -0.5)
            nc.gpsimd.memset(onesb[:, :], 1.0)
            nc.gpsimd.memset(onesf[:, :], 1.0).then_inc(s.memsets, 1)
            pool.wait_ge(s.memsets, 1)
            done = [0]

            def rsqrt(lo, n, wait, value, signal, shifted=False):
                pool.wait_ge(wait, value)
                nc.gpsimd.tensor_scalar(rstd[:, lo:lo + n], mv[:, lo:lo + n, 1], LN_EPS, None, ALU.add).then_inc(s.pool, 1)
                done[0] += 1
                pool.wait_ge(s.pool, done[0])
                ins = tt(rstd[:, lo:lo + n], rstd[:, lo:lo + n], mhalf[:, lo:lo + n], ALU.pow)
                if not shifted:
                    ins.then_inc(signal, 1)
                    return
                ins.then_inc(s.pool, 1)
                nc.gpsimd.tensor_scalar(shift[:, lo:lo + n], mv[:, lo:lo + n, 0], -1.0, None, ALU.mult).then_inc(s.pool, 1)
                done[0] += 2
                pool.wait_ge(s.pool, done[0])
                tt(shift[:, lo:lo + n], shift[:, lo:lo + n], rstd[:, lo:lo + n], ALU.mult).then_inc(signal, n)


            def products(h):
                pool.wait_ge(ctx_in[h // 4], 16)
                if h == 2:
                    pool.wait_ge(s.kv_first, 1)
                if h >= 2:
                    pool.wait_ge(s.y_ready, h - 1)
                for i in range(HD0):
                    n = i + 1
                    c = CT[:, :, h, :]
                    ins = tt(kv[:, h % 2, :, pair(i) * B:(pair(i) + n) * B].rearrange("p k (j b) -> p k j b", b=B),
                             c[:, :, 0:n * B].rearrange("p k (j b) -> p k j b", b=B),
                             c[:, :, i * B:(i + 1) * B].unsqueeze(2).to_broadcast([128, DK, n, B]), ALU.mult)
                ins.then_inc(s.kv_ready, 1)

            rsqrt(0, 4, s.ln1_stats, 1, s.rstd1, True)
            products(1)
            for c in range(1, 4):
                rsqrt(4 * c, 4, s.ln1_stats, c + 1, s.rstd1, True)
            for h in range(NT):
                if h + 2 < NT:
                    products(h + 2)
                pool.wait_ge(s.prod_raw, h + 1)
                tt(prod[:, h % 2, 1, POOL_SUM:512], prod[:, h % 2, 1, POOL_SUM:512], prod[:, h % 2, 1, 512 + POOL_SUM:1024],
                   ALU.add).then_inc(s.prod_pool, 1)
                if h % 2 and h >= 3:
                    rsqrt(h - 3, 2, s.ln2_stats, h - 1, s.rstd2, True)
            rsqrt(NT - 2, 2, s.ln2_stats, NT, s.rstd2, True)
            for g in range(4):
                pool.wait_ge(s.sh_copied, g + 1)
                tt(shs[:, g, :], shs[:, g, :], shu[:, g % 2, :], ALU.mult).then_inc(s.sh_h, 1)
            pool.wait_ge(s.blocks, 1)
            tt(blkid[:, 1], blk1[:, 1], cf[:, C_TOK:C_TOK + NT].unsqueeze(2).to_broadcast([128, NT, NB]), ALU.mult).then_inc(s.blocks2, 1)
            pool.wait_ge(s.pos, 1)
            for v in range(4):
                src = slf[:, v, :] if v < 2 else wc[:, v - 2, :]
                ins = tt(SP4[:, v, :].rearrange("p (h j) -> p h j", j=HD0), src.unsqueeze(2).to_broadcast([128, NT, HD0]),
                         cf[:, C_J:C_J + HD0].unsqueeze(1).to_broadcast([128, NT, HD0]), ALU.mult)
            ins.then_inc(s.spread, 1)
            pool.wait_ge(s.spread, 1)
            pool.wait_ge(s.xn_out, NT * 16)
            pool.wait_ge(s.tokens, 1)
            for n in range(NB):
                if n >= 4:
                    pool.wait_ge(s.xg_xp, n - 3)
                pool.indirect_dma_start(out=xg[:, n % 4, :], out_offset=None, in_=Xn,
                                        in_offset=bass.IndirectOffsetOnAxis(ap=tok[:, n:n + 1], axis=0)).then_inc(xg_in[n % 4], 16)
            for i in range(4):
                pool.wait_ge(yg_out[i], 16 * ((NB - i + 3) // 4))
            pool.wait_ge(s.slotsB, 1)

            def gather(b):
                if b >= 4:
                    pool.wait_ge(s.res2, b - 3)
                for q in range(2):
                    pool.indirect_dma_start(out=gb[:, b % 4, q, :], out_offset=None, in_=YG,
                                            in_offset=bass.IndirectOffsetOnAxis(ap=slotB[:, q, b:b + 1], axis=0)).then_inc(gat[b % 4], 16)

            for b in range(4):
                gather(b)
            for b in range(4):
                rsqrt(b, 1, s.ln3_stats, b + 1, s.rstd3)
            for u in range(32):
                v = u - 2
                if 0 <= v < 24 and v % 8 < 4:
                    b = 4 * (v // 8 + 1) + v % 8
                    rsqrt(b, 1, s.ln3_stats, b + 1, s.rstd3)
                    pool.wait_ge(s.rstd3, b + 1)
                if v in (17, 25):
                    rsqrt(v // 8 * 4 - 8, 4, s.d_stats, v // 8 - 1, s.rstd4)
                    pool.wait_ge(s.rstd4, v // 8 - 1)
                pool.wait_ge(s.rope_mul, u + 1)
                if 1 <= u < 25 and (u - 1) % 8 < 4:
                    b = 4 * ((u - 1) // 8 + 1) + (u - 1) % 8
                    pool.wait_ge(gat[b % 4], 32 * (b // 4 + 1))
                if u >= 2:
                    pool.wait_ge(s.s_ready, 2 * u - 2)
                tt(Q[64:128, u % 2, 0, :], ra[64:128, u % 2, :], rbm[64:128, u % 2, :], ALU.add).then_inc(s.q_r, 1)
                pool.wait_ge(s.q_r, 2 * u + 1)
                tt(Q[0:64, u % 2, 1, :], ra[0:64, u % 2, :], rbm[0:64, u % 2, :], ALU.add).then_inc(s.q_r, 1)
                pool.wait_ge(s.q_r, 2 * u + 2)
                if 0 <= v + 2 < 24 and (v + 2) % 8 < 4:
                    gather(4 * ((v + 2) // 8 + 1) + (v + 2) % 8)
            rsqrt(8, 4, s.d_stats, 3, s.rstd4)
            rsqrt(12, 4, s.d_stats, 4, s.rstd4)

        @block.vector
        def _(dve):
            tt = nc.vector.tensor_tensor
            ts = nc.vector.tensor_scalar
            stt = nc.vector.scalar_tensor_tensor
            red = nc.vector.tensor_reduce
            steps = [0]

            def link(ins):
                steps[0] += 1
                ins.then_inc(s.dve, 1)
                dve.wait_ge(s.dve, steps[0])

            def stats(t, signal=None):
                link(nc.vector.bn_stats(st[:, t, :], X[:, t, :]))
                ins = nc.vector.bn_aggr(mv[:, t, :], st[:, t, :])
                if signal is not None:
                    ins.then_inc(signal, 1)

            def normalise(t, dst):
                return ts(dst, X[:, t, :], mv[:, t, 0:1], rstd[:, t:t + 1], ALU.subtract, ALU.mult)

            nc.vector.memset(zk[:, :], 0.0).then_inc(s.zk_set, 1)
            dve.wait_ge(s.ssm, 32)
            tt(zk[:, 127:128], zk[:, 127:128], dsb[:, :], ALU.add).then_inc(s.zk_d, 1)
            for c in range(4):
                dve.wait_ge(x_in[c], 16)
                for t in range(4 * c, 4 * c + 4):
                    stats(t, s.ln1_stats if t == 4 * c + 3 else None)
                if c == 0:
                    dve.wait_ge(ctx_in[0], 16)
                    for i in range(HD0):
                        n = i + 1
                        ins = tt(kv[:, 0, :, pair(i) * B:(pair(i) + n) * B].rearrange("p k (j b) -> p k j b", b=B),
                                 CT[:, :, 0, 0:n * B].rearrange("p k (j b) -> p k j b", b=B),
                                 CT[:, :, 0, i * B:(i + 1) * B].unsqueeze(2).to_broadcast([128, DK, n, B]), ALU.mult)
                    ins.then_inc(s.kv_first, 1)
            dve.wait_ge(s.ident_in, 16)
            dve.wait_ge(s.const, 16)
            link(nc.vector.tensor_copy(identb, ident))
            link(nc.vector.tensor_copy(trib, cf[:, C_UP:C_UP + 128]))
            link(nc.vector.tensor_copy(placeb, cf[:, C_K4:C_K4 + 128]))
            L = RT[:, 0:256].rearrange("p (t e) -> p t e", t=NT)
            for h in range(NT + 1):
                if h < NT:
                    dve.wait_ge(s.y_ready, h + 1)
                    if h % 2 == 0:
                        dve.wait_ge(s.x_T, h // 2 + 1)
                    if h >= 2:
                        dve.wait_ge(s.out_ready, h - 1)
                    pr = prod[:, h % 2, :, :].rearrange("p k (i j b) -> p k i j b", i=HD0, j=HD0)
                    q = QT[:, :, h, :].rearrange("p k (i b) -> p k i b", b=B)
                    p = 3 * (h % 2)
                    for i in range(HD0):
                        if i <= 5:
                            y = bank(p, 2)[:, :, pair(i) * B:(pair(i) + i + 1) * B]
                        else:
                            o = (pair(i) - PA) * B
                            y = bank(p + 2)[:, 0:2 * PB * B].rearrange("p (k n) -> p k n", k=2)[:, :, o:o + (i + 1) * B]
                        y = y.rearrange("p k (j b) -> p k j b", b=B)
                        ins = tt(pr[:, :, i, 0:i + 1, :], y, q[:, :, i, :].unsqueeze(2).to_broadcast([128, DK, i + 1, B]), ALU.mult)
                        if i:
                            ins = tt(pr[:, :, 0:i, i, :], y[:, :, 0:i, :], q[:, :, 0:i, :], ALU.mult)
                    ins.then_inc(s.prod_raw, 1)
                t = h - 1
                if 0 <= t < NT:
                    if t == 0:
                        dve.wait_ge(s.tg_ready, 1)
                    dve.wait_ge(s.out_ready, t + 1)
                    stt(X[:, t, :], bank(6 + t % 2)[:, 0:256], tg[:, 0:1], X[:, t, :], ALU.mult, ALU.add).then_inc(s.res1, 1)
                if h < NT:
                    dve.wait_ge(s.prod_raw, h + 1)
                    tt(prod[:, h % 2, 0, 0:512], prod[:, h % 2, 0, 0:512], prod[:, h % 2, 0, 512:1024], ALU.add)
                    tt(prod[:, h % 2, 1, 0:POOL_SUM], prod[:, h % 2, 1, 0:POOL_SUM], prod[:, h % 2, 1, 512:512 + POOL_SUM],
                       ALU.add).then_inc(s.prod_ready, 1)
                if 0 <= t < NT:
                    dve.wait_ge(s.res1, t + 1)
                    stats(t, s.ln2_stats)
            dve.wait_ge(s.lg_ready, 1)
            dve.wait_ge(s.shared_w, 5 * 16)
            tt(L, bank(4)[:, 0:256].rearrange("p (t e) -> p t e", t=NT), rb[:, :].unsqueeze(1).to_broadcast([128, NT, E]),
               ALU.add).then_inc(s.lg_sb, 1)
            dve.wait_ge(s.lg_sb, 1)

            def ob(ap):
                return ap.unsqueeze(2).to_broadcast([128, 16, 16])

            def mb(ap):
                return ap.unsqueeze(1).to_broadcast([128, 16, 16])

            m16, s16 = small[:, 0:16], small[:, 16:32]
            link(red(m16, L, AX, ALU.max))
            tt(L, L, ob(m16), ALU.subtract).then_inc(s.max_sub, 1)
            dve.wait_ge(s.exp_r, 1)
            link(red(s16, L, AX, ALU.add))
            link(nc.vector.reciprocal(s16, s16))
            link(tt(L, L, ob(s16), ALU.mult))
            top = R2[:, 0:128].rearrange("p (t v) -> p t v", t=NT)
            idx = R2[:, 128:256].bitcast(u32).rearrange("p (t v) -> p t v", t=NT)
            for t in range(NT):
                ins = nc.vector.max(top[:, t, :], L[:, t, :])
            link(ins)
            for t in range(NT):
                ins = nc.vector.max_index(idx[:, t, :], top[:, t, :], L[:, t, :])
            link(ins)
            idf = R2[:, 256:288].rearrange("p (v t) -> p v t", v=2)
            link(nc.vector.tensor_copy(idf.rearrange("p v t -> p t v"), idx[:, :, 0:2]))
            oh = RT[:, 256:768].rearrange("p (v t e) -> p v t e", v=2, t=NT)
            for v in range(2):
                ins = tt(oh[:, v], ob(idf[:, v, :]), mb(cf[:, C_IOTA:C_IOTA + 16]), ALU.is_equal)
            link(ins)
            Mb = RT[:, 768:904].bitcast(bf16).rearrange("p (t e) -> p t e", t=NT + 1)
            nc.vector.memset(Mb[:, NT, :], 0.0)
            tt(Mb[:, 0:NT, :], oh[:, 0], oh[:, 1], ALU.add).then_inc(s.onehot, 1)
            link(tt(m16, top[:, :, 0], top[:, :, 1], ALU.add))
            link(ts(m16, m16, W_EPS, None, ALU.add))
            link(nc.vector.reciprocal(m16, m16))
            link(ts(m16, m16, tg[:, 2:3], None, ALU.mult))
            for v in range(2):
                ins = tt(wc[:, v, :], top[:, :, v], m16, ALU.mult)
            link(ins)
            dve.wait_ge(s.counts, 1)
            rank = bank(6)[:, 0:256].rearrange("p (t e) -> p t e", t=NT)
            total = bank(6)[:, NT * E:(NT + 1) * E]
            Rb = R2[:, 320:576].rearrange("p (t e) -> p t e", t=NT)
            tmp = R2[:, 640:896].rearrange("p (a b) -> p a b", a=16)
            nb_, sb_, en_ = small[:, 0:16], small[:, 16:32], small[:, 48:64]
            link(tt(tmp, ob(total), mb(cf[:, C_THR:C_THR + 16]), ALU.is_gt))
            link(red(nb_, tmp, AX, ALU.add))
            link(tt(tmp, cf[:, C_TRI:C_TRI + 256].rearrange("p (a b) -> p a b", a=16), mb(nb_), ALU.mult))
            link(red(sb_, tmp, AX, ALU.add))
            link(tt(en_, sb_, nb_, ALU.add))
            stt(Rb, mb(sb_), 128.0, rank, ALU.mult, ALU.add).then_inc(s.cnt_read, 1)
            dve.wait_ge(s.cnt_read, 1)
            for v in range(2):
                link(tt(tmp, oh[:, v], Rb, ALU.mult))
                link(red(slf[:, v, :], tmp, AX, ALU.add))
            link(nc.vector.tensor_copy(slot[:, :, :], slf))
            bits = small2[:, 64:128].bitcast(i32).rearrange("p (a v t) -> p a v t", a=2, v=2)
            ts(bits[:, 0], slot[:, :, :], 127, None, ALU.bitwise_and)
            link(ts(bits[:, 1], slot[:, :, :], 7, None, ALU.logical_shift_right))
            ts(posf, bits[:, 0], float(LOOKBACK // 2), None, ALU.add)
            nc.vector.tensor_copy(blkf, bits[:, 1]).then_inc(s.pos, 1)
            dve.wait_ge(s.pos, 1)
            blk_c = cf[:, C_BLK:C_BLK + NB].unsqueeze(1).to_broadcast([128, 32, NB])
            flat = "p v t n -> p (v t) n"
            tt(blk1.rearrange(flat), blk_c, blkf.rearrange("p v t -> p (v t)").unsqueeze(2).to_broadcast([128, 32, NB]),
               ALU.is_equal).then_inc(s.blocks, 1)
            dve.wait_ge(s.blocks, 1)
            tt(blkid[:, 0], blk1[:, 0], cf[:, C_TOK:C_TOK + NT].unsqueeze(2).to_broadcast([128, NT, NB]), ALU.mult)
            for v in range(2):
                for t in range(NT):
                    ins = ts(place[:, v, t, :], placeb, posf[:, v, t:t + 1], None, ALU.is_equal)
                ins.then_inc(s.places, 1)
            dve.wait_ge(s.tok_ps, 1)
            nc.vector.tensor_copy(tok[:, :], bank(7)[:, 0:NB]).then_inc(s.tokens, 1)

            def shared_residual(g):
                dve.wait_ge(s.sh_dn, g + 1)
                for c in range(2):
                    t = 4 * g + 2 * c
                    ins = stt(X[:, t:t + 2, :], bank((4, 0, 2, 4)[g] + c).rearrange("p (t d) -> p t d", t=2), tg[:, 2:3],
                              X[:, t:t + 2, :], ALU.mult, ALU.add)
                ins.then_inc(s.sh_res, 1)

            shared_residual(0)
            shared_residual(1)
            tb = R2[:, 0:NB * E].rearrange("p (n e) -> p n e", e=E)
            ef = R2[:, 768:768 + NB]
            dve.wait_ge(s.spread, 1)
            link(tt(tb, en_.unsqueeze(1).to_broadcast([128, NB, E]), cf[:, C_BLK:C_BLK + NB].unsqueeze(2).to_broadcast([128, NB, E]), ALU.is_le))
            link(red(ef, tb, AX, ALU.add))
            link(ts(ef, ef, float(E - 1), None, ALU.min))
            nc.vector.tensor_copy(eid[:, :], ef).then_inc(s.slots, 1)
            dve.wait_ge(s.slots, 1)

            for g in range(2, 4):
                shared_residual(g)
            dve.wait_ge(s.spread_ps, 1)
            nc.vector.tensor_copy(slotB[:, :, :], bank(6)[:, 0:2 * B].rearrange("p (v b) -> p v b", v=2))
            nc.vector.tensor_copy(wcB[:, :, :], bank(6)[:, 2 * B:4 * B].rearrange("p (v b) -> p v b", v=2)).then_inc(s.slotsB, 1)
            dve.wait_ge(s.slotsB, 1)
            def mask(c, step):
                d = R2[:, 0:512].rearrange("p (b k) -> p b k", b=4)
                if step == 0:
                    link(tt(d, cf[:, C_K4:C_K4 + 128].unsqueeze(1).to_broadcast([128, 4, 128]),
                            segf[:, 4 * c:4 * c + 4].unsqueeze(2).to_broadcast([128, 4, 128]), ALU.subtract))
                elif step == 1:
                    link(tt(d, d, d, ALU.mult))
                else:
                    ts(maskb[:, 4 * c:4 * c + 4, :], d, (LOOKBACK / 2.0) ** 2, NEG, ALU.is_gt, ALU.mult).then_inc(s.mask, 1)
                    dve.wait_ge(s.mask, c + 1)

            dve.wait_ge(s.seg, 16)
            link(nc.vector.tensor_copy(segf[:, :], segi[:, :]))
            for n in range(NB + 2):
                if 8 <= n < 20:
                    mask((n - 8) // 3, (n - 8) % 3)
                if n < NB:
                    dve.wait_ge(s.silu, n + 1)
                    if n >= 2:
                        dve.wait_ge(s.h_xp, n - 1)
                    tt(hh[:, n % 2, :], sg[:, n % 2, :], bank(2 + n % 2)[:, I:2 * I], ALU.mult).then_inc(s.h_ready, 1)
                m = n - 1
                if 0 <= m < NB:
                    dve.wait_ge(s.h_xp, m + 1)
                    if m >= 2:
                        dve.wait_ge(s.y_blk, m - 1)
                    nc.vector.tensor_copy(hT[:, m % 2, :], bank(4 + m % 2)[:, 0:I]).then_inc(s.h_T, 1)
                m = n - 2
                if 0 <= m < NB:
                    dve.wait_ge(s.y_blk, m + 1)
                    if m >= 4:
                        dve.wait_ge(yg_out[m % 4], 16 * (m // 4))
                    nc.vector.tensor_copy(yb[:, m % 4, :], bank(6 + m % 2)[:, 0:D]).then_inc(s.y_sb, 1)

            def combine(b):
                dve.wait_ge(gat[b % 4], 32 * (b // 4 + 1))
                if b == 0:
                    dve.wait_ge(s.xin, 8 * 16)
                link(stt(X[:, b, :], gb[:, b % 4, 0, :], wcB[:, 0, b:b + 1], X[:, b, :], ALU.mult, ALU.add))
                stt(X[:, b, :], gb[:, b % 4, 1, :], wcB[:, 1, b:b + 1], X[:, b, :], ALU.mult, ALU.add).then_inc(s.res2, 1)
                dve.wait_ge(s.res2, b + 1)
                stats(b, s.ln3_stats)

            def row(b):
                dve.wait_ge(s.rstd3, b + 1)
                if b >= 4:
                    dve.wait_ge(s.xn3_xp, 2 * (b // 4))
                normalise(b, xb[:, b % 4, :]).then_inc(s.xn3, 1)

            def rope(u):
                dve.wait_ge(s.proj, u + 1)
                if u >= 2:
                    dve.wait_ge(s.q_r, 2 * u - 2)
                for dst, w in ((rbm, sinT), (ra, cosT)):
                    ins = tt(dst[:, u % 2, :].rearrange("p (b s) -> p b s", b=4), bank(3).rearrange("p (b s) -> p b s", b=4),
                             w.unsqueeze(1).to_broadcast([128, 4, 128]), ALU.mult)
                ins.then_inc(s.rope_read, 1)
                dve.wait_ge(s.rope_read, u + 1)
                nc.vector.stream_shuffle(rbm[:, u % 2, :], rbm[:, u % 2, :], PARTNER).then_inc(s.rope_mul, 1)

            def residual(i, b3):
                b, half = 4 * (i // 8) + i % 8 // 2, i % 2
                dve.wait_ge(s.op_ready, i + 1)
                x_ = X[:, b, half * 128:(half + 1) * 128]
                stt(x_, bank(b3)[:, 0:128], tg[:, 1:2], x_, ALU.mult, ALU.add).then_inc(s.res3, 1)
                if half:
                    dve.wait_ge(s.res3, i + 1)
                    stats(b, s.d_stats if b % 4 == 3 else None)

            sc = small[:, 40:43]

            def scales():
                dve.wait_ge(s.scale_r, 1)
                ts(sc, bank(4)[:, 0:3], 1.0 / (HID * D), None, ALU.mult).then_inc(s.scale_sb, 1)
                dve.wait_ge(s.scale_sb, 1)
                link(ts(small[:, 43:46], sc, 0.5, None, ALU.mult))
                link(ts(small[:, 46:49], sc, -0.5, None, ALU.mult))
                link(nc.vector.reciprocal(small[:, 50:51], sc[:, 0:1]))
                link(ts(small[:, 50:51], small[:, 50:51], 0.5, None, ALU.mult))
                link(tt(small[:, 49:50], sc[:, 0:1], sc[:, 1:2], ALU.mult))
                link(tt(small[:, 49:50], small[:, 49:50], sc[:, 2:3], ALU.mult))
                link(ts(small[:, 49:50], small[:, 49:50], tg[:, 3:4], 2.0, ALU.mult, ALU.mult))

            def ternary(i, half):
                w, q, n = ((w1f, w1q, DK * HID), (w3f, w3q, DK * HID), (w2f, w2q, NC * D))[i]
                w, q = w.rearrange("p k n -> p (k n)"), q.rearrange("p k n -> p (k n)")
                low = wtmp[:, 0:n]
                if not half:
                    link(ts(low, w, small[:, 46 + i:47 + i], None, ALU.is_lt))
                    return
                stt(q, w, small[:, 43 + i:44 + i], low, ALU.is_gt, ALU.subtract).then_inc(s.ternary, 1)
                dve.wait_ge(s.ternary, i + 1)

            turned = [R2[:, 64 + 512 * z:576 + 512 * z] for z in range(2)]

            def rope_keys(c):
                dve.wait_ge(s.kr_ready, c + 1)
                for z, w in enumerate((cosT, sinT)):
                    ins = tt(turned[z].rearrange("p (b s) -> p b s", b=4),
                             bank((0, 5)[c]).rearrange("p (b s) -> p b s", b=4), w.unsqueeze(1).to_broadcast([128, 4, 128]), ALU.mult)
                ins.then_inc(s.kr_mul, 1)
                dve.wait_ge(s.kr_mul, c + 1)
                link(nc.vector.stream_shuffle(turned[1], turned[1], PARTNER))
                for half in range(2):
                    b, k = 8 * c + 4 * half, 64 * half
                    for lo, dst in ((64, K01), (0, K10)):
                        ins = tt(dst[lo:lo + 64, b:b + 4, :].rearrange("p b s -> p (b s)"), turned[0][k:k + 64, :],
                                 turned[1][k:k + 64, :], ALU.add)
                ins.then_inc(s.kr_sb, 1)
                dve.wait_ge(s.kr_sb, c + 1)

            def rows(g):
                dve.wait_ge(s.rstd4, g + 1)
                if g >= 1:
                    dve.wait_ge(s.xn4_xp, 2 * g)
                for b in range(4):
                    normalise(4 * g + b, x3n[:, b, :]).then_inc(s.xn4, 1)

            def split_rows(g, t):
                h = slice(t * 256, (t + 1) * 256)
                dve.wait_ge(s.split_hi, 2 * g + t + 1)
                tt(xp[g % 2][1][:, :, h], bank(t if g else 4).rearrange("p (k n) -> p k n", k=DK), xp[g % 2][0][:, :, h],
                   ALU.subtract).then_inc(s.split_lo, 1)

            def output(g, b, b3):
                dve.wait_ge(s.dn_ready, 4 * g + b + 1)
                stt(X[:, 4 * g + b, :], bank(b3)[:, 0:D], small[:, 49:50], X[:, 4 * g + b, :], ALU.mult, ALU.add).then_inc(s.yout, 1)

            for b in range(4):
                combine(b)
            for b in range(4):
                row(b)
            rope_keys(0)
            rope(0)
            rope(1)
            for u in range(33):
                if u < 32:
                    for a in range(2):
                        h = slice(4 * a, 4 * a + 4)
                        dve.wait_ge(s.s_ready, 2 * u + a + 1)
                        link(red(mx[:, u % 2, h], bank(a).rearrange("p (i k) -> p i k", i=4), AX, ALU.max))
                        ts(nm[:, u % 2, h], mx[:, u % 2, h], -SCALE, None, ALU.mult).then_inc(s.max_ready, 1)
                if u == 0:
                    rope_keys(1)
                if u < 24 and u % 8 < 4:
                    combine(4 * (u // 8 + 1) + u % 8)
                if u == FFN_SCALE + 1:
                    scales()
                if u >= 9:
                    residual(u - 9, 4)
                if 0 <= u - 1 < 24 and (u - 1) % 8 < 4:
                    row(4 * ((u - 1) // 8 + 1) + (u - 1) % 8)
                if u == FFN_ROWS[0] - 1:
                    rows(0)
                if u < 32:
                    dve.wait_ge(s.exp_done, 2 * u + 2)
                    link(nc.vector.reciprocal(ri[:, u % 2, :], rs[:, u % 2, :]))
                    tt(P[:, u % 2], P[:, u % 2], ri[:, u % 2, :].unsqueeze(2).to_broadcast([128, 8, 128]), ALU.mult).then_inc(s.p_norm, 1)
                if u + 2 < 32:
                    rope(u + 2)
                if u == 19:
                    nc.vector.memset(w2f[:, NC - 1, :], 0.0).then_inc(s.w_abs, 1)
                if u in FFN_ROWS:
                    split_rows(0, FFN_ROWS.index(u))
                if u == FFN_SCALE + 7:
                    link(nc.vector.memset(wlast, 0.0))
                    nc.vector.tensor_copy(wlast[:, :, 0:LAST], w1q[:, :, HID - LAST:HID])
                    nc.vector.tensor_copy(wlast[:, :, 64:64 + LAST], w3q[:, :, HID - LAST:HID]).then_inc(s.w_last, 1)
                if FFN_SCALE < u <= FFN_SCALE + 6:
                    ternary((u - FFN_SCALE - 1) // 2, (u - FFN_SCALE - 1) % 2)

            for n in range(4 * NC):
                g, c = n // NC, n % NC
                m = min(128, HID - c * 128)
                dve.wait_ge(s.up_silu, n + 1)
                linear = bank(3 + 2 * (n % 2))[0:m, :] if c < NC - 1 else bank(2 + 2 * (n % 2))[64:64 + m, :]
                stt(gg[0:m, n % 2, :], linear, small[0:m, 50:51], sl[0:m, n % 2, :], ALU.mult, ALU.mult).then_inc(s.g_ready, 1)
                if c == 0 and 1 <= g < 3:
                    rows(g + 1)
                if g and c >= 2:
                    output(g - 1, c - 2, 6 + c % 2)
                dve.wait_ge(s.g_hi, n + 1)
                tt(gs[g % 2][1][0:m, c, :], gg[0:m, n % 2, :], gs[g % 2][0][0:m, c, :], ALU.subtract).then_inc(s.g_lo, 1)
                if n == 0:
                    rows(1)
                if n < 4:
                    for i in (24 + 2 * n, 25 + 2 * n):
                        residual(i, 6 + i % 2)
                if c in (2, 3) and g < 3:
                    split_rows(g + 1, c - 2)
            for b in range(4):
                output(3, b, (0, 1, 6, 7)[b])


_OUT = (B, S, D)


def _rotation_order():
    import numpy as np
    r = np.arange(R)
    return r % 16 + 16 * (r // 32) + R // 2 * (r % 32 // 16)


def _constants():
    import numpy as np
    p = np.arange(128)
    cf = np.zeros((128, NCF), np.float32)
    cf[:, C_ID:C_ID + 128] = np.eye(128)
    half = R // 2
    inv = (1.0 / np.float32(10000.0) ** (np.arange(half, dtype=np.float32) / np.float32(half))).astype(np.float32)
    ang = np.arange(128, dtype=np.float32)[None, :] * inv[_rotation_order()[p % R] % half][:, None]
    cf[:, C_COS:C_COS + 128] = np.cos(ang)
    cf[:, C_SIN:C_SIN + 128] = np.sin(ang) * np.where(p % 32 < 16, 1.0, -1.0)[:, None]
    cf[:, C_K4:C_K4 + 128] = p[None, :] + LOOKBACK // 2
    cf[:, C_TRI:C_TRI + 256] = np.tril(np.ones((16, 16)), -1).reshape(1, 256)
    cf[:, C_THR:C_THR + 16] = 128 * np.arange(16)
    cf[:, C_IOTA:C_IOTA + 16] = np.arange(16)
    cf[:, C_BLK:C_BLK + NB] = np.arange(NB)
    cf[:, C_UP:C_UP + 128] = np.triu(np.ones((128, 128)), 1)
    cf[:, C_J:C_J + HD0] = p[:, None] // B == np.arange(HD0)
    cf[:, C_B:C_B + B] = p[:, None] % B == np.arange(B)
    cf[:, C_TOK:C_TOK + NT] = 128 * np.arange(NT)[None, :] + p[:, None]
    return cf


def kernel(x, ctx_2048, itok_BxS_0_1023, g_xattn, g_ffn, L0_xattn_ssm_kernel, L0_xattn_D, L0_ffn_Wr, L0_ffn_bias,
           L0_ffn_Wg, L0_ffn_Wu, L0_ffn_Wd, L0_ffn_sWg, L0_ffn_sWu, L0_ffn_sWd, L1_xattn_W_kvc, L1_xattn_W_dq,
           L1_xattn_W_uq, L1_xattn_W_qr, L1_xattn_W_uk, L1_xattn_W_kr, L1_xattn_W_uv, L1_xattn_W_o,
           L1_ffn_w1, L1_ffn_w3, L1_ffn_w2):
    import numpy as np
    import concourse.bacc as bacc
    from concourse import mybir
    from concourse.bass_utils import run_bass_kernel_spmd

    def t(a):
        return np.ascontiguousarray(np.asarray(a).T)

    def tiles(a):
        return np.ascontiguousarray(np.asarray(a).reshape(B, NH0, HD0, D).transpose(2, 0, 1, 3)).reshape(128, NT, D)

    def back(a, axis):
        a = np.asarray(a)
        halves = a.reshape(a.shape[:axis] + (DK, 128) + a.shape[axis + 1:])
        return np.ascontiguousarray(np.flip(halves, axis + 1)).reshape(a.shape)

    cf = _constants()
    given = {
        "x": tiles(x), "ctxd": np.ascontiguousarray(back(tiles(ctx_2048), 2).reshape(128, NT, DK, 128).transpose(3, 2, 1, 0)), "segT": t(itok_BxS_0_1023), "gates": np.concatenate([np.asarray(g_xattn), np.asarray(g_ffn)]),
        "ssm": L0_xattn_ssm_kernel, "ssmD": L0_xattn_D, "WrT": t(L0_ffn_Wr), "rbias": L0_ffn_bias,
        "Wg": L0_ffn_Wg, "Wu": L0_ffn_Wu, "Wd": L0_ffn_Wd, "sWg": L0_ffn_sWg, "sWu": L0_ffn_sWu, "sWd": L0_ffn_sWd,
        "Wkvc": back(L1_xattn_W_kvc, 0), "Wdq": L1_xattn_W_dq, "WuqT": t(L1_xattn_W_uq), "Wqr": np.asarray(L1_xattn_W_qr).reshape(QC, H // 2, 2, R)[:, :, ::-1, :][..., _rotation_order()],
        "WukT": t(L1_xattn_W_uk), "Wkr": np.asarray(L1_xattn_W_kr)[:, _rotation_order()], "WuvT": t(L1_xattn_W_uv), "Wo": L1_xattn_W_o,
        "w1T": t(L1_ffn_w1), "w3T": t(L1_ffn_w3), "w2T": t(L1_ffn_w2), "constf": cf,
    }
    nc = bacc.Bacc("TRN2", target_bir_lowering=False, num_devices=1)
    arrays, args = {}, []
    for name, a in given.items():
        a = np.ascontiguousarray(a)
        arrays[f"in_{name}"] = a
        args.append(nc.dram_tensor(f"in_{name}", a.shape, mybir.dt.from_np(a.dtype), kind="ExternalInput").ap())
    args.append(nc.dram_tensor("out_0", _OUT, mybir.dt.float32, kind="ExternalOutput").ap())
    flamingo_kernel(nc, *args)
    r = run_bass_kernel_spmd(nc, [arrays], core_ids=[0])
    return r.results[0]["out_0"]
```
